# Optimizing a Trainium2 kernel written in Bass

```python
import numpy as np
import jax
import jax.numpy as jnp

def _softmax(x, axis=-1):
    return jax.nn.softmax(x, axis=axis)

def _gelu(x):
    return jax.nn.gelu(x, approximate=True)

def _silu(x):
    return jax.nn.silu(x)

def _sigmoid(x):
    return jax.nn.sigmoid(x)

def _layernorm(x, axis=-1, eps=1e-05):
    m = jnp.mean(x, axis=axis, keepdims=True)
    v = jnp.var(x, axis=axis, keepdims=True)
    return (x - m) / jnp.sqrt(v + eps)

def _scatter_add(tgt, idx, src, axis=0):
    return tgt.at[idx].add(src)

def _segment_sum(src, seg, n):
    return jax.ops.segment_sum(src, seg, n)
kernel_name = 'mk_gnn_ffn_d2_gnn_r16_c327fc'

def setup_inputs(seed: int=0):
    np.random.seed(seed)
    _w = jnp.asarray

    def _rec_inputs():
        import jax
        import jax.numpy as jnp
        _gk = jax.random.key(seed)
        x = -0.0003713 + 1 * jax.random.normal(jax.random.fold_in(_gk, 1), (3125, 256), jnp.float32)
        _s = jax.random.randint(jax.random.fold_in(_gk, 2), (50000,), 0, 3125, jnp.int32)
        _d = jax.random.randint(jax.random.fold_in(_gk, 3), (50000,), 0, 3125, jnp.int32)
        _loop = jnp.arange(3125, dtype=jnp.int32)
        src = jnp.concatenate([_s, _d, _loop])
        dst = jnp.concatenate([_d, _s, _loop])
        _o = jnp.argsort(dst, stable=True)
        src = src[_o]
        dst = dst[_o]
        return (x, src, dst)
    x, src, dst = _rec_inputs()

    def _L0_gnn_setup():
        import jax, jax.numpy as jnp
        import numpy as np
        N_NODES = 3125
        N_EDGES = 50000
        IN_FEATS = 256
        HIDDEN = 256

        def _sage_conv(x, src, dst, Wl, bl, Wr):
            msg = x[src]
            agg = jax.ops.segment_sum(msg, dst, num_segments=N_NODES)
            cnt = jax.ops.segment_sum(jnp.ones((src.shape[0],), dtype=x.dtype), dst, num_segments=N_NODES)
            mean = agg / jnp.maximum(cnt, 1.0)[:, None]
            return mean @ Wl.T + bl + x @ Wr.T
        key = jax.random.key(seed)
        ks = jax.random.split(key, 8)
        x = jax.random.normal(ks[0], (N_NODES, IN_FEATS), dtype=jnp.float32)
        edge_index = jax.random.randint(ks[1], (2, N_EDGES), 0, N_NODES, dtype=jnp.int32)
        s = 1.0 / np.sqrt(IN_FEATS)
        W1l = jax.random.uniform(ks[2], (HIDDEN, IN_FEATS), minval=-s, maxval=s, dtype=jnp.float32)
        b1 = jax.random.uniform(ks[3], (HIDDEN,), minval=-s, maxval=s, dtype=jnp.float32)
        W1r = jax.random.uniform(ks[4], (HIDDEN, IN_FEATS), minval=-s, maxval=s, dtype=jnp.float32)
        s2 = 1.0 / np.sqrt(HIDDEN)
        W2l = jax.random.uniform(ks[5], (HIDDEN, HIDDEN), minval=-s2, maxval=s2, dtype=jnp.float32)
        b2 = jax.random.uniform(ks[6], (HIDDEN,), minval=-s2, maxval=s2, dtype=jnp.float32)
        W2r = jax.random.uniform(ks[7], (HIDDEN, HIDDEN), minval=-s2, maxval=s2, dtype=jnp.float32)
        return {'x': x, 'edge_index': edge_index, 'W1l': W1l, 'b1': b1, 'W1r': W1r, 'W2l': W2l, 'b2': b2, 'W2r': W2r}
    _L0_gnn_all = _L0_gnn_setup()
    _L0_gnn_in = {k: v for k, v in _L0_gnn_all.items() if k in ('W1l', 'b1', 'W1r', 'W2l', 'b2', 'W2r')}
    del _L0_gnn_all

    def _L0_ffn_setup():
        import jax, jax.numpy as jnp
        import numpy as np
        B, S, D, E, H, K = (4, 256, 256, 8, 512, 2)
        key = jax.random.key(seed)
        ks = jax.random.split(key, 6)
        x = jax.random.normal(ks[0], (B, S, D), jnp.float32)
        Wg = jax.random.normal(ks[1], (D, E), jnp.float32) * 0.02
        bg = jnp.zeros((E,), jnp.float32)
        W1 = jax.random.normal(ks[2], (E, D, H), jnp.float32) * 0.02
        b1 = jnp.zeros((E, H), jnp.float32)
        W2 = jax.random.normal(ks[3], (E, H, D), jnp.float32) * 0.02
        b2 = jnp.zeros((E, D), jnp.float32)
        return {'x': x, 'Wg': Wg, 'bg': bg, 'W1': W1, 'b1': b1, 'W2': W2, 'b2': b2}
    _L0_ffn_all = _L0_ffn_setup()
    _L0_ffn_in = {k: v for k, v in _L0_ffn_all.items() if k in ('Wg', 'bg', 'W1', 'b1', 'W2', 'b2')}
    del _L0_ffn_all

    def _L1_gnn_setup():
        import jax, jax.numpy as jnp
        import numpy as np
        NUM_NODES = 6250
        HIDDEN = 256
        NUM_EDGES = 100000

        def _sage_conv(x, edge_index, w_l, w_r, b):
            src, dst = (edge_index[0], edge_index[1])
            n = x.shape[0]
            nbr_sum = jax.ops.segment_sum(x[src], dst, num_segments=n)
            deg = jax.ops.segment_sum(jnp.ones((src.shape[0],), x.dtype), dst, num_segments=n)
            nbr_mean = nbr_sum / jnp.maximum(deg, 1.0)[:, None]
            return nbr_mean @ w_l.T + x @ w_r.T + b
        key = jax.random.key(seed)
        ks = jax.random.split(key, 8)

        def glorot(k, shape):
            lim = float(np.sqrt(6.0 / (shape[0] + shape[1])))
            return jax.random.uniform(k, shape, jnp.float32, -lim, lim)
        return {'node_features': jax.random.normal(ks[0], (NUM_NODES, HIDDEN), jnp.float32), 'w1_l': glorot(ks[1], (HIDDEN, HIDDEN)), 'w1_r': glorot(ks[2], (HIDDEN, HIDDEN)), 'b1': jnp.zeros((HIDDEN,), jnp.float32), 'w2_l': glorot(ks[3], (HIDDEN, HIDDEN)), 'w2_r': glorot(ks[4], (HIDDEN, HIDDEN)), 'b2': jnp.zeros((HIDDEN,), jnp.float32), 'edge_index': jax.random.randint(ks[5], (2, NUM_EDGES), 0, NUM_NODES, jnp.int64)}
    _L1_gnn_all = _L1_gnn_setup()
    _L1_gnn_in = {k: v for k, v in _L1_gnn_all.items() if k in ('w1_l', 'w1_r', 'b1', 'w2_l', 'w2_r', 'b2')}
    del _L1_gnn_all

    def _L1_ffn_setup():
        import jax, jax.numpy as jnp
        import numpy as np
        B, A = (256, 8)
        IN, OUT = (256, 256)
        SH1, SH2 = (256, 128)
        EH1, EH2 = (128, 64)
        E, TOPK = (4, 2)

        def _shared_mlp(x, W1, b1, W2, b2, W3, b3):
            h = jax.nn.relu(x @ W1 + b1)
            h = jax.nn.relu(h @ W2 + b2)
            return h @ W3 + b3

        def _experts_mlp(x, eW1, eb1, eW2, eb2, eW3, eb3):
            h = jax.nn.relu(jnp.einsum('baf,efh->ebah', x, eW1) + eb1[:, None, None, :])
            h = jax.nn.relu(jnp.einsum('ebah,ehg->ebag', h, eW2) + eb2[:, None, None, :])
            o = jnp.einsum('ebag,ego->ebao', h, eW3) + eb3[:, None, None, :]
            return jnp.moveaxis(o, 0, -1)
        key = jax.random.key(seed)
        ks = jax.random.split(key, 16)
        s = 0.05
        return {'x': jax.random.normal(ks[0], (B, A, IN), jnp.float32), 'sW1': jax.random.normal(ks[1], (IN, SH1), jnp.float32) * s, 'sb1': jnp.zeros((SH1,), jnp.float32), 'sW2': jax.random.normal(ks[2], (SH1, SH2), jnp.float32) * s, 'sb2': jnp.zeros((SH2,), jnp.float32), 'sW3': jax.random.normal(ks[3], (SH2, OUT), jnp.float32) * s, 'sb3': jnp.zeros((OUT,), jnp.float32), 'eW1': jax.random.normal(ks[4], (E, IN, EH1), jnp.float32) * s, 'eb1': jnp.zeros((E, EH1), jnp.float32), 'eW2': jax.random.normal(ks[5], (E, EH1, EH2), jnp.float32) * s, 'eb2': jnp.zeros((E, EH2), jnp.float32), 'eW3': jax.random.normal(ks[6], (E, EH2, OUT), jnp.float32) * s, 'eb3': jnp.zeros((E, OUT), jnp.float32), 'gW': jax.random.normal(ks[7], (IN, E), jnp.float32) * s, 'gb': jnp.zeros((E,), jnp.float32)}
    _L1_ffn_all = _L1_ffn_setup()
    _L1_ffn_in = {k: v for k, v in _L1_ffn_all.items() if k in ('sW1', 'sb1', 'sW2', 'sb2', 'sW3', 'sb3', 'eW1', 'eb1', 'eW2', 'eb2', 'eW3', 'eb3', 'gW', 'gb')}
    del _L1_ffn_all
    return {'x': x, 'src': src, 'dst': dst, 'L0_gnn_W1l': _L0_gnn_in['W1l'], 'L0_gnn_b1': _L0_gnn_in['b1'], 'L0_gnn_W1r': _L0_gnn_in['W1r'], 'L0_gnn_W2l': _L0_gnn_in['W2l'], 'L0_gnn_b2': _L0_gnn_in['b2'], 'L0_gnn_W2r': _L0_gnn_in['W2r'], 'L0_ffn_Wg': _L0_ffn_in['Wg'], 'L0_ffn_bg': _L0_ffn_in['bg'], 'L0_ffn_W1': _L0_ffn_in['W1'], 'L0_ffn_b1': _L0_ffn_in['b1'], 'L0_ffn_W2': _L0_ffn_in['W2'], 'L0_ffn_b2': _L0_ffn_in['b2'], 'L1_gnn_w1_l': _L1_gnn_in['w1_l'], 'L1_gnn_w1_r': _L1_gnn_in['w1_r'], 'L1_gnn_b1': _L1_gnn_in['b1'], 'L1_gnn_w2_l': _L1_gnn_in['w2_l'], 'L1_gnn_w2_r': _L1_gnn_in['w2_r'], 'L1_gnn_b2': _L1_gnn_in['b2'], 'L1_ffn_sW1': _L1_ffn_in['sW1'], 'L1_ffn_sb1': _L1_ffn_in['sb1'], 'L1_ffn_sW2': _L1_ffn_in['sW2'], 'L1_ffn_sb2': _L1_ffn_in['sb2'], 'L1_ffn_sW3': _L1_ffn_in['sW3'], 'L1_ffn_sb3': _L1_ffn_in['sb3'], 'L1_ffn_eW1': _L1_ffn_in['eW1'], 'L1_ffn_eb1': _L1_ffn_in['eb1'], 'L1_ffn_eW2': _L1_ffn_in['eW2'], 'L1_ffn_eb2': _L1_ffn_in['eb2'], 'L1_ffn_eW3': _L1_ffn_in['eW3'], 'L1_ffn_eb3': _L1_ffn_in['eb3'], 'L1_ffn_gW': _L1_ffn_in['gW'], 'L1_ffn_gb': _L1_ffn_in['gb']}

def reference(x, src, dst, L0_gnn_W1l, L0_gnn_b1, L0_gnn_W1r, L0_gnn_W2l, L0_gnn_b2, L0_gnn_W2r, L0_ffn_Wg, L0_ffn_bg, L0_ffn_W1, L0_ffn_b1, L0_ffn_W2, L0_ffn_b2, L1_gnn_w1_l, L1_gnn_w1_r, L1_gnn_b1, L1_gnn_w2_l, L1_gnn_w2_r, L1_gnn_b2, L1_ffn_sW1, L1_ffn_sb1, L1_ffn_sW2, L1_ffn_sb2, L1_ffn_sW3, L1_ffn_sb3, L1_ffn_eW1, L1_ffn_eb1, L1_ffn_eW2, L1_ffn_eb2, L1_ffn_eW3, L1_ffn_eb3, L1_ffn_gW, L1_ffn_gb):
    import jax
    import jax.numpy as jnp

    def _L0_gnn_ref(x, edge_index, W1l, b1, W1r, W2l, b2, W2r):
        import jax, jax.numpy as jnp
        import numpy as np
        N_NODES = 3125
        N_EDGES = 50000
        IN_FEATS = 256
        HIDDEN = 256

        def _sage_conv(x, src, dst, Wl, bl, Wr):
            msg = x[src]
            agg = jax.ops.segment_sum(msg, dst, num_segments=N_NODES)
            cnt = jax.ops.segment_sum(jnp.ones((src.shape[0],), dtype=x.dtype), dst, num_segments=N_NODES)
            mean = agg / jnp.maximum(cnt, 1.0)[:, None]
            return mean @ Wl.T + bl + x @ Wr.T
        src, dst = (edge_index[0], edge_index[1])
        h = jax.nn.relu(_sage_conv(x, src, dst, W1l, b1, W1r))
        out = _sage_conv(h, src, dst, W2l, b2, W2r)
        return out

    def _L0_ffn_ref(x, Wg, bg, W1, b1, W2, b2):
        import jax, jax.numpy as jnp
        import numpy as np
        B, S, D, E, H, K = (4, 256, 256, 8, 512, 2)
        Bv, Sv, Dv = x.shape
        gate_scores = x @ Wg + bg
        _, idx = jax.lax.top_k(gate_scores, K)
        mask = jax.nn.one_hot(idx, E, dtype=x.dtype).sum(axis=-2)
        xf = x.reshape(-1, Dv)
        mf = mask.reshape(-1, E)
        h = jax.nn.gelu(jnp.einsum('td,edh->teh', xf, W1) + b1[None], approximate=False)
        y = jnp.einsum('teh,ehd->ted', h, W2) + b2[None]
        out = jnp.einsum('ted,te->td', y, mf)
        return out.reshape(Bv, Sv, Dv)

    def _L1_gnn_ref(node_features, w1_l, w1_r, b1, w2_l, w2_r, b2, edge_index):
        import jax, jax.numpy as jnp
        import numpy as np
        NUM_NODES = 6250
        HIDDEN = 256
        NUM_EDGES = 100000

        def _sage_conv(x, edge_index, w_l, w_r, b):
            src, dst = (edge_index[0], edge_index[1])
            n = x.shape[0]
            nbr_sum = jax.ops.segment_sum(x[src], dst, num_segments=n)
            deg = jax.ops.segment_sum(jnp.ones((src.shape[0],), x.dtype), dst, num_segments=n)
            nbr_mean = nbr_sum / jnp.maximum(deg, 1.0)[:, None]
            return nbr_mean @ w_l.T + x @ w_r.T + b
        h = _sage_conv(node_features, edge_index, w1_l, w1_r, b1)
        h = jax.nn.relu(h)
        out = _sage_conv(h, edge_index, w2_l, w2_r, b2)
        return out

    def _L1_ffn_ref(x, sW1, sb1, sW2, sb2, sW3, sb3, eW1, eb1, eW2, eb2, eW3, eb3, gW, gb):
        import jax, jax.numpy as jnp
        import numpy as np
        B, A = (256, 8)
        IN, OUT = (256, 256)
        SH1, SH2 = (256, 128)
        EH1, EH2 = (128, 64)
        E, TOPK = (4, 2)

        def _shared_mlp(x, W1, b1, W2, b2, W3, b3):
            h = jax.nn.relu(x @ W1 + b1)
            h = jax.nn.relu(h @ W2 + b2)
            return h @ W3 + b3

        def _experts_mlp(x, eW1, eb1, eW2, eb2, eW3, eb3):
            h = jax.nn.relu(jnp.einsum('baf,efh->ebah', x, eW1) + eb1[:, None, None, :])
            h = jax.nn.relu(jnp.einsum('ebah,ehg->ebag', h, eW2) + eb2[:, None, None, :])
            o = jnp.einsum('ebag,ego->ebao', h, eW3) + eb3[:, None, None, :]
            return jnp.moveaxis(o, 0, -1)
        all_out = _experts_mlp(x, eW1, eb1, eW2, eb2, eW3, eb3)
        shared = _shared_mlp(x, sW1, sb1, sW2, sb2, sW3, sb3)
        gates = jax.nn.softmax(x @ gW + gb, axis=-1)
        topv, topi = jax.lax.top_k(gates, TOPK)
        topw = jax.nn.softmax(topv, axis=-1)
        sel = jnp.take_along_axis(all_out, topi[:, :, None, :], axis=-1)
        gated = jnp.sum(sel * topw[:, :, None, :], axis=-1)
        return shared + gated
    edge_index = jnp.stack([src, dst])
    x = x + _L0_gnn_ref(_layernorm(x, axis=-1), edge_index, L0_gnn_W1l, L0_gnn_b1, L0_gnn_W1r, L0_gnn_W2l, L0_gnn_b2, L0_gnn_W2r)
    x = x + _L0_ffn_ref(_layernorm(x, axis=-1)[None], L0_ffn_Wg, L0_ffn_bg, L0_ffn_W1, L0_ffn_b1, L0_ffn_W2, L0_ffn_b2)[0]
    x = x + _L1_gnn_ref(_layernorm(x, axis=-1), L1_gnn_w1_l, L1_gnn_w1_r, L1_gnn_b1, L1_gnn_w2_l, L1_gnn_w2_r, L1_gnn_b2, edge_index)
    x = x + _L1_ffn_ref(_layernorm(x, axis=-1)[None], L1_ffn_sW1, L1_ffn_sb1, L1_ffn_sW2, L1_ffn_sb2, L1_ffn_sW3, L1_ffn_sb3, L1_ffn_eW1, L1_ffn_eb1, L1_ffn_eW2, L1_ffn_eb2, L1_ffn_eW3, L1_ffn_eb3, L1_ffn_gW, L1_ffn_gb)[0]
    return x

_drawn_inputs = setup_inputs


def setup_inputs(seed=0):
    import zlib

    import numpy as np

    out = dict(_drawn_inputs(seed))
    spreads = {'L0_ffn_bg': (0.0, 0.1),
     'L0_ffn_b1': (0.0, 0.1),
     'L0_ffn_b2': (0.0, 0.1),
     'L1_gnn_b1': (0.0, 0.1),
     'L1_gnn_b2': (0.0, 0.1),
     'L1_ffn_sb1': (0.0, 0.536),
     'L1_ffn_sb2': (0.0, 0.308),
     'L1_ffn_sb3': (0.0, 0.1),
     'L1_ffn_eb1': (0.0, 0.8),
     'L1_ffn_eb2': (0.0, 0.631),
     'L1_ffn_eb3': (0.0, 0.1),
     'L1_ffn_gb': (0.0, 0.529)}
    factors = {}
    for name, (base, spread) in spreads.items():
        noise = np.random.default_rng([zlib.crc32(name.encode()), seed]).standard_normal(out[name].shape)
        drawn = base * np.exp(spread * noise) if base else spread * noise
        out[name] = jnp.asarray(drawn.astype(out[name].dtype))
    for name, factor in factors.items():
        out[name] = (out[name] * factor).astype(out[name].dtype)
    return out
```

```python
from contextlib import ExitStack, contextmanager

import concourse.bass as bass
from concourse import mybir

F32, F16, I32 = mybir.dt.float32, mybir.dt.float16, mybir.dt.int32
ALU = mybir.AluOpType
ACT = mybir.ActivationFunctionType
AX = mybir.AxisListType
ds = bass.ds

P = 128
D = 256
KD = D // P
NODES = 3125
TILES = -(-NODES // P)
ROWS = TILES * P
CT = 5
CHUNKS = TILES // CT
CH = CT * P
SUB = CH // 2
EDGES = 103125
ETILES = -(-EDGES // P)
W = 9
VIS = 4
WINS = 348
PAIRS = WINS // 2
UNROLL = 6
WG = 3
NW = TILES * W
EG = 7
EPAD = (EG * P + 1) * P
SG = 13
SSTEPS = ETILES // SG
FAR = 4096
SPLIT = 2048.0
XS = 1024.0
EPS = 1e-5
E0, H0 = 8, 512
HB = H0 // P
ST = 256
STMAX = (2 * ROWS + E0 * (ST - 1)) // ST
SLOTS = STMAX * ST
E1, SH1, SH2, EH1, EH2 = 4, 256, 128, 128, 64

assert W * WINS >= NODES and SSTEPS * SG == ETILES and CHUNKS * CT == TILES
assert PAIRS % UNROLL == 0 and STMAX % 2 == 0


class Chain:

    def __init__(self, eng, sem):
        self.eng, self.sem, self.base, self.n = eng, sem, 0, 0

    def mark(self, ins):
        ins.then_inc(self.sem, 1)
        self.n += 1
        return self.base + self.n

    def wait(self):
        self.eng.wait_ge(self.sem, self.base + self.n)

    def done(self, ins):
        self.mark(ins)
        self.wait()

    @contextmanager
    def loop(self, start, end, per):
        before = self.n
        with self.eng.Fori(start, end) as i:
            self.base, self.n = before + (i - start) * per, 0
            yield i
            assert self.n == per, (self.n, per)
        self.base, self.n = 0, before + (end - start) * per


class Prog:

    def __init__(self, nc, ctx, tag=""):
        self.nc, self.ctx, self.tag, self.sems = nc, ctx, tag, []
        ctx.callback(self.clear)

    def clear(self):
        if self.sems:
            self.nc.clear_and_free_semaphores(self.sems)
            self.nc.all_engine_barrier(sem_only=True)

    def sb(self, name, shape, dt):
        return self.ctx.enter_context(self.nc.sbuf_tensor(self.tag + name, shape, dt))

    def ps(self, name, shape, dt=F32):
        return self.ctx.enter_context(self.nc.psum_tensor(self.tag + name, shape, dt))

    def sem(self, name):
        self.sems.append(self.nc.alloc_semaphore(self.tag + name))
        return self.sems[-1]


NORM_MARKS = 2 * CT + 5


def norm_stats(nc, ch, rows, st, mv, var_ready, rstd_from, n, rstd, tmp):
    for t in range(CT):
        ch.mark(nc.vector.bn_stats(st[:, t, :], rows[:, t, :]))
    ch.wait()
    nc.vector.memset(tmp[:, 3, :], 0.0)
    for t in range(CT):
        ch.mark(nc.vector.bn_aggr(mv[:, t, :], st[:, t, :]))
    ch.wait()
    ins = nc.vector.tensor_scalar(tmp[:, 0, :], mv[:, :, 1], EPS, None, ALU.add)
    ins.then_inc(var_ready, 1)
    ch.eng.wait_ge(rstd_from, n)
    ch.done(nc.vector.reciprocal(tmp[:, 1, :], tmp[:, 2, :]))
    ch.done(nc.vector.tensor_tensor(tmp[:, 3, :], tmp[:, 1, :], tmp[:, 1, :], ALU.mult))
    ch.done(nc.vector.tensor_tensor(tmp[:, 4, :], tmp[:, 3, :], tmp[:, 0, :], ALU.mult))
    ch.done(nc.vector.tensor_scalar(tmp[:, 5, :], tmp[:, 4, :], -0.5, 1.5, ALU.mult, ALU.add))
    ch.done(nc.vector.tensor_tensor(rstd[:, :], tmp[:, 1, :], tmp[:, 5, :], ALU.mult))


def norm_apply(nc, ch, out, rows, mv, rstd):
    for t in range(CT):
        ch.mark(nc.vector.tensor_scalar(out[:, t, :], rows[:, t, :], mv[:, t, 0:1], rstd[:, t:t + 1],
                                        ALU.subtract, ALU.mult))


def root(nc, act, tmp, var_ready, root_done, n):
    act.wait_ge(var_ready, n)
    nc.scalar.activation(tmp[:, 2, :], tmp[:, 0, :], ACT.Sqrt).then_inc(root_done, 1)


def transposed_place(bank, f, t):
    return bank[f][:, t * P:(t + 1) * P] if t < CT - 1 else bank[2][:, f * P:(f + 1) * P]


def transpose_chunk(nc, pe, bank, rows, ident):
    for t in range(CT):
        for f in range(KD):
            last = nc.tensor.transpose(transposed_place(bank, f, t), rows[:, t, f * P:(f + 1) * P], ident[:, :])
    return last


def evacuate_transposed(nc, bank, out):
    four = (CT - 1) * P
    nc.scalar.activation(out[:, 0, 0:four], bank[0][:, 0:four], ACT.Copy)
    nc.scalar.activation(out[:, 1, 0:four], bank[1][:, 0:four], ACT.Copy)
    return nc.scalar.activation(out[:, :, four:CH], bank[2][:, 0:2 * P].rearrange("p (f n) -> p f n", f=KD), ACT.Copy)


def normalise(nc, g, tag, rows_from, rows_to=None, idx=None, setup=False):
    with ExitStack() as ctx:
        pr = Prog(nc, ctx, tag)
        xr = pr.sb("rows", [P, CT, D], F32)
        xn = pr.sb("norm", [P, CT, D], F32)
        part = pr.sb("part", [P, CT, 2, D], F16)
        xt = pr.sb("xt", [P, KD, CH], F32)
        st = pr.sb("st", [P, CT, 6], F32)
        mv = pr.sb("mv", [P, CT, 2], F32)
        tmp = pr.sb("tmp", [P, 6, CT], F32)
        rstd = pr.sb("rstd", [P, CT], F32)
        spare = pr.sb("spare", [P, 1], F32)
        if idx is not None:
            chosen = pr.sb("chosen", [P, 2, CT, D], F32)
            off = pr.sb("off", [P, 2, CT], I32)
        if setup:
            zero = pr.sb("zero", [P, 8 * D], F32)
        bank = [pr.ps(f"ps{i}", [P, 512]) for i in range(3)]
        s = {n: pr.sem(n) for n in ("rows_in", "var_ready", "root_done", "norm_done", "rows_free", "high_done",
                                    "parts_done", "chain", "turned", "xt_ready", "part_out", "xt_out", "zero_ready",
                                    "zero_out", "ident_ready", "pool_chain", "gathered", "summed", "sum_out",
                                    "off_ready")}
        block = ctx.enter_context(nc.Block())
        chunk_of = lambda ap, at: ap.rearrange("(t p) d -> p t d", p=P)[:, ds(at, CT), :]

        @block.sync
        def _(sp):
            with sp.Fori(0, CHUNKS) as c:
                at, to = sp.snap(c * CT), sp.snap(c * (CT * 2 * D))
                if idx is not None:
                    sp.wait_ge(s["sum_out"], 16 * c)
                sp.wait_ge(s["rows_free"], c)
                sp.dma_start(xr[:, :, :], chunk_of(rows_from, at)).then_inc(s["rows_in"], 16)
                sp.wait_ge(s["parts_done"], c + 1)
                sp.dma_start(g["parts"][:, ds(to, CT * 2 * D)],
                             part[:, :, :, :].rearrange("p t a d -> p (t a d)")).then_inc(s["part_out"], 16)
            sp.wait_ge(s["part_out"], 16 * CHUNKS)

        @block.vector
        def _(dve):
            ch = Chain(dve, s["chain"])
            if setup:
                nc.vector.memset(zero[:, :], 0.0).then_inc(s["zero_ready"], 1)
            with ch.loop(0, CHUNKS, NORM_MARKS + CT + (4 if idx is not None else 0)) as c:
                dve.wait_ge(s["rows_in"], 16 * (c + 1))
                if idx is not None:
                    dve.wait_ge(s["gathered"], 16 * 2 * CT * c)
                    ch.mark(nc.vector.tensor_copy(off[:, 0, :], idx[:, 0, ds(c * CT, CT)]))
                    ch.done(nc.vector.tensor_copy(off[:, 1, :], idx[:, 1, ds(c * CT, CT)]))
                    nc.vector.memset(spare[:, :], 0.0).then_inc(s["off_ready"], 1)
                    dve.wait_ge(s["gathered"], 16 * 2 * CT * (c + 1))
                    for n in range(2):
                        ch.done(nc.vector.tensor_tensor(xr[:, :, :], xr[:, :, :], chosen[:, n, :, :], ALU.add))
                    nc.vector.memset(tmp[:, 5, :], 0.0).then_inc(s["summed"], 1)
                norm_stats(nc, ch, xr, st, mv, s["var_ready"], s["root_done"], c + 1, rstd, tmp)
                dve.wait_ge(s["turned"], c)
                norm_apply(nc, ch, xn, xr, mv, rstd)
                ch.wait()
                nc.vector.tensor_copy(spare[:, :], mv[:, 0, 0:1]).then_inc(s["norm_done"], 1)
                dve.wait_ge(s["part_out"], 16 * c)
                nc.vector.tensor_scalar(part[:, :, 0, :], xn[:, :, :], XS, None, ALU.mult).then_inc(s["high_done"], 1)
                dve.wait_ge(s["high_done"], c + 1)
                nc.vector.scalar_tensor_tensor(part[:, :, 1, :], xn[:, :, :], XS, part[:, :, 0, :],
                                               ALU.mult, ALU.subtract).then_inc(s["parts_done"], 1)

        @block.scalar
        def _(act):
            with act.Fori(0, CHUNKS) as c:
                if idx is not None:
                    act.wait_ge(s["summed"], c + 1)
                    act.dma_start(chunk_of(rows_to, c * CT), xr[:, :, :]).then_inc(s["sum_out"], 16)
                root(nc, act, tmp, s["var_ready"], s["root_done"], c + 1)
                act.wait_ge(s["norm_done"], c + 1)
                act.sem_inc(s["rows_free"], 1)
                act.wait_ge(s["turned"], c + 1)
                act.wait_ge(s["xt_out"], 16 * c)
                evacuate_transposed(nc, bank, xt).then_inc(s["xt_ready"], 1)
                act.wait_ge(s["xt_ready"], c + 1)
                act.dma_start(g["xt"][:, :, ds(c * CH, CH)], xt[:, :, :]).then_inc(s["xt_out"], 16)
            act.wait_ge(s["xt_out"], 16 * CHUNKS)
            if idx is not None:
                act.wait_ge(s["sum_out"], 16 * CHUNKS)

        @block.tensor
        def _(pe):
            if setup:
                pe.wait_ge(s["ident_ready"], 1)
            with pe.Fori(0, CHUNKS) as c:
                pe.wait_ge(s["norm_done"], c + 1)
                pe.wait_ge(s["xt_ready"], c)
                transpose_chunk(nc, pe, bank, xn, g["ident"]).then_inc(s["turned"], 1)

        @block.gpsimd
        def _(pool):
            if setup:
                nc.gpsimd.memset(g["ident"][:, :], 0.0).then_inc(s["pool_chain"], 1)
                pool.wait_ge(s["pool_chain"], 1)
                nc.gpsimd.affine_select(out=g["ident"][:, :], in_=g["ident"][:, :], compare_op=ALU.not_equal, fill=1.0,
                                        base=0, pattern=[[-1, P]], channel_multiplier=1).then_inc(s["ident_ready"], 1)
                pool.wait_ge(s["zero_ready"], 1)
                for n in range(SLOTS // (8 * P)):
                    pool.dma_start(g["slots_in"][n * 8 * P:(n + 1) * 8 * P, :].rearrange("(p r) d -> p (r d)", r=8),
                                   zero[:, :]).then_inc(s["zero_out"], 16)
                sure = 2 * ROWS // ST * ST
                half = (SLOTS - sure) // 2
                for n in range(2):
                    pool.dma_start(g["slots_out"][sure + n * half:sure + (n + 1) * half, :].rearrange("(p r) d -> p (r d)", p=P),
                                   zero[:, 0:half // P * D]).then_inc(s["zero_out"], 16)
                pool.wait_ge(s["zero_out"], 16 * (SLOTS // (8 * P) + 2))
            if idx is not None:
                for c in range(CHUNKS):
                    pool.wait_ge(s["rows_free"], c)
                    pool.wait_ge(s["off_ready"], c + 1)
                    for n in range(2):
                        for t in range(CT):
                            pool.indirect_dma_start(out=chosen[:, n, t, :], out_offset=None, in_=g["slots_out"],
                                                    in_offset=bass.IndirectOffsetOnAxis(ap=off[:, n, t:t + 1], axis=0)
                                                    ).then_inc(s["gathered"], 16)


def window_keys(nc, io, g):
    with ExitStack() as ctx:
        pr = Prog(nc, ctx)
        dt = pr.sb("w_dst", [P, EG, P], I32)
        dn = pr.sb("w_next", [P, EG, P], I32)
        key = pr.sb("w_key", [P, WINS * VIS, 2], F16)
        low7 = pr.sb("w_low7", [P, WINS * VIS, 2], F16)
        wi = pr.sb("w_iota", [P, WG * P], I32)
        wlo = pr.sb("w_lo", [P, WG * P], F32)
        whi = pr.sb("w_hi", [P, WG * P], F32)
        first = pr.sb("w_first", [P, EG], F32)
        gt = pr.sb("w_gt", [P, EG * P], F32)
        below = pr.sb("w_below", [P, 2, EG, WG * P], F16)
        ones16 = pr.sb("w_ones16", [P, 1], F16)
        ones = pr.sb("w_ones", [P, 1], F32)
        m = pr.sb("w_m", [P, 2, WG], F32)
        lo = pr.sb("w_lotile", [P, 2, WG], F32)
        over = pr.sb("w_over", [P, WG + 1], F32)
        bad = pr.sb("w_bad", [P, 1], F32)
        idx = pr.sb("w_idx", [P, VIS, WG], I32)
        gd = pr.sb("w_gd", [P, WG, VIS, P], I32)
        gs = pr.sb("w_gs", [P, WG, VIS, P], I32)
        ints = pr.sb("w_ints", [P, 2, WG * VIS * P], I32)
        fl = pr.sb("w_fl", [P, 3, WG, VIS, P], F32)
        tr = pr.sb("w_tr", [P, 3, WG * P, VIS], F32)
        pm = pr.ps("w_pm", [P, 2 * WG])
        pt = [pr.ps(f"w_pt{i}", [P, VIS, P]) for i in range(3)]
        pf = pr.ps("w_pf", [P, 1])
        dst_in, iota_ready, below_ready = pr.sem("dst_in"), pr.sem("iota_ready"), pr.sem("below_ready")
        chain, counted, idx_ready, gathered = (pr.sem("vector_chain"), pr.sem("counted"), pr.sem("idx_ready"),
                                               pr.sem("gathered"))
        fl_ready, turned, taken, bad_ready, summed = (pr.sem("fl_ready"), pr.sem("turned"), pr.sem("taken"),
                                                      pr.sem("bad_ready"), pr.sem("summed"))
        keys_ready, keys_out = pr.sem("keys_ready"), pr.sem("keys_out")
        block = ctx.enter_context(nc.Block())
        N = WG * VIS * P

        @block.sync
        def _(sp):
            sp.dma_start(dt[:, :, :], io["dst"][0:EG * P * P].rearrange("(g p e) -> p g e", p=P, e=P)).then_inc(dst_in, 16)
            sp.dma_start(dn[:, :, :], io["dst"][1:EG * P * P + 1].rearrange("(g p e) -> p g e", p=P, e=P)).then_inc(dst_in, 16)
            sp.wait_ge(keys_ready, 2)
            sp.dma_start(g["keys"][0], key[:, :, :]).then_inc(keys_out, 16)
            sp.dma_start(g["keys"][1], low7[:, :, :]).then_inc(keys_out, 16)
            sp.wait_ge(keys_out, 32)

        @block.gpsimd
        def _(pool):
            nc.gpsimd.iota(wi[:, :], pattern=[[W, WG * P]], base=0, channel_multiplier=0).then_inc(iota_ready, 1)
            pool.wait_ge(idx_ready, 1)
            for w in range(WG):
                for i in range(VIS):
                    for rows, to in ((io["dst"], gd), (io["src"], gs)):
                        pool.indirect_dma_start(out=to[:, w, i, :], out_offset=None, in_=rows.rearrange("(t e) -> t e", e=P),
                                                in_offset=bass.IndirectOffsetOnAxis(ap=idx[:, i, w:w + 1], axis=0)
                                                ).then_inc(gathered, 16)

        @block.vector
        def _(dve):
            ch = Chain(dve, chain)
            ch.mark(nc.vector.memset(ones16[:, :], 1.0))
            ch.mark(nc.vector.memset(ones[:, :], 1.0))
            dve.wait_ge(iota_ready, 1)
            ch.mark(nc.vector.tensor_copy(wlo[:, :], wi[:, :]))
            ch.mark(nc.vector.tensor_scalar(whi[:, :], wi[:, :], float(W), None, ALU.add))
            dve.wait_ge(dst_in, 32)
            ch.mark(nc.vector.tensor_copy(first[:, :], dt[:, :, 0]))
            ch.done(nc.vector.tensor_tensor(gt[:, :], dt[:, :, :].rearrange("p g e -> p (g e)"),
                                            dn[:, :, :].rearrange("p g e -> p (g e)"), ALU.is_gt))
            ch.mark(nc.vector.reduce_sum(over[:, WG:WG + 1], gt[:, :], AX.X))
            for n, edge in ((0, wlo), (1, whi)):
                for q in range(EG):
                    last = nc.vector.tensor_scalar(below[:, n, q, :], edge[:, :], first[:, q:q + 1], None, ALU.is_gt)
            last.then_inc(below_ready, 1)
            dve.wait_ge(counted, 1)
            ch.done(nc.vector.tensor_copy(m[:, :, :], pm[:, :].rearrange("p (n w) -> p n w", n=2)))
            ch.done(nc.vector.tensor_scalar(lo[:, 0, :], m[:, 0, :], -1.0, 0.0, ALU.add, ALU.max))
            for i in range(VIS):
                last = nc.vector.tensor_scalar(idx[:, i, :], lo[:, 0, :], float(i), None, ALU.add)
            last.then_inc(idx_ready, 1)
            ch.done(nc.vector.tensor_tensor(lo[:, 1, :], m[:, 1, :], lo[:, 0, :], ALU.subtract))
            ch.done(nc.vector.tensor_scalar(over[:, 0:WG], lo[:, 1, :], float(VIS), None, ALU.is_gt))
            nc.vector.reduce_sum(bad[:, :], over[:, :], AX.X).then_inc(bad_ready, 1)
            dve.wait_ge(summed, 1)
            ch.mark(nc.vector.tensor_copy(g["flag"][0:1, 0:1], pf[0:1, 0:1]))
            dve.wait_ge(gathered, 16 * 2 * WG * VIS)
            src = gs[:, :, :, :].rearrange("p w i e -> p (w i e)")
            dst = gd[:, :, :, :].rearrange("p w i e -> p (w i e)")
            flat = fl[:, :, :, :, :].rearrange("p a w i e -> p a (w i e)")
            ch.mark(nc.vector.tensor_scalar(ints[:, 0, :], src, 7, None, ALU.logical_shift_right))
            ch.done(nc.vector.tensor_scalar(ints[:, 1, :], src, P - 1, None, ALU.bitwise_and))
            ch.mark(nc.vector.tensor_copy(flat[:, 0, :], dst))
            ch.mark(nc.vector.scalar_tensor_tensor(flat[:, 1, :], ints[:, 0, :], float(W), dst, ALU.mult, ALU.add))
            nc.vector.tensor_copy(flat[:, 2, :], ints[:, 1, :]).then_inc(fl_ready, 1)
            dve.wait_ge(fl_ready, 1)
            for n in range(3 * WG):
                a, w = divmod(n, WG)
                dve.wait_ge(turned, n + 1)
                nc.vector.tensor_copy(tr[:, a, w * P:(w + 1) * P, :].rearrange("p v i -> p i v"),
                                      pt[n % 3][:, :, :]).then_inc(taken, 1)
            dve.wait_ge(taken, 3 * WG)
            base = wlo[:, :].unsqueeze(2).broadcast_to([P, WG * P, VIS])
            t1, t2 = fl[:, 0, :, :, :].rearrange("p w i e -> p (w i e)"), fl[:, 1, :, :, :].rearrange("p w i e -> p (w i e)")
            u = fl[:, 2, :, :, :].rearrange("p w i e -> p (w i e)")
            three = lambda ap: ap.rearrange("p (v i) -> p v i", i=VIS)
            ch.mark(nc.vector.tensor_tensor(three(t1), tr[:, 0, :, :], base, ALU.subtract))
            ch.done(nc.vector.tensor_tensor(three(t2), tr[:, 1, :, :], base, ALU.subtract))
            ch.done(nc.vector.tensor_scalar(t2, t2, 1.0, None, ALU.add))
            ch.done(nc.vector.scalar_tensor_tensor(u, t1, 0.0, t2, ALU.is_ge, ALU.mult))
            n = WINS * VIS
            twice = lambda ap: ap.unsqueeze(2).broadcast_to([P, n, 2])
            nc.vector.scalar_tensor_tensor(key[:, :, :], twice(t1[:, 0:n]), float(W), twice(u[:, 0:n]),
                                           ALU.is_lt, ALU.mult).then_inc(keys_ready, 1)
            nc.vector.tensor_copy(low7[:, :, :],
                                  twice(tr[:, 2, :, :].rearrange("p v i -> p (v i)")[:, 0:n])).then_inc(keys_ready, 1)

        @block.tensor
        def _(pe):
            pe.wait_ge(below_ready, 1)
            for n in range(2):
                for w in range(WG):
                    for q in range(EG):
                        last = nc.tensor.matmul(pm[:, n * WG + w:n * WG + w + 1], below[:, n, q, w * P:(w + 1) * P],
                                                ones16[:, :], start=(q == 0), stop=(q == EG - 1))
            last.then_inc(counted, 1)
            pe.wait_ge(bad_ready, 1)
            nc.tensor.matmul(pf[0:1, 0:1], bad[:, :], ones[:, :], start=True, stop=True).then_inc(summed, 1)
            pe.wait_ge(fl_ready, 1)
            for n in range(3 * WG):
                a, w = divmod(n, WG)
                if n >= 3:
                    pe.wait_ge(taken, n - 2)
                for i in range(VIS):
                    last = nc.tensor.transpose(pt[n % 3][:, i, :], fl[:, a, w, i, :], g["ident"][:, :])
                last.then_inc(turned, 1)


def aggregate(nc, pe, flag, adj, at, stationary, bank, hib, hi_in, hi_used, n):
    def tile(k, moving, first=False, last=False):
        seen = set()
        ops = stationary(k)
        for j, (f, operand) in enumerate(ops):
            ins = nc.tensor.matmul(bank[f], operand, moving, start=first and f not in seen,
                                   stop=last and f not in [x for x, _ in ops[j + 1:]])
            seen.add(f)
        return ins

    tile(0, adj[:, 0, at], first=True)
    with pe.If(flag != 0):
        with pe.Fori(0, TILES) as k:
            pe.wait_ge(hi_in, 16 * (n * TILES + k + 1))
            tile(k, hib[:, :])
            tile(k, hib[:, :]).then_inc(hi_used, 1)
    with pe.Else():
        pe.nop()
    for k in range(1, TILES):
        ins = tile(k, adj[:, k, at], last=(k == TILES - 1))
    return ins


def feed_upper_counts(sp, g, flag, hib, hi_in, hi_used):
    with sp.If(flag != 0):
        with sp.Fori(0, 2 * CHUNKS) as n:
            with sp.Fori(0, TILES) as k:
                sp.wait_ge(hi_used, n * TILES + k)
                sp.dma_start(hib[:, :], g["upper"][ds(k * P, P), ds(n * SUB, SUB)]).then_inc(hi_in, 16)
    with sp.Else():
        sp.nop()


def build_counts(nc, io, g, adj):
    with ExitStack() as ctx:
        pr = Prog(nc, ctx)
        key = pr.sb("b_key", [P, WINS * VIS, 2], F16)
        low7 = pr.sb("b_low7", [P, WINS * VIS, 2], F16)
        it = pr.sb("b_it", [P, 512], I32)
        it16 = pr.sb("b_it16", [P, NW + 1], F16)
        ib16 = pr.sb("b_ib16", [P, P], F16)
        ones = pr.sb("b_ones", [P, P], F16)
        sel = pr.sb("b_sel", [P, 4 * VIS, NW + 1], F16)
        low = pr.sb("b_low", [P, 4 * VIS, P], F16)
        degree = pr.sb("b_degree", [P, 2, SUB], F32)
        inv = pr.sb("b_inv", [P, 2, SUB], F32)
        win = pr.sb("b_win", [P, WINS], F32)
        gst = pr.sb("g_st", [P, 2, SG], I32)
        gi = pr.sb("g_int", [P, 2, SG], I32)
        gf = pr.sb("g_fl", [P, 3, SG], F32)
        gk = pr.sb("g_key", [P, SG, 2], F16)
        gl = pr.sb("g_low", [P, SG, 2], F16)
        gc = pr.sb("g_count", [P, 3, NW], I32)
        ghi = pr.sb("g_hi", [P, NW], F16)
        hib = pr.sb("g_hib", [P, SUB], F16)
        pw = [pr.ps(f"b_pw{i}", [P, 512]) for i in range(2)]
        pd = [pr.ps(f"b_pd{i}", [P, SUB]) for i in range(2)]
        s = {n: pr.sem("b_" + n) for n in (
            "const", "chain", "ready", "sel_ready", "multiplied", "copied", "g_in", "g_sel", "g_mult", "g_win",
            "g_split", "g_copied", "g_hi_out", "g_edge", "hi_in", "hi_used", "deg", "degree", "inv_done", "inv_out", "adj_done", "keys_in")}
        block = ctx.enter_context(nc.Block())
        NWIN = WINS * W

        def one_hot(out, values, names, width):
            r = values.shape[1]
            shape = [P, r, width // 2, 2]
            return nc.vector.tensor_tensor(
                out.rearrange("p r (h two) -> p r h two", two=2),
                names[:, 0:width].rearrange("p (h two) -> p h two", two=2).unsqueeze(1).broadcast_to(shape),
                values.unsqueeze(2).broadcast_to(shape), ALU.is_equal)

        @block.gpsimd
        def _(pool):
            nc.gpsimd.iota(it[:, :], pattern=[[1, 512]], base=0, channel_multiplier=0).then_inc(s["const"], 1)

        @block.vector
        def _(dve):
            ch = Chain(dve, s["chain"])
            dve.wait_ge(s["const"], 1)
            ch.mark(nc.vector.tensor_copy(it16[:, :], it[:, 1:NW + 2]))
            ch.mark(nc.vector.tensor_copy(ib16[:, :], it[:, 0:P]))
            ch.mark(nc.vector.memset(ones[:, :], 1.0))
            ch.mark(nc.vector.tensor_scalar(win[:, :], it[:, 0:WINS], float(W), None, ALU.mult))
            ch.mark(nc.vector.memset(adj[:, :, NWIN:ROWS], 0.0))
            ch.wait()
            nc.vector.memset(gf[:, 0, :], 0.0).then_inc(s["ready"], 1)
            dve.wait_ge(s["ready"], 1)
            flag = dve.value_load(g["flag"][0:1, 0:1])
            with dve.If(flag != 0):
                with dve.Fori(0, WINS) as v:
                    with dve.Fori(0, SSTEPS) as u:
                        n = v * SSTEPS + u
                        gch = Chain(dve, s["g_edge"])
                        gch.base = (n * 6) + v * 3
                        dve.wait_ge(s["g_in"], 32 * (n + 1))
                        gch.mark(nc.vector.tensor_scalar(gi[:, 0, :], gst[:, 1, :], 7, None, ALU.logical_shift_right))
                        gch.mark(nc.vector.tensor_scalar(gi[:, 1, :], gst[:, 1, :], P - 1, None, ALU.bitwise_and))
                        gch.done(nc.vector.tensor_scalar(gf[:, 0, :], gst[:, 0, :], win[:, ds(v, 1)], None, ALU.subtract))
                        gch.done(nc.vector.scalar_tensor_tensor(gf[:, 1, :], gi[:, 0, :], float(W), gf[:, 0, :],
                                                                ALU.mult, ALU.add))
                        gch.done(nc.vector.tensor_scalar(gf[:, 2, :], gf[:, 1, :], 1.0, None, ALU.add))
                        dve.wait_ge(s["g_mult"], n)
                        gch.done(nc.vector.scalar_tensor_tensor(gf[:, 1, :], gf[:, 0, :], 0.0, gf[:, 2, :],
                                                                ALU.is_ge, ALU.mult))
                        two = lambda ap: ap.unsqueeze(2).broadcast_to([P, SG, 2])
                        nc.vector.scalar_tensor_tensor(gk[:, :, :], two(gf[:, 0, :]), float(W), two(gf[:, 1, :]),
                                                       ALU.is_lt, ALU.mult).then_inc(s["g_split"], 1)
                        nc.vector.tensor_copy(gl[:, :, :], two(gi[:, 1, :])).then_inc(s["g_split"], 1)
                        dve.wait_ge(s["g_split"], 2 * (n + 1))
                        one_hot(sel[:, 0:SG, :], gk[:, :, :], it16, NW + 1)
                        one_hot(low[:, 0:SG, :], gl[:, :, :], ib16, P).then_inc(s["g_sel"], 1)
                    gch = Chain(dve, s["g_edge"])
                    gch.base = (v + 1) * SSTEPS * 6 + v * 3
                    dve.wait_ge(s["g_win"], v + 1)
                    gch.done(nc.vector.tensor_copy(gc[:, 0, :], pw[0][:, 0:NW]))
                    gch.mark(nc.vector.tensor_scalar(gc[:, 1, :], gc[:, 0, :], 11, None, ALU.logical_shift_right))
                    gch.done(nc.vector.tensor_scalar(gc[:, 2, :], gc[:, 0, :], int(SPLIT) - 1, None, ALU.bitwise_and))
                    dve.wait_ge(s["g_hi_out"], 16 * (v + 1))
                    nc.vector.tensor_copy(adj[:, :, ds(v * W, W)], gc[:, 2, :].rearrange("p (k j) -> p k j", j=W))
                    nc.vector.tensor_scalar(ghi[:, :], gc[:, 1, :], SPLIT / 2, None, ALU.mult).then_inc(s["g_copied"], 1)
                dve.wait_ge(s["g_copied"], WINS)
                nc.vector.memset(gf[:, 0, :], 0.0).then_inc(s["adj_done"], 1)
            with dve.Else():
                dve.wait_ge(s["keys_in"], 32)
                with dve.Fori(0, PAIRS // UNROLL) as body:
                    for u in range(UNROLL):
                        pair = body * UNROLL + u
                        at, slot = ds(pair * 2 * VIS, 2 * VIS), slice(u % 2 * 2 * VIS, (u % 2 + 1) * 2 * VIS)
                        dve.wait_ge(s["multiplied"], pair)
                        one_hot(sel[:, slot, :], key[:, at, :], it16, NW + 1)
                        one_hot(low[:, slot, :], low7[:, at, :], ib16, P).then_inc(s["sel_ready"], 1)
            with dve.Fori(0, CHUNKS) as c:
                for half in range(2):
                    dve.wait_ge(s["deg"], 2 * c + half + 1)
                    nc.vector.tensor_scalar(degree[:, half, :], pd[half][:, :], 1.0, XS, ALU.max, ALU.mult
                                            ).then_inc(s["degree"], 1)
                    dve.wait_ge(s["inv_out"], 32 * c)
                    dve.wait_ge(s["degree"], 2 * c + half + 1)
                    nc.vector.reciprocal(inv[:, half, :], degree[:, half, :]).then_inc(s["inv_done"], 1)

        @block.scalar
        def _(act):
            act.wait_ge(s["ready"], 1)
            flag = act.value_load(g["flag"][0:1, 0:1])
            with act.If(flag != 0):
                act.nop()
            with act.Else():
                act.sem_inc(s["copied"], 1)
                with act.Fori(0, PAIRS // UNROLL) as body:
                    for u in range(UNROLL):
                        pair = body * UNROLL + u
                        act.wait_ge(s["multiplied"], pair + 2)
                        nc.scalar.activation(
                            adj[:, :, ds(pair * 2 * W, 2 * W)].rearrange("p k (w j) -> p w k j", j=W),
                            pw[u % 2][:, 0:2 * NW].rearrange("p (w k j) -> p w k j", w=2, j=W), ACT.Copy).then_inc(s["copied"], 1)
                act.wait_ge(s["copied"], PAIRS + 1)
                act.sem_inc(s["adj_done"], 1)
            with act.Fori(0, CHUNKS) as c:
                for half in range(2):
                    act.wait_ge(s["inv_done"], 2 * c + half + 1)
                    act.dma_start(g["inv"][:, ds(c * CH + half * SUB, SUB)], inv[0:1, half, :]).then_inc(s["inv_out"], 16)
            act.wait_ge(s["inv_out"], 32 * CHUNKS)

        @block.tensor
        def _(pe):
            pe.wait_ge(s["ready"], 1)
            pe.sem_inc(s["multiplied"], 1)
            flag = pe.value_load(g["flag"][0:1, 0:1])
            with pe.If(flag != 0):
                with pe.Fori(0, WINS) as v:
                    def step(n, first):
                        pe.wait_ge(s["g_sel"], n + 1)
                        for i in range(SG):
                            ins = nc.tensor.matmul(pw[0][:, 0:NW], low[:, i, :], sel[:, i, 0:NW],
                                                   start=first and i == 0, stop=i == SG - 1)
                        ins.then_inc(s["g_mult"], 1)
                    pe.wait_ge(s["g_copied"], v)
                    step(v * SSTEPS, True)
                    with pe.Fori(1, SSTEPS) as u:
                        step(v * SSTEPS + u, False)
                    pe.wait_ge(s["g_mult"], (v + 1) * SSTEPS)
                    pe.sem_inc(s["g_win"], 1)
            with pe.Else():
                with pe.Fori(0, PAIRS // UNROLL) as body:
                    for u in range(UNROLL):
                        pair = body * UNROLL + u
                        pe.wait_ge(s["sel_ready"], pair + 1)
                        pe.wait_ge(s["copied"], pair)
                        for w in range(2):
                            for i in range(VIS):
                                n = u % 2 * 2 * VIS + w * VIS + i
                                ins = nc.tensor.matmul(pw[u % 2][:, w * NW:(w + 1) * NW], low[:, n, :], sel[:, n, 0:NW],
                                                       start=i == 0, stop=i == VIS - 1)
                        ins.then_inc(s["multiplied"], 1)
            pe.wait_ge(s["adj_done"], 1)
            with pe.Fori(0, CHUNKS) as c:
                for half in range(2):
                    pe.wait_ge(s["inv_done"], 2 * c)
                    aggregate(nc, pe, flag, adj, ds(c * CH + half * SUB, SUB), lambda k: [(0, ones[:, :])],
                              [pd[half][:, :]], hib, s["hi_in"], s["hi_used"], 2 * c + half).then_inc(s["deg"], 1)

        @block.sync
        def _(sp):
            sp.dma_start(key[:, :, :], g["keys"][0]).then_inc(s["keys_in"], 16)
            sp.dma_start(low7[:, :, :], g["keys"][1]).then_inc(s["keys_in"], 16)
            sp.wait_ge(s["ready"], 1)
            flag = sp.value_load(g["flag"][0:1, 0:1])
            with sp.If(flag != 0):
                sp.dma_start(g["upper"].rearrange("(k p) n -> p k n", p=P)[:, :, NWIN:ROWS],
                             adj[:, :, NWIN:ROWS]).then_inc(s["g_hi_out"], 16)
                with sp.Fori(0, WINS) as v:
                    with sp.Fori(0, SSTEPS) as u:
                        sp.wait_ge(s["g_sel"], v * SSTEPS + u)
                        for n, rows in enumerate((io["dst"], io["src"])):
                            sp.dma_start(gst[:, n, :], rows.rearrange("(t e) -> e t", e=P)[:, ds(u * SG, SG)],
                                         allow_slow_non_contiguous=True).then_inc(s["g_in"], 16)
                    sp.wait_ge(s["g_copied"], v + 1)
                    sp.dma_start(g["upper"].rearrange("(k p) n -> p k n", p=P)[:, :, ds(v * W, W)],
                                 ghi[:, :].rearrange("p (k j) -> p k j", j=W)).then_inc(s["g_hi_out"], 16)
                sp.wait_ge(s["g_hi_out"], 16 * (WINS + 1))
            with sp.Else():
                sp.nop()
            sp.wait_ge(s["adj_done"], 1)
            feed_upper_counts(sp, g, flag, hib, s["hi_in"], s["hi_used"])


BT = -(-CT // 2)


def in_bank(banks, n):
    count = min(2, CT - 2 * n)
    return slice(2 * n, 2 * n + count), banks[n][:, 0:count * D].rearrange("p (t d) -> p t d", d=D)


def conv_tensors(pr):
    t = {
        "parts": pr.sb("c_parts", [P, TILES, 2, D], F16),
        "inv": pr.sb("c_inv", [P, CH], F32),
        "mean": pr.sb("c_mean", [P, KD, CH], F32),
        "own": pr.sb("c_own", [P, KD, CH], F32),
        "wl": pr.sb("c_wl", [P, KD, D], F32),
        "wr": pr.sb("c_wr", [P, KD, D], F32),
        "hib": pr.sb("c_hib", [P, SUB], F16),
        "agg": [[pr.ps(f"c_agg{h}{f}", [P, SUB]) for f in range(KD)] for h in range(2)],
        "bank": [pr.ps(f"c_bank{i}", [P, 512]) for i in range(4)],
    }
    return t


def conv_tensor_engine(nc, g, adj, t, s, dense, turn):
    def agg(pe, flag, c, h):
        pe.wait_ge(s["mean_done"], 4 * c - 2 + 2 * h) if not isinstance(c, int) else None
        aggregate(nc, pe, flag, adj, ds(c * CH + h * SUB, SUB),
                  lambda k: [(f, t["parts"][:, k, a, f * P:(f + 1) * P]) for a in range(2) for f in range(KD)],
                  [t["agg"][h][f][:, :] for f in range(KD)], t["hib"], s["hi_in"], s["hi_used"], 2 * c + h
                  ).then_inc(s["agg_done"], 1)

    def run(pe):
        pe.wait_ge(s["parts_in"], 16)
        flag = pe.value_load(g["flag"][0:1, 0:1])
        agg(pe, flag, 0, 0)
        agg(pe, flag, 0, 1)
        with pe.Fori(1, CHUNKS) as c:
            agg(pe, flag, c, 0)
            dense(pe, c - 1)
            agg(pe, flag, c, 1)
            turn(pe, c - 1)
        dense(pe, CHUNKS - 1)
        turn(pe, CHUNKS - 1)
    return run


def mean_half(nc, dve, t, s, c, h):
    dve.wait_ge(s["agg_done"], 2 * c + h + 1)
    if h == 0:
        dve.wait_ge(s["inv_in"], 16 * (c + 1))
        dve.wait_ge(s["dense_done"], c)
    for f in range(KD):
        at = slice(h * SUB, (h + 1) * SUB)
        nc.vector.tensor_tensor(t["mean"][:, f, at], t["agg"][h][f][:, :], t["inv"][:, at], ALU.mult
                                ).then_inc(s["mean_done"], 1)


def load_chunk_inv(sp, g, t, s, c, at):
    sp.wait_ge(s["mean_done"], 4 * c)
    sp.dma_start(t["inv"][:, :], g["inv"][:, ds(at, CH)].broadcast_to([P, CH])).then_inc(s["inv_in"], 16)


CONV_SEMS = ("weights_in", "parts_in", "inv_in", "own_in", "agg_done", "mean_done", "dense_done", "hi_in",
             "hi_used", "chain", "ready", "turned", "stored")


def first_conv(nc, io, g, adj, tag, names):
    wl, b, wr = names
    with ExitStack() as ctx:
        pr = Prog(nc, ctx, tag)
        t = conv_tensors(pr)
        h = pr.sb("c_h", [P, KD, CH], F32)
        bias = pr.sb("c_bias", [P, KD], F32)
        small = pr.sb("c_small", [P, 6, KD], F32)
        part = t["own"][:, :, :].bitcast(F16).rearrange("p f n -> p (f n)").rearrange("p (t a d) -> p t a d", t=CT, a=2)
        s = {n: pr.sem("f_" + n) for n in CONV_SEMS + ("norms_in", "group_done", "h_done", "h_out", "high_done",
                                                       "low_done", "part_out", "scale_done")}
        block = ctx.enter_context(nc.Block())

        @block.sync
        def _(sp):
            sp.dma_start(t["parts"][:, :, :, :].rearrange("p t a d -> p (t a d)"), g["parts"]).then_inc(s["parts_in"], 16)
            sp.dma_start(bias[:, :], io[b].rearrange("(f p) -> p f", p=P), allow_slow_non_contiguous=True).then_inc(s["norms_in"], 16)
            sp.dma_start(t["mean"][:, :, 0:D], io[wl].rearrange("(f p) k -> p f k", p=P)).then_inc(s["norms_in"], 16)
            sp.dma_start(t["mean"][:, :, D:2 * D], io[wr].rearrange("(f p) k -> p f k", p=P)).then_inc(s["norms_in"], 16)
            sp.dma_start(t["wl"][:, :, :], io[wl + "_T"].rearrange("(k p) f -> p k f", p=P)).then_inc(s["weights_in"], 16)
            sp.dma_start(t["wr"][:, :, :], io[wr + "_T"].rearrange("(k p) f -> p k f", p=P)).then_inc(s["weights_in"], 16)

            with sp.Fori(0, CHUNKS) as c:
                at = sp.snap(c * CH)
                load_chunk_inv(sp, g, t, s, c, at)
                sp.wait_ge(s["part_out"], 16 * c)
                sp.dma_start(t["own"][:, :, :], g["xt"][:, :, ds(at, CH)]).then_inc(s["own_in"], 16)

        @block.gpsimd
        def _(pool):
            pool.wait_ge(s["parts_in"], 16)
            flag = pool.value_load(g["flag"][0:1, 0:1])
            feed_upper_counts(pool, g, flag, t["hib"], s["hi_in"], s["hi_used"])

        @block.vector
        def _(dve):
            ch = Chain(dve, s["chain"])
            dve.wait_ge(s["norms_in"], 48)
            for f in range(KD):
                ch.mark(nc.vector.tensor_reduce(small[:, 0, f:f + 1], t["mean"][:, f, 0:2 * D], AX.X, ALU.add,
                                                apply_absolute_value=True))
                ch.mark(nc.vector.tensor_reduce(small[:, 1, f:f + 1], bias[:, f:f + 1], AX.X, ALU.add,
                                                apply_absolute_value=True))
            ch.wait()
            ch.done(nc.vector.scalar_tensor_tensor(small[:, 2, :], small[:, 0, :], 16.0, small[:, 1, :], ALU.mult, ALU.add))
            ch.done(nc.vector.tensor_scalar(small[:, 3, :], small[:, 2, :], 1e-20, None, ALU.max))
            ch.done(nc.vector.tensor_scalar(small[:, 4, :].bitcast(I32), small[:, 3, :].bitcast(I32), 0x7F800000, None,
                                            ALU.bitwise_and))
            ch.done(nc.vector.tensor_scalar(g["unscale"][:, :], small[:, 4, :], 2.0 ** -14, None, ALU.mult))
            ch.done(nc.vector.reciprocal(g["scale"][:, :], g["unscale"][:, :]))
            nc.vector.tensor_tensor(small[:, 5, :], bias[:, :], g["scale"][:, :], ALU.mult).then_inc(s["scale_done"], 1)

            def low_parts(c):
                for n in range(BT):
                    dve.wait_ge(s["high_done"], BT * c + n + 1)
                    tiles, bank = in_bank(t["bank"], n)
                    nc.vector.tensor_tensor(part[:, tiles, 1, :], bank, part[:, tiles, 0, :], ALU.subtract
                                            ).then_inc(s["low_done"], 1)

            mean_half(nc, dve, t, s, 0, 0)
            mean_half(nc, dve, t, s, 0, 1)
            with dve.Fori(1, CHUNKS) as c:
                mean_half(nc, dve, t, s, c, 0)
                mean_half(nc, dve, t, s, c, 1)
                low_parts(c - 1)
            low_parts(CHUNKS - 1)

        @block.scalar
        def _(act):
            act.wait_ge(s["scale_done"], 1)
            with act.Fori(0, CHUNKS) as c:
                act.wait_ge(s["h_out"], 16 * c)
                act.wait_ge(s["turned"], BT * c)
                for n in range(4):
                    f, half = n % 2, n // 2
                    act.wait_ge(s["group_done"], 4 * c + n + 1)
                    nc.scalar.activation(h[:, f, half * SUB:(half + 1) * SUB], t["bank"][n][:, 0:SUB], ACT.Relu,
                                         bias=small[:, 5, f:f + 1], scale=g["scale"][:, f:f + 1]).then_inc(s["h_done"], 1)
                act.wait_ge(s["h_done"], 4 * (c + 1))
                act.dma_start(g["ht"][:, :, ds(c * CH, CH)], h[:, :, :]).then_inc(s["h_out"], 16)
                for n in range(BT):
                    act.wait_ge(s["turned"], BT * c + n + 1)
                    tiles, bank = in_bank(t["bank"], n)
                    nc.scalar.activation(part[:, tiles, 0, :], bank, ACT.Copy).then_inc(s["high_done"], 1)
                act.wait_ge(s["low_done"], BT * (c + 1))
                act.dma_start(g["parts"][:, ds(c * CT * 2 * D, CT * 2 * D)],
                              part.rearrange("p t a d -> p (t a d)")).then_inc(s["part_out"], 16)
            act.wait_ge(s["h_out"], 16 * CHUNKS)
            act.wait_ge(s["part_out"], 16 * CHUNKS)

        def dense(pe, c):
            pe.wait_ge(s["weights_in"], 32)
            pe.wait_ge(s["mean_done"], 4 * (c + 1))
            pe.wait_ge(s["own_in"], 16 * (c + 1))
            pe.wait_ge(s["low_done"], BT * c)
            for n in range(4):
                f, at = n % 2, slice(n // 2 * SUB, (n // 2 + 1) * SUB)
                for k in range(KD):
                    nc.tensor.matmul(t["bank"][n][:, 0:SUB], t["wl"][:, k, f * P:(f + 1) * P], t["mean"][:, k, at],
                                     start=k == 0, stop=False)
                for k in range(KD):
                    ins = nc.tensor.matmul(t["bank"][n][:, 0:SUB], t["wr"][:, k, f * P:(f + 1) * P], t["own"][:, k, at],
                                           start=False, stop=k == KD - 1)
                ins.then_inc(s["group_done"], 1)
            pe.wait_ge(s["group_done"], 4 * (c + 1))
            pe.sem_inc(s["dense_done"], 1)

        def turn(pe, c):
            pe.wait_ge(s["h_done"], 4 * (c + 1))
            for n in range(CT):
                for f in range(KD):
                    ins = nc.tensor.transpose(t["bank"][n // 2][:, n % 2 * D + f * P:n % 2 * D + (f + 1) * P],
                                              h[:, f, n * P:(n + 1) * P], g["ident"][:, :])
                if n % 2 or n == CT - 1:
                    ins.then_inc(s["turned"], 1)

        block.tensor(conv_tensor_engine(nc, g, adj, t, s, dense, turn))


def second_conv(nc, io, g, adj, tag, names, rows_from, rows_to, keep_norm):
    wl, b, wr = names
    with ExitStack() as ctx:
        pr = Prog(nc, ctx, tag)
        t = conv_tensors(pr)
        xr = pr.sb("s_rows", [P, CT, D], F32)
        bias = pr.sb("s_bias", [P, D], F32)
        st = pr.sb("s_st", [P, CT, 6], F32)
        mv = pr.sb("s_mv", [P, CT, 2], F32)
        tmp = pr.sb("s_tmp", [P, 6, CT], F32)
        rstd = pr.sb("s_rstd", [P, CT], F32)
        s = {n: pr.sem("s_" + n) for n in CONV_SEMS + ("bias_in", "rows_in", "tile_done", "sum_done", "x_out",
                                                       "var_ready", "root_done", "norm_done", "xt_ready", "xt_out",
                                                       "norm_out", "scaled")}
        block = ctx.enter_context(nc.Block())
        chunk_of = lambda ap, c: ap.rearrange("(t p) d -> p t d", p=P)[:, ds(c * CT, CT), :]

        @block.sync
        def _(sp):
            sp.dma_start(t["parts"][:, :, :, :].rearrange("p t a d -> p (t a d)"), g["parts"]).then_inc(s["parts_in"], 16)
            sp.dma_start(t["wl"][:, :, :], io[wl + "_T"].rearrange("(k p) f -> p k f", p=P)).then_inc(s["weights_in"], 16)
            sp.dma_start(t["wr"][:, :, :], io[wr + "_T"].rearrange("(k p) f -> p k f", p=P)).then_inc(s["weights_in"], 16)
            sp.dma_start(bias[:, :], io[b].rearrange("(a n) -> a n", a=1).broadcast_to([P, D])).then_inc(s["bias_in"], 16)
            with sp.Fori(0, CHUNKS) as c:
                at = sp.snap(c * CH)
                load_chunk_inv(sp, g, t, s, c, at)
                if keep_norm:
                    sp.wait_ge(s["norm_out"], 16 * c)
                sp.wait_ge(s["turned"], c)
                sp.dma_start(xr[:, :, :], chunk_of(rows_from, c)).then_inc(s["rows_in"], 16)
                sp.wait_ge(s["xt_out"], 16 * c)
                sp.dma_start(t["own"][:, :, :], g["ht"][:, :, ds(at, CH)]).then_inc(s["own_in"], 16)

        @block.gpsimd
        def _(pool):
            pool.wait_ge(s["parts_in"], 16)
            flag = pool.value_load(g["flag"][0:1, 0:1])
            feed_upper_counts(pool, g, flag, t["hib"], s["hi_in"], s["hi_used"])

        @block.vector
        def _(dve):
            ch = Chain(dve, s["chain"])
            dve.wait_ge(s["weights_in"], 32)
            for k in range(KD):
                ch.mark(nc.vector.tensor_scalar(t["wl"][:, k, :], t["wl"][:, k, :], g["unscale"][:, k:k + 1], XS,
                                                ALU.mult, ALU.mult))
                ch.mark(nc.vector.tensor_scalar(t["wr"][:, k, :], t["wr"][:, k, :], g["unscale"][:, k:k + 1], None,
                                                ALU.mult))
            ch.wait()
            nc.vector.memset(tmp[:, :, :], 0.0).then_inc(s["scaled"], 1)
            dve.wait_ge(s["scaled"], 1)
            dve.wait_ge(s["bias_in"], 16)
            start = ch.n
            per = 1 + NORM_MARKS

            def finish(c):
                ch.base, ch.n = start + c * per, 0
                dve.wait_ge(s["rows_in"], 16 * (c + 1))
                ch.done(nc.vector.tensor_tensor(xr[:, :, :], xr[:, :, :], bias[:, :].unsqueeze(1).broadcast_to([P, CT, D]),
                                                ALU.add))
                for n in range(BT):
                    dve.wait_ge(s["tile_done"], BT * c + n + 1)
                    tiles, bank = in_bank(t["bank"], n)
                    nc.vector.tensor_tensor(xr[:, tiles, :], bank, xr[:, tiles, :], ALU.add).then_inc(s["sum_done"], 1)
                dve.wait_ge(s["sum_done"], BT * (c + 1))
                norm_stats(nc, ch, xr, st, mv, s["var_ready"], s["root_done"], c + 1, rstd, tmp)
                assert ch.n == per, ch.n
                dve.wait_ge(s["x_out"], 16 * (c + 1))
                for n in range(CT):
                    nc.vector.tensor_scalar(xr[:, n, :], xr[:, n, :], mv[:, n, 0:1], rstd[:, n:n + 1],
                                            ALU.subtract, ALU.mult).then_inc(s["norm_done"], 1)

            mean_half(nc, dve, t, s, 0, 0)
            mean_half(nc, dve, t, s, 0, 1)
            with dve.Fori(1, CHUNKS) as c:
                mean_half(nc, dve, t, s, c, 0)
                finish(c - 1)
                mean_half(nc, dve, t, s, c, 1)
            finish(CHUNKS - 1)

        @block.scalar
        def _(act):
            with act.Fori(0, CHUNKS) as c:
                act.wait_ge(s["sum_done"], BT * (c + 1))
                act.dma_start(chunk_of(rows_to, c), xr[:, :, :]).then_inc(s["x_out"], 16)
                root(nc, act, tmp, s["var_ready"], s["root_done"], c + 1)
                if keep_norm:
                    act.wait_ge(s["norm_done"], CT * (c + 1))
                    act.dma_start(chunk_of(g["norm"], c), xr[:, :, :]).then_inc(s["norm_out"], 16)
                act.wait_ge(s["turned"], c + 1)
                evacuate_transposed(nc, t["bank"], t["own"]).then_inc(s["xt_ready"], 1)
                act.wait_ge(s["xt_ready"], c + 1)
                act.dma_start(g["xt"][:, :, ds(c * CH, CH)], t["own"][:, :, :]).then_inc(s["xt_out"], 16)
            act.wait_ge(s["x_out"], 16 * CHUNKS)
            act.wait_ge(s["xt_out"], 16 * CHUNKS)
            if keep_norm:
                act.wait_ge(s["norm_out"], 16 * CHUNKS)

        def dense(pe, c):
            pe.wait_ge(s["scaled"], 1)
            pe.wait_ge(s["mean_done"], 4 * (c + 1))
            pe.wait_ge(s["own_in"], 16 * (c + 1))
            pe.wait_ge(s["xt_ready"], c)
            for n in range(CT):
                at, to = slice(n * P, (n + 1) * P), t["bank"][n // 2][:, n % 2 * D:(n % 2 + 1) * D]
                for k in range(KD):
                    nc.tensor.matmul(to, t["mean"][:, k, at], t["wl"][:, k, :], start=k == 0, stop=False)
                for k in range(KD):
                    ins = nc.tensor.matmul(to, t["own"][:, k, at], t["wr"][:, k, :], start=False, stop=k == KD - 1)
                if n % 2 or n == CT - 1:
                    ins.then_inc(s["tile_done"], 1)
            pe.wait_ge(s["tile_done"], BT * (c + 1))
            pe.sem_inc(s["dense_done"], 1)

        def turn(pe, c):
            pe.wait_ge(s["norm_done"], CT * (c + 1))
            transpose_chunk(nc, pe, t["bank"], xr, g["ident"]).then_inc(s["turned"], 1)

        block.tensor(conv_tensor_engine(nc, g, adj, t, s, dense, turn))


def first_of_largest(nc, ch, sc, m, eq, rank, mv, one, down, shape):
    bc = lambda ap: ap.unsqueeze(2).broadcast_to(shape)
    ch.done(nc.vector.reduce_max(m, sc, AX.X))
    ch.done(nc.vector.tensor_tensor(eq, sc, bc(m), ALU.is_equal))
    ch.done(nc.vector.tensor_tensor(rank, eq, down.unsqueeze(1).broadcast_to(shape), ALU.mult))
    ch.done(nc.vector.reduce_max(mv, rank, AX.X))
    ch.done(nc.vector.tensor_tensor(one, rank, bc(mv), ALU.is_equal))


def route(nc, io, g):
    with ExitStack() as ctx:
        pr = Prog(nc, ctx, "r_")
        xt = pr.sb("xt", [P, 2, KD, CH], F32)
        rows = pr.sb("rows", [P, TILES, D], F32)
        wg = pr.sb("wg", [P, KD, E0], F32)
        bg = pr.sb("bg", [P, E0], F32)
        S3 = [P, TILES, E0]
        f = {n: pr.sb(n, S3, F32) for n in ("sc", "eq", "rank", "o1", "o2", "sl")}
        f2 = {n: pr.sb(n, [P, TILES], F32) for n in ("m", "mv", "pick")}
        mask = pr.sb("mask", S3, F16)
        pre = pr.sb("pre", [P, TILES + 1, E0], F32)
        ones = pr.sb("ones", [P, TILES], F32)
        down_i = pr.sb("down_i", [P, E0], I32)
        down = pr.sb("down", [P, E0], F32)
        step_i = pr.sb("step_i", [P, STMAX], I32)
        step = pr.sb("step", [P, STMAX], F32)
        tri32 = pr.sb("tri32", [P, P], F32)
        tri = pr.sb("tri", [P, P], F16)
        all1 = pr.sb("all1", [P, P], F16)
        cnt_i = pr.sb("cnt_i", [P, 3, E0], I32)
        cnt = pr.sb("cnt", [P, 5, E0], F32)
        past = pr.sb("past", [P, STMAX, E0], F32)
        tile_f = pr.sb("tile_f", [P, 2, STMAX], F32)
        ps_sc = pr.ps("ps_sc", S3)
        ps_rank = pr.ps("ps_rank", S3)
        ps_tot = pr.ps("ps_tot", S3)
        s = {n: pr.sem(n) for n in ("xt_in0", "xt_in1", "w_in", "rows_in", "iotas", "scored", "chain", "mask_ready",
                                    "ranked", "idx_ready", "scattered", "const")}
        block = ctx.enter_context(nc.Block())

        @block.sync
        def _(sp):
            sp.dma_start(wg[:, :, :], io["L0_ffn_Wg"].rearrange("(k p) e -> p k e", p=P)).then_inc(s["w_in"], 16)
            sp.dma_start(bg[:, :], io["L0_ffn_bg"].rearrange("(a e) -> a e", a=1).broadcast_to([P, E0])).then_inc(s["w_in"], 16)
            for c in range(CHUNKS):
                if c >= 2:
                    sp.wait_ge(s["scored"], c - 1)
                sp.dma_start(xt[:, c % 2, :, :], g["xt"][:, :, c * CH:(c + 1) * CH]).then_inc(s[f"xt_in{c % 2}"], 16)
            sp.dma_start(rows[:, :, :], g["norm"].rearrange("(t p) d -> p t d", p=P)).then_inc(s["rows_in"], 16)

        @block.tensor
        def _(pe):
            pe.wait_ge(s["w_in"], 32)
            for c in range(CHUNKS):
                pe.wait_ge(s[f"xt_in{c % 2}"], 16 * (c // 2 + 1))
                for t in range(CT):
                    for k in range(KD):
                        ins = nc.tensor.matmul(ps_sc[:, c * CT + t, :], xt[:, c % 2, k, t * P:(t + 1) * P], wg[:, k, :],
                                               start=k == 0, stop=k == KD - 1)
                ins.then_inc(s["scored"], 1)
            pe.wait_ge(s["mask_ready"], 1)
            nc.tensor.matmul(ps_rank[:, :, :], tri[:, :], mask[:, :, :], start=True, stop=True)
            nc.tensor.matmul(ps_tot[:, :, :], all1[:, :], mask[:, :, :], start=True, stop=True).then_inc(s["ranked"], 1)

        @block.vector
        def _(dve):
            ch = Chain(dve, s["chain"])
            ch.mark(nc.vector.memset(all1[:, :], 1.0))
            ch.mark(nc.vector.memset(ones[:, :], 1.0))
            ch.mark(nc.vector.memset(pre[:, 0, :], 0.0))
            dve.wait_ge(s["iotas"], 3)
            ch.mark(nc.vector.tensor_copy(down[:, :], down_i[:, :]))
            ch.mark(nc.vector.tensor_copy(step[:, :], step_i[:, :]))
            ch.mark(nc.vector.tensor_copy(tri[:, :], tri32[:, :]))
            dve.wait_ge(s["scored"], CHUNKS)
            ch.done(nc.vector.tensor_tensor(f["sc"][:, :, :], ps_sc[:, :, :], bg[:, :].unsqueeze(1).broadcast_to(S3), ALU.add))
            a = {n: v[:, :, :] for n, v in f.items()}
            first_of_largest(nc, ch, a["sc"], f2["m"][:, :], a["eq"], a["rank"], f2["mv"][:, :], a["o1"], down[:, :], S3)
            ch.done(nc.vector.scalar_tensor_tensor(a["sc"], a["o1"], -3e38, a["sc"], ALU.mult, ALU.add))
            first_of_largest(nc, ch, a["sc"], f2["m"][:, :], a["eq"], a["rank"], f2["mv"][:, :], a["o2"], down[:, :], S3)
            nc.vector.tensor_tensor(mask[:, :, :], a["o1"], a["o2"], ALU.add).then_inc(s["mask_ready"], 1)
            dve.wait_ge(s["ranked"], 1)
            ch.mark(nc.vector.tensor_copy(a["sc"], ps_tot[:, :, :]))
            ch.done(nc.vector.tensor_copy(a["sl"], ps_rank[:, :, :]))
            for e in range(E0):
                ch.mark(nc.vector.tensor_tensor_scan(pre[:, 1:TILES + 1, e], ones[:, :], f["sc"][:, :, e], 0.0,
                                                     ALU.mult, ALU.add))
            ch.wait()
            ch.done(nc.vector.tensor_scalar(cnt[:, 0, :], pre[:, TILES, :], float(ST - 1), None, ALU.add))
            ch.done(nc.vector.tensor_copy(cnt_i[:, 0, :], cnt[:, 0, :]))
            ch.done(nc.vector.tensor_scalar(cnt_i[:, 1, :], cnt_i[:, 0, :], ST.bit_length() - 1, None, ALU.logical_shift_right))
            ch.done(nc.vector.tensor_copy(cnt[:, 1, :], cnt_i[:, 1, :]))
            ch.done(nc.vector.tensor_tensor_scan(cnt[:, 2, :], ones[:, 0:E0], cnt[:, 1, :], 0.0, ALU.mult, ALU.add))
            ch.done(nc.vector.tensor_tensor(cnt[:, 3, :], cnt[:, 2, :], cnt[:, 1, :], ALU.subtract))
            ch.mark(nc.vector.tensor_scalar(cnt[:, 4, :], cnt[:, 3, :], float(ST), None, ALU.mult))
            ch.done(nc.vector.tensor_tensor(a["sl"], a["sl"], pre[:, 0:TILES, :], ALU.add))
            ch.done(nc.vector.tensor_tensor(a["sl"], a["sl"], cnt[:, 4, :].unsqueeze(1).broadcast_to(S3), ALU.add))
            for n, one in ((0, "o1"), (1, "o2")):
                ch.done(nc.vector.tensor_tensor(a["eq"], a[one], a["sl"], ALU.mult))
                ch.done(nc.vector.reduce_sum(f2["pick"][:, :], a["eq"], AX.X))
                ins = nc.vector.tensor_copy(g["slot"][:, n, :], f2["pick"][:, :])
                ch.done(ins)
            nc.vector.memset(f2["m"][:, :], 0.0).then_inc(s["idx_ready"], 1)
            ch.done(nc.vector.tensor_tensor(past[:, :, :], cnt[:, 2, :].unsqueeze(1).broadcast_to([P, STMAX, E0]),
                                            step[:, :].unsqueeze(2).broadcast_to([P, STMAX, E0]), ALU.is_le))
            ch.done(nc.vector.reduce_sum(tile_f[:, 0, :], past[:, :, :], AX.X))
            ch.done(nc.vector.tensor_scalar(tile_f[:, 1, :], tile_f[:, 0, :], float(E0 - 1), None, ALU.min))
            ch.mark(nc.vector.tensor_copy(g["expert"][:, :], tile_f[:, 1, :]))
            ch.done(nc.vector.tensor_scalar(cnt[:, 0, 0:1], cnt[:, 2, E0 - 1:E0], 1.0, None, ALU.add))
            ch.done(nc.vector.tensor_copy(cnt_i[:, 2, 0:1], cnt[:, 0, 0:1]))
            ch.done(nc.vector.tensor_scalar(g["pairs"][:, :], cnt_i[:, 2, 0:1], 1, None, ALU.logical_shift_right))

        @block.gpsimd
        def _(pool):
            nc.gpsimd.iota(down_i[:, :], pattern=[[-1, E0]], base=E0, channel_multiplier=0).then_inc(s["iotas"], 1)
            nc.gpsimd.iota(step_i[:, :], pattern=[[1, STMAX]], base=0, channel_multiplier=0).then_inc(s["iotas"], 1)
            nc.gpsimd.memset(tri32[:, :], 1.0).then_inc(s["const"], 1)
            pool.wait_ge(s["const"], 1)
            nc.gpsimd.affine_select(out=tri32[:, :], in_=tri32[:, :], compare_op=ALU.is_gt, fill=0.0, base=0,
                                    pattern=[[1, P]], channel_multiplier=-1).then_inc(s["iotas"], 1)
            pool.wait_ge(s["rows_in"], 16)
            pool.wait_ge(s["idx_ready"], 1)
            for n in range(2):
                for t in range(TILES):
                    pool.indirect_dma_start(out=g["slots_in"], in_=rows[:, t, :], in_offset=None,
                                            out_offset=bass.IndirectOffsetOnAxis(ap=g["slot"][:, n, t:t + 1], axis=0)
                                            ).then_inc(s["scattered"], 16)
            pool.wait_ge(s["scattered"], 16 * 2 * TILES)


def experts(nc, io, g):
    with ExitStack() as ctx:
        pr = Prog(nc, ctx, "e_")
        NT = ST // P
        w1 = pr.sb("w1", [P, 2, KD, H0], F32)
        w2 = pr.sb("w2", [P, 2, HB, D], F32)
        b1 = pr.sb("b1", [P, 2, HB], F32)
        b2 = pr.sb("b2", [P, 2, D], F32)
        xr = pr.sb("xr", [P, 2, NT, D], F32)
        xt = pr.sb("xt", [P, KD, ST], F32)
        h = pr.sb("h", [P, HB, ST], F32)
        y = pr.sb("y", [P, 2, NT, D], F32)
        px = [pr.ps(f"px{k}", [P, ST]) for k in range(KD)]
        ph = [pr.ps(f"ph{n}", [P, 2, ST]) for n in range(HB // 2)]
        py = pr.ps("py", [P, NT, D])
        s = {n: pr.sem(n) for n in ("in0", "in1", "turned", "xt0", "xt1", "h_mm", "h_done", "y_mm", "y_done",
                                    "y_out0", "y_out1")}
        LOADS = 5 * 16
        block = ctx.enter_context(nc.Block())
        pairs_on = lambda eng: eng.value_load(g["pairs"][0:1, 0:1], min_val=1, max_val=STMAX // 2)

        @block.sync
        def _(sp):
            pairs = pairs_on(sp)
            with sp.Fori(0, pairs) as pair:
                for u in range(2):
                    j = pair * 2 + u
                    e = sp.value_load(g["expert"][0:1, ds(j, 1)], min_val=0, max_val=E0 - 1)
                    sp.wait_ge(s["y_mm"], j)
                    sp.wait_ge(s["y_done"], j)
                    got = s[f"in{u}"]
                    sp.dma_start(xr[:, u, :, :], g["slots_in"].rearrange("(t p) d -> p t d", p=P)[:, ds(j * NT, NT), :]).then_inc(got, 16)
                    sp.dma_start(w1[:, u, :, :], io["L0_ffn_W1"].rearrange("e (k p) h -> p (e k) h", p=P)[:, ds(e * KD, KD), :]).then_inc(got, 16)
                    sp.dma_start(w2[:, u, :, :], io["L0_ffn_W2"].rearrange("e (k p) d -> p (e k) d", p=P)[:, ds(e * HB, HB), :]).then_inc(got, 16)
                    sp.dma_start(b1[:, u, :], io["L0_ffn_b1"].rearrange("e (k p) -> p (e k)", p=P)[:, ds(e * HB, HB)],
                                 allow_slow_non_contiguous=True).then_inc(got, 16)
                    sp.dma_start(b2[:, u, :], io["L0_ffn_b2"][ds(e, 1), :].broadcast_to([P, D])).then_inc(got, 16)

        @block.tensor
        def _(pe):
            pairs = pairs_on(pe)
            pe.sem_inc(s["y_mm"], 1)
            with pe.Fori(0, pairs) as pair:
                for u in range(2):
                    j = pair * 2 + u
                    pe.wait_ge(s[f"in{u}"], LOADS * (pair + 1))
                    for k in range(KD):
                        for t in range(NT):
                            ins = nc.tensor.transpose(px[k][:, t * P:(t + 1) * P], xr[:, u, t, k * P:(k + 1) * P], g["ident"][:, :])
                        ins.then_inc(s["turned"], 1)
                    pe.wait_ge(s["xt0"], j + 1)
                    pe.wait_ge(s["xt1"], j + 1)
                    for n in range(HB):
                        for k in range(KD):
                            ins = nc.tensor.matmul(ph[n // 2][:, n % 2, :], w1[:, u, k, n * P:(n + 1) * P], xt[:, k, :],
                                                   start=k == 0, stop=k == KD - 1)
                        if n % 2:
                            ins.then_inc(s["h_mm"], 1)
                    pe.wait_ge(s["h_done"], HB * (j + 1))
                    pe.wait_ge(s["y_done"], j + 1)
                    for t in range(NT):
                        for n in range(HB):
                            ins = nc.tensor.matmul(py[:, t, :], h[:, n, t * P:(t + 1) * P], w2[:, u, n, :],
                                                   start=n == 0, stop=n == HB - 1)
                    ins.then_inc(s["y_mm"], 1)

        @block.scalar
        def _(act):
            pairs = pairs_on(act)
            with act.Fori(0, pairs) as pair:
                for u in range(2):
                    j = pair * 2 + u
                    act.wait_ge(s["turned"], 2 * j + 2)
                    nc.scalar.activation(xt[:, 1, :], px[1][:, :], ACT.Copy).then_inc(s["xt1"], 1)
                    for n in range(HB):
                        act.wait_ge(s["h_mm"], 2 * j + n // 2 + 1)
                        nc.scalar.activation(h[:, n, :], ph[n // 2][:, n % 2, :], ACT.Gelu, bias=b1[:, u, n:n + 1]
                                             ).then_inc(s["h_done"], 1)

        @block.vector
        def _(dve):
            pairs = pairs_on(dve)
            dve.sem_inc(s["y_done"], 1)
            with dve.Fori(0, pairs) as pair:
                for u in range(2):
                    j = pair * 2 + u
                    dve.wait_ge(s["turned"], 2 * j + 1)
                    nc.vector.tensor_copy(xt[:, 0, :], px[0][:, :]).then_inc(s["xt0"], 1)
                    dve.wait_ge(s[f"y_out{u}"], 16 * pair)
                    dve.wait_ge(s["y_mm"], j + 2)
                    nc.vector.tensor_tensor(y[:, u, :, :], py[:, :, :], b2[:, u, :].unsqueeze(1).broadcast_to([P, NT, D]),
                                            ALU.add).then_inc(s["y_done"], 1)

        @block.gpsimd
        def _(pool):
            pairs = pairs_on(pool)
            with pool.Fori(0, pairs) as pair:
                for u in range(2):
                    j = pair * 2 + u
                    pool.wait_ge(s["y_done"], j + 2)
                    pool.dma_start(g["slots_out"].rearrange("(t p) d -> p t d", p=P)[:, ds(j * NT, NT), :],
                                   y[:, u, :, :]).then_inc(s[f"y_out{u}"], 16)
            for u in range(2):
                pool.wait_ge(s[f"y_out{u}"], 16 * pairs)


def last_experts(nc, io, g, rows_from, out):
    with ExitStack() as ctx:
        pr = Prog(nc, ctx, "m_")
        F = "L1_ffn_"
        sw1 = pr.sb("sw1", [P, KD, SH1], F32)
        sw2 = pr.sb("sw2", [P, SH1 // P, SH2], F32)
        sw3 = pr.sb("sw3", [P, D], F32)
        ew1 = pr.sb("ew1", [P, KD, E1, EH1], F32)
        ew2 = pr.sb("ew2", [P, E1, EH2], F32)
        ew3 = pr.sb("ew3", [EH2 + 1, E1, D], F32)
        gw = pr.sb("gw", [P, KD, E1], F32)
        gb = pr.sb("gb", [P, E1], F32)
        sb1 = pr.sb("sb1", [P, SH1 // P], F32)
        sb2 = pr.sb("sb2", [P, 1], F32)
        sb3 = pr.sb("sb3", [P, D], F32)
        eb1 = pr.sb("eb1", [P, E1], F32)
        eb2 = pr.sb("eb2", [EH2, E1], F32)
        xt = pr.sb("xt", [P, KD, CH], F32)
        h1 = pr.sb("h1", [P, SH1 // P, CH], F32)
        h2 = pr.sb("h2", [P, CH], F32)
        eh1 = pr.sb("eh1", [P, 2, CH], F32)
        eh2 = pr.sb("eh2", [EH2 + 1, 2, CH], F32)
        acc = pr.sb("acc", [P, CT, D], F32)
        down_i = pr.sb("down_i", [P, E1], I32)
        down = pr.sb("down", [P, E1], F32)
        S3 = [P, CT, E1]
        f = {n: pr.sb(n, S3, F32) for n in ("sc", "d", "ex", "gate", "eq", "rank", "o1", "o2", "w1", "w2", "wt")}
        f2 = {n: pr.sb(n, [P, CT], F32) for n in ("mx", "sm", "rs", "m1", "m2", "mv", "dd", "t", "t1", "r2", "v2")}
        bank = [pr.ps(f"bank{i}", [P, 512]) for i in range(7)]
        pg = pr.ps("pg", S3)
        s = {n: pr.sem(n) for n in ("w_in", "xt_in", "acc_in", "down_ready", "gate_mm", "chain", "exp_in1", "exp_in2",
                                    "exp1", "exp2", "mm", "act_took", "dve_took", "ready", "out_done", "gate_taken")}
        block = ctx.enter_context(nc.Block())
        NB = len(bank)
        LOADS = 15
        ORDER = ["S1", "E1.0", "S2", "E2.0", "E1.1", "S3", "E3.0", "E2.1", "E1.2", "E3.1", "E2.2", "E1.3", "E3.2",
                 "E2.3", "E3.3"]
        GROUPS = {"S1": 4, "S2": 2, "S3": BT, "E1": 2, "E2": 2, "E3": BT}
        first, n = {}, 0
        for name in ORDER:
            first[name] = n
            n += GROUPS[name[:2]]
        TOTAL = n
        by_dve = [x[:2] in ("S3", "E3") for x in ORDER for _ in range(GROUPS[x[:2]])]
        taken = [sum(1 for b in by_dve[:i + 1] if b == by_dve[i]) for i in range(TOTAL)]
        ACT_N, DVE_N = by_dve.count(False), by_dve.count(True)

        def group_taken(eng, c, i):
            if by_dve[i]:
                eng.wait_ge(s["dve_took"], c * DVE_N + taken[i])
            else:
                eng.wait_ge(s["act_took"], c * ACT_N + taken[i])

        @block.sync
        def _(sp):
            loads = [
                (sw1[:, :, :], io[F + "sW1"].rearrange("(k p) n -> p k n", p=P)),
                (sw2[:, :, :], io[F + "sW2"].rearrange("(k p) n -> p k n", p=P)),
                (sw3[:, :], io[F + "sW3"]),
                (gw[:, :, :], io[F + "gW"].rearrange("(k p) n -> p k n", p=P)),
                (gb[:, :], io[F + "gb"].rearrange("(a n) -> a n", a=1).broadcast_to([P, E1])),
                (sb1[:, :], io[F + "sb1"].rearrange("(k p) -> p k", p=P)),
                (sb2[:, :], io[F + "sb2"].rearrange("(p a) -> p a", a=1)),
                (sb3[:, :], io[F + "sb3"].rearrange("(a n) -> a n", a=1).broadcast_to([P, D])),
                (eb1[:, :], io[F + "eb1"].rearrange("e p -> p e")),
                (eb2[:, :], io[F + "eb2"].rearrange("e p -> p e")),
                (ew3[EH2:EH2 + 1, :, :], io[F + "eb3"].rearrange("(a e) n -> a e n", a=1)),
                (ew2[:, :, :], io[F + "eW2"].rearrange("e p n -> p e n")),
                (ew3[0:EH2, :, :], io[F + "eW3"].rearrange("e p n -> p e n")),
            ] + [(ew1[:, k, :, :], io[F + "eW1"][:, k * P:(k + 1) * P, :].rearrange("e p n -> p e n")) for k in range(KD)]
            assert len(loads) == LOADS
            for to, fr in loads:
                sp.dma_start(to, fr, allow_slow_non_contiguous=True).then_inc(s["w_in"], 16)
            with sp.Fori(0, CHUNKS) as c:
                at, row = sp.snap(c * CH), sp.snap(c * CT)
                sp.wait_ge(s["act_took"], ACT_N * c)
                sp.dma_start(xt[:, :, :], g["xt"][:, :, ds(at, CH)]).then_inc(s["xt_in"], 16)
                sp.wait_ge(s["out_done"], 16 * c)
                sp.dma_start(acc[:, :, :], rows_from.rearrange("(t p) d -> p t d", p=P)[:, ds(row, CT), :]).then_inc(s["acc_in"], 16)

        @block.gpsimd
        def _(pool):
            nc.gpsimd.iota(down_i[:, :], pattern=[[-1, E1]], base=E1, channel_multiplier=0).then_inc(s["down_ready"], 1)
            with pool.Fori(0, CHUNKS - 1) as c:
                pool.wait_ge(s["dve_took"], DVE_N * (c + 1))
                pool.dma_start(out[ds(c * CH, CH), :].rearrange("(t p) d -> p t d", p=P), acc[:, :, :]).then_inc(s["out_done"], 16)
            pool.wait_ge(s["dve_took"], DVE_N * CHUNKS)
            at = (CHUNKS - 1) * CH
            full = (NODES - at) // P
            pool.dma_start(out[at:at + full * P, :].rearrange("(t p) d -> p t d", p=P), acc[:, 0:full, :]).then_inc(s["out_done"], 16)
            rest = NODES - at - full * P
            pool.dma_start(out[NODES - rest:NODES, :], acc[0:rest, full, :]).then_inc(s["out_done"], 16)
            pool.wait_ge(s["out_done"], 16 * (CHUNKS + 1))

        @block.tensor
        def _(pe):
            pe.wait_ge(s["w_in"], 16 * LOADS)
            pe.wait_ge(s["ready"], 1)
            with pe.Fori(0, CHUNKS) as c:
                pe.wait_ge(s["xt_in"], 16 * (c + 1))
                pe.wait_ge(s["gate_taken"], c)
                for t in range(CT):
                    for k in range(KD):
                        ins = nc.tensor.matmul(pg[:, t, :], xt[:, k, t * P:(t + 1) * P], gw[:, k, :], start=k == 0, stop=k == KD - 1)
                ins.then_inc(s["gate_mm"], 1)
                pe.wait_ge(s["act_took"], ACT_N * c)
                pe.wait_ge(s["dve_took"], DVE_N * c)
                for name in ORDER:
                    kind, e = name[:2], int(name[3:] or 0)
                    need = {"S2": "S1", "S3": "S2", "E2": f"E1.{e}", "E3": f"E2.{e}"}.get(kind)
                    if need:
                        group_taken(pe, c, first[need] + GROUPS[need[:2]] - 1)
                    for n in range(GROUPS[kind]):
                        i = first[name] + n
                        if i >= NB:
                            group_taken(pe, c, i - NB)
                        b = bank[i % NB]
                        half = slice((n if kind != "S1" else n // 2) * SUB, ((n if kind != "S1" else n // 2) + 1) * SUB)
                        if kind == "S1":
                            for k in range(KD):
                                ins = nc.tensor.matmul(b[:, 0:SUB], sw1[:, k, n % 2 * P:(n % 2 + 1) * P], xt[:, k, half],
                                                       start=k == 0, stop=k == KD - 1)
                        elif kind == "E1":
                            for k in range(KD):
                                ins = nc.tensor.matmul(b[:, 0:SUB], ew1[:, k, e, :], xt[:, k, half], start=k == 0, stop=k == KD - 1)
                        elif kind == "S2":
                            for k in range(SH1 // P):
                                ins = nc.tensor.matmul(b[:, 0:SUB], sw2[:, k, :], h1[:, k, half], start=k == 0, stop=k == SH1 // P - 1)
                        elif kind == "E2":
                            ins = nc.tensor.matmul(b[0:EH2, 0:SUB], ew2[:, e, :], eh1[:, e % 2, half], start=True, stop=True)
                        else:
                            for t in range(2 * n, min(2 * n + 2, CT)):
                                to = b[:, t % 2 * D:(t % 2 + 1) * D]
                                if kind == "S3":
                                    ins = nc.tensor.matmul(to, h2[:, t * P:(t + 1) * P], sw3[:, :], start=True, stop=True)
                                else:
                                    ins = nc.tensor.matmul(to, eh2[:, e % 2, t * P:(t + 1) * P], ew3[:, e, :], start=True, stop=True)
                        ins.then_inc(s["mm"], 1)

        @block.scalar
        def _(act):
            act.wait_ge(s["w_in"], 16 * LOADS)
            with act.Fori(0, CHUNKS) as c:
                for name in ORDER:
                    kind, e = name[:2], int(name[3:] or 0)
                    if name == "E1.0":
                        act.wait_ge(s["exp_in1"], c + 1)
                        nc.scalar.activation(f["ex"][:, :, :], f["d"][:, :, :], ACT.Exp).then_inc(s["exp1"], 1)
                    if name == "E2.0":
                        act.wait_ge(s["exp_in2"], c + 1)
                        nc.scalar.activation(f2["t"][:, :], f2["dd"][:, :], ACT.Exp).then_inc(s["exp2"], 1)
                    if kind in ("S3", "E3"):
                        continue
                    for n in range(GROUPS[kind]):
                        i = first[name] + n
                        b = bank[i % NB]
                        half = slice((n if kind != "S1" else n // 2) * SUB, ((n if kind != "S1" else n // 2) + 1) * SUB)
                        act.wait_ge(s["mm"], c * TOTAL + i + 1)
                        if kind == "S1":
                            to, fr, bias = h1[:, n % 2, half], b[:, 0:SUB], sb1[:, n % 2:n % 2 + 1]
                        elif kind == "E1":
                            to, fr, bias = eh1[:, e % 2, half], b[:, 0:SUB], eb1[:, e:e + 1]
                        elif kind == "S2":
                            to, fr, bias = h2[:, half], b[:, 0:SUB], sb2[:, 0:1]
                        else:
                            to, fr, bias = eh2[0:EH2, e % 2, half], b[0:EH2, 0:SUB], eb2[:, e:e + 1]
                        nc.scalar.activation(to, fr, ACT.Relu, bias=bias).then_inc(s["act_took"], 1)

        @block.vector
        def _(dve):
            ch = Chain(dve, s["chain"])
            dve.wait_ge(s["down_ready"], 1)
            ch.mark(nc.vector.tensor_copy(down[:, :], down_i[:, :]))
            ch.done(nc.vector.memset(eh2[EH2:EH2 + 1, :, :], 1.0))
            nc.vector.memset(f2["sm"][:, :], 1.0).then_inc(s["ready"], 1)
            dve.wait_ge(s["ready"], 1)
            dve.wait_ge(s["w_in"], 16 * LOADS)
            a = {n: v[:, :, :] for n, v in f.items()}
            a2 = {n: v[:, :] for n, v in f2.items()}
            bc = lambda ap: ap.unsqueeze(2).broadcast_to(S3)
            with ch.loop(0, CHUNKS, 23) as c:
                dve.wait_ge(s["gate_mm"], c + 1)
                ch.done(nc.vector.tensor_tensor(a["sc"], pg[:, :, :], gb[:, :].unsqueeze(1).broadcast_to(S3), ALU.add))
                nc.vector.memset(a2["sm"], 0.0).then_inc(s["gate_taken"], 1)
                ch.done(nc.vector.reduce_max(a2["mx"], a["sc"], AX.X))
                nc.vector.tensor_tensor(a["d"], a["sc"], bc(a2["mx"]), ALU.subtract).then_inc(s["exp_in1"], 1)
                dve.wait_ge(s["exp1"], c + 1)
                dve.wait_ge(s["gate_taken"], c + 1)
                ch.done(nc.vector.reduce_sum(a2["sm"], a["ex"], AX.X))
                ch.done(nc.vector.reciprocal(a2["rs"], a2["sm"]))
                ch.done(nc.vector.tensor_tensor(a["gate"], a["ex"], bc(a2["rs"]), ALU.mult))
                first_of_largest(nc, ch, a["gate"], a2["m1"], a["eq"], a["rank"], a2["mv"], a["o1"], down[:, :], S3)
                ch.done(nc.vector.scalar_tensor_tensor(a["gate"], a["o1"], -2.0, a["gate"], ALU.mult, ALU.add))
                first_of_largest(nc, ch, a["gate"], a2["m2"], a["eq"], a["rank"], a2["mv"], a["o2"], down[:, :], S3)
                nc.vector.tensor_tensor(a2["dd"], a2["m2"], a2["m1"], ALU.subtract).then_inc(s["exp_in2"], 1)
                dve.wait_ge(s["exp2"], c + 1)
                ch.done(nc.vector.tensor_scalar(a2["t1"], a2["t"], 1.0, None, ALU.add))
                ch.done(nc.vector.reciprocal(a2["r2"], a2["t1"]))
                ch.mark(nc.vector.tensor_tensor(a2["v2"], a2["t"], a2["r2"], ALU.mult))
                ch.done(nc.vector.tensor_tensor(a["w1"], a["o1"], bc(a2["r2"]), ALU.mult))
                ch.done(nc.vector.tensor_tensor(a["w2"], a["o2"], bc(a2["v2"]), ALU.mult))
                ch.done(nc.vector.tensor_tensor(a["wt"], a["w1"], a["w2"], ALU.add))
                dve.wait_ge(s["acc_in"], 16 * (c + 1))
                ch.done(nc.vector.tensor_tensor(acc[:, :, :], acc[:, :, :], sb3[:, :].unsqueeze(1).broadcast_to([P, CT, D]), ALU.add))
                for name in ORDER:
                    kind, e = name[:2], int(name[3:] or 0)
                    if kind not in ("S3", "E3"):
                        continue
                    for n in range(GROUPS[kind]):
                        i = first[name] + n
                        dve.wait_ge(s["mm"], c * TOTAL + i + 1)
                        tiles, b = in_bank([bank[i % NB]] * BT, n)
                        if kind == "S3":
                            ins = nc.vector.tensor_tensor(acc[:, tiles, :], b, acc[:, tiles, :], ALU.add)
                        else:
                            dve.wait_ge(s["dve_took"], c * DVE_N + taken[i] - BT)
                            for t in range(tiles.start, tiles.stop):
                                ins = nc.vector.scalar_tensor_tensor(acc[:, t, :], b[:, t - tiles.start, :], f["wt"][:, t, e:e + 1],
                                                                     acc[:, t, :], ALU.mult, ALU.add)
                        ins.then_inc(s["dve_took"], 1)


def program(nc, io, out):
    dram = lambda name, shape, dt: nc.dram_tensor(name, shape, dt).ap()
    g = {
        "parts": dram("parts", (P, TILES * 2 * D), F16),
        "xt": dram("xt", (P, KD, ROWS), F32),
        "ht": dram("ht", (P, KD, ROWS), F32),
        "slots_in": dram("slots_in", (SLOTS, D), F32),
        "slots_out": dram("slots_out", (SLOTS, D), F32),
        "norm": dram("norm", (ROWS, D), F32),
        "x1": dram("x1", (ROWS, D), F32),
        "x2": dram("x2", (ROWS, D), F32),
        "x3": dram("x3", (ROWS, D), F32),
        "upper": dram("upper", (ROWS, ROWS), F16),
        "inv": dram("inv", (1, ROWS), F32),
        "keys": dram("keys", (2, P, WINS * VIS, 2), F16),
    }
    with ExitStack() as ctx:
        pr = Prog(nc, ctx)
        g["ident"] = pr.sb("ident", [P, P], F32)
        g["flag"] = pr.sb("flag", [1, 1], I32)
        g["scale"] = pr.sb("scale", [P, KD], F32)
        g["unscale"] = pr.sb("unscale", [P, KD], F32)
        g["slot"] = pr.sb("slot", [P, 2, TILES], I32)
        g["expert"] = pr.sb("expert", [P, STMAX], I32)
        g["pairs"] = pr.sb("pairs", [P, 1], I32)
        normalise(nc, g, "n1_", io["x"], setup=True)
        window_keys(nc, io, g)
        adj = pr.sb("adj", [P, TILES, ROWS], F16)
        build_counts(nc, io, g, adj)
        first_conv(nc, io, g, adj, "l0a_", ("L0_gnn_W1l", "L0_gnn_b1", "L0_gnn_W1r"))
        second_conv(nc, io, g, adj, "l0b_", ("L0_gnn_W2l", "L0_gnn_b2", "L0_gnn_W2r"), io["x"], g["x1"], True)
        route(nc, io, g)
        experts(nc, io, g)
        normalise(nc, g, "n2_", g["x1"], rows_to=g["x2"], idx=g["slot"])
        first_conv(nc, io, g, adj, "l1a_", ("L1_gnn_w1_l", "L1_gnn_b1", "L1_gnn_w1_r"))
        second_conv(nc, io, g, adj, "l1b_", ("L1_gnn_w2_l", "L1_gnn_b2", "L1_gnn_w2_r"), g["x2"], g["x3"], False)
        last_experts(nc, io, g, g["x3"], out)


GNN_WEIGHTS = ("L0_gnn_W1l", "L0_gnn_W1r", "L0_gnn_W2l", "L0_gnn_W2r",
               "L1_gnn_w1_l", "L1_gnn_w1_r", "L1_gnn_w2_l", "L1_gnn_w2_r")


def layout(inputs):
    import numpy as np

    def padded(a, rows, value):
        return np.concatenate([a, np.full((rows - a.shape[0],) + a.shape[1:], value, a.dtype)])

    arrays = {n: np.ascontiguousarray(a) for n, a in inputs.items()}
    arrays["x"] = padded(arrays["x"], ROWS, 0)
    arrays["src"] = padded(arrays["src"], EPAD, 0)
    arrays["dst"] = padded(arrays["dst"], EPAD, FAR)
    for n in GNN_WEIGHTS:
        arrays[n + "_T"] = np.ascontiguousarray(arrays[n].T)
    return arrays


def kernel(**inputs):
    import concourse.bacc as bacc
    from concourse.bass_utils import run_bass_kernel_spmd

    nc = bacc.Bacc("TRN2", target_bir_lowering=False, num_devices=1)
    arrays = layout(inputs)
    io = {n: nc.dram_tensor("in_" + n, a.shape, mybir.dt.from_np(a.dtype), kind="ExternalInput").ap()
          for n, a in arrays.items()}
    out = nc.dram_tensor("out", (NODES, D), F32, kind="ExternalOutput").ap()
    program(nc, io, out)
    r = run_bass_kernel_spmd(nc, [{"in_" + n: a for n, a in arrays.items()}], core_ids=[0])
    return r.results[0]["out"]
```

```python
from contextlib import ExitStack, contextmanager

import concourse.bass as bass
from concourse import mybir

F32, F16, I32 = mybir.dt.float32, mybir.dt.float16, mybir.dt.int32
ALU = mybir.AluOpType
ACT = mybir.ActivationFunctionType
AX = mybir.AxisListType
ds = bass.ds

P = 128
D = 256
KD = D // P
NODES = 3125
TILES = -(-NODES // P)
ROWS = TILES * P
CT = 5
CHUNKS = TILES // CT
CH = CT * P
SUB = CH // 2
EDGES = 103125
ETILES = -(-EDGES // P)
W = 6
VIS = 3
WINS = 522
GW = 3
GROUPS = WINS // GW
UNROLL = 6
SLOT = 3
BODIES = GROUPS // UNROLL
BW = UNROLL * GW * W
WG = -(-WINS // P)
NW = TILES * W
EG = 7
EPAD = (EG * P + 1) * P
SG = 13
SSTEPS = ETILES // SG
FAR = 4096
SPLIT = 2048.0
XS = 1024.0
EPS = 1e-5
E0, H0 = 8, 512
HB = H0 // P
ST = 256
STMAX = (2 * ROWS + E0 * (ST - 1)) // ST
SLOTS = STMAX * ST
E1, SH1, SH2, EH1, EH2 = 4, 256, 128, 128, 64

assert W * WINS >= NODES and SSTEPS * SG == ETILES and CHUNKS * CT == TILES
assert BODIES * UNROLL * GW == WINS and NW % 2 == 0 and STMAX % 2 == 0


class Chain:

    def __init__(self, eng, sem):
        self.eng, self.sem, self.base, self.n = eng, sem, 0, 0

    def mark(self, ins):
        ins.then_inc(self.sem, 1)
        self.n += 1
        return self.base + self.n

    def wait(self):
        self.eng.wait_ge(self.sem, self.base + self.n)

    def done(self, ins):
        self.mark(ins)
        self.wait()

    @contextmanager
    def loop(self, start, end, per):
        before = self.n
        with self.eng.Fori(start, end) as i:
            self.base, self.n = before + (i - start) * per, 0
            yield i
            assert self.n == per, (self.n, per)
        self.base, self.n = 0, before + (end - start) * per


class Prog:

    def __init__(self, nc, ctx, tag=""):
        self.nc, self.ctx, self.tag, self.sems = nc, ctx, tag, []
        ctx.callback(self.clear)

    def clear(self):
        if self.sems:
            self.nc.clear_and_free_semaphores(self.sems)
            self.nc.all_engine_barrier(sem_only=True)

    def sb(self, name, shape, dt):
        return self.ctx.enter_context(self.nc.sbuf_tensor(self.tag + name, shape, dt))

    def ps(self, name, shape, dt=F32):
        return self.ctx.enter_context(self.nc.psum_tensor(self.tag + name, shape, dt))

    def sem(self, name):
        self.sems.append(self.nc.alloc_semaphore(self.tag + name))
        return self.sems[-1]


NORM_MARKS = 2 * CT + 5


def norm_stats(nc, ch, rows, st, mv, var_ready, rstd_from, n, rstd, tmp):
    for t in range(CT):
        ch.mark(nc.vector.bn_stats(st[:, t, :], rows[:, t, :]))
    ch.wait()
    nc.vector.memset(tmp[:, 3, :], 0.0)
    for t in range(CT):
        ch.mark(nc.vector.bn_aggr(mv[:, t, :], st[:, t, :]))
    ch.wait()
    ins = nc.vector.tensor_scalar(tmp[:, 0, :], mv[:, :, 1], EPS, None, ALU.add)
    ins.then_inc(var_ready, 1)
    ch.eng.wait_ge(rstd_from, n)
    ch.done(nc.vector.reciprocal(tmp[:, 1, :], tmp[:, 2, :]))
    ch.done(nc.vector.tensor_tensor(tmp[:, 3, :], tmp[:, 1, :], tmp[:, 1, :], ALU.mult))
    ch.done(nc.vector.tensor_tensor(tmp[:, 4, :], tmp[:, 3, :], tmp[:, 0, :], ALU.mult))
    ch.done(nc.vector.tensor_scalar(tmp[:, 5, :], tmp[:, 4, :], -0.5, 1.5, ALU.mult, ALU.add))
    ch.done(nc.vector.tensor_tensor(rstd[:, :], tmp[:, 1, :], tmp[:, 5, :], ALU.mult))


def norm_apply(nc, ch, out, rows, mv, rstd):
    for t in range(CT):
        ch.mark(nc.vector.tensor_scalar(out[:, t, :], rows[:, t, :], mv[:, t, 0:1], rstd[:, t:t + 1],
                                        ALU.subtract, ALU.mult))


def root(nc, act, tmp, var_ready, root_done, n):
    act.wait_ge(var_ready, n)
    nc.scalar.activation(tmp[:, 2, :], tmp[:, 0, :], ACT.Sqrt).then_inc(root_done, 1)


def transposed_place(bank, f, t):
    return bank[f][:, t * P:(t + 1) * P] if t < CT - 1 else bank[2][:, f * P:(f + 1) * P]


def transpose_chunk(nc, pe, bank, rows, ident):
    for t in range(CT):
        for f in range(KD):
            last = nc.tensor.transpose(transposed_place(bank, f, t), rows[:, t, f * P:(f + 1) * P], ident[:, :])
    return last


def evacuate_transposed(nc, bank, out):
    four = (CT - 1) * P
    nc.scalar.activation(out[:, 0, 0:four], bank[0][:, 0:four], ACT.Copy)
    nc.scalar.activation(out[:, 1, 0:four], bank[1][:, 0:four], ACT.Copy)
    return nc.scalar.activation(out[:, :, four:CH], bank[2][:, 0:2 * P].rearrange("p (f n) -> p f n", f=KD), ACT.Copy)


def over_chunks(eng, body):
    with eng.Fori(0, CHUNKS // 2) as i:
        body(i * 2, 0, i)
        body(i * 2 + 1, 1, i)
    assert CHUNKS % 2 == 1
    body(CHUNKS - 1, 0, CHUNKS // 2)


class Normalise:

    def __init__(self, nc, pr, g, rows_from, rows_to=None, idx=None):
        self.nc, self.g, self.rows_from, self.rows_to, self.idx = nc, g, rows_from, rows_to, idx
        self.xr = pr.sb("rows", [P, 2, CT, D], F32)
        self.xn = pr.sb("norm", [P, CT, D], F32)
        self.part = pr.sb("part", [P, CT, 2, D], F16)
        self.xt = pr.sb("xt", [P, KD, CH], F32)
        self.st = pr.sb("st", [P, CT, 6], F32)
        self.mv = pr.sb("mv", [P, CT, 2], F32)
        self.tmp = pr.sb("tmp", [P, 6, CT], F32)
        self.rstd = pr.sb("rstd", [P, CT], F32)
        if idx is not None:
            self.chosen = pr.sb("chosen", [P, 2, 2, CT, D], F32)
        self.bank = [pr.ps(f"ps{i}", [P, 512]) for i in range(3)]
        self.s = {n: pr.sem(n) for n in ("rows_in0", "rows_in1", "var_ready", "root_done", "norm_done", "rows_free0",
                                         "rows_free1", "high_done", "parts_done", "n_chain", "n_turned", "xt_ready",
                                         "part_out", "xt_out", "gathered0", "gathered1", "summed", "sum_out0",
                                         "sum_out1")}

    def chunk_of(self, ap, c):
        return ap.rearrange("(t p) d -> p t d", p=P)[:, ds(c * CT, CT), :]

    def sync(self, sp):
        s = self.s

        def body(c, u, i):
            at, to = (sp.snap(c * CT), sp.snap(c * (CT * 2 * D))) if not isinstance(c, int) else (c * CT, c * CT * 2 * D)
            rows = self.rows_from.rearrange("(t p) d -> p t d", p=P)[:, ds(at, CT), :]
            if self.idx is not None:
                sp.wait_ge(s[f"sum_out{u}"], 16 * i)
            sp.wait_ge(s[f"rows_free{u}"], i)
            sp.dma_start(self.xr[:, u, :, :], rows).then_inc(s[f"rows_in{u}"], 16)

        over_chunks(sp, body)

    def vector(self, dve):
        nc, s, part, xn = self.nc, self.s, self.part, self.xn
        ch = Chain(dve, s["n_chain"])
        per = NORM_MARKS + CT + (2 if self.idx is not None else 0)

        def body(c, u, i):
            xr = self.xr[:, u, :, :]
            ch.base, ch.n = c * per, 0
            dve.wait_ge(s[f"rows_in{u}"], 16 * (i + 1))
            if self.idx is not None:
                dve.wait_ge(s[f"gathered{u}"], 16 * 2 * CT * (i + 1))
                for n in range(2):
                    ch.done(nc.vector.tensor_tensor(xr, xr, self.chosen[:, u, n, :, :], ALU.add))
                dve.sem_inc(s["summed"], 1)
            norm_stats(nc, ch, xr, self.st, self.mv, s["var_ready"], s["root_done"], c + 1, self.rstd, self.tmp)
            dve.wait_ge(s["n_turned"], c)
            norm_apply(nc, ch, xn, xr, self.mv, self.rstd)
            ch.wait()
            dve.sem_inc(s["norm_done"], 1)
            assert ch.n == per, ch.n
            dve.wait_ge(s["part_out"], 16 * c)
            nc.vector.tensor_scalar(part[:, :, 0, :], xn[:, :, :], XS, None, ALU.mult).then_inc(s["high_done"], 1)
            dve.wait_ge(s["high_done"], c + 1)
            nc.vector.scalar_tensor_tensor(part[:, :, 1, :], xn[:, :, :], XS, part[:, :, 0, :],
                                           ALU.mult, ALU.subtract).then_inc(s["parts_done"], 1)

        over_chunks(dve, body)

    def scalar(self, act):
        nc, s = self.nc, self.s

        def body(c, u, i):
            if self.idx is not None:
                act.wait_ge(s["summed"], c + 1)
                act.dma_start(self.chunk_of(self.rows_to, c), self.xr[:, u, :, :]).then_inc(s[f"sum_out{u}"], 16)
            root(nc, act, self.tmp, s["var_ready"], s["root_done"], c + 1)
            act.wait_ge(s["norm_done"], c + 1)
            act.sem_inc(s[f"rows_free{u}"], 1)
            act.wait_ge(s["n_turned"], c + 1)
            act.wait_ge(s["xt_out"], 16 * c)
            evacuate_transposed(nc, self.bank, self.xt).then_inc(s["xt_ready"], 1)
            act.wait_ge(s["xt_ready"], c + 1)
            act.dma_start(self.g["xt"][:, :, ds(c * CH, CH)], self.xt[:, :, :]).then_inc(s["xt_out"], 16)
            act.wait_ge(s["parts_done"], c + 1)
            act.dma_start(self.g["parts"][:, ds(c * (CT * 2 * D), CT * 2 * D)],
                          self.part[:, :, :, :].rearrange("p t a d -> p (t a d)")).then_inc(s["part_out"], 16)

        over_chunks(act, body)
        act.wait_ge(s["part_out"], 16 * CHUNKS)
        act.wait_ge(s["xt_out"], 16 * CHUNKS)
        if self.idx is not None:
            act.wait_ge(s["sum_out0"], 16 * (CHUNKS // 2 + 1))
            act.wait_ge(s["sum_out1"], 16 * (CHUNKS // 2))

    def tensor(self, pe):
        s = self.s

        def body(c, u, i):
            pe.wait_ge(s["norm_done"], c + 1)
            pe.wait_ge(s["xt_ready"], c)
            transpose_chunk(self.nc, pe, self.bank, self.xn, self.g["ident"]).then_inc(s["n_turned"], 1)

        over_chunks(pe, body)

    def gpsimd(self, pool):
        for c in range(CHUNKS):
            if c >= 2:
                pool.wait_ge(self.s["summed"], c - 1)
            for n in range(2):
                for t in range(CT):
                    at = c * CT + t
                    pool.indirect_dma_start(out=self.chosen[:, c % 2, n, t, :], out_offset=None, in_=self.g["slots_out"],
                                            in_offset=bass.IndirectOffsetOnAxis(ap=self.idx[:, n, at:at + 1], axis=0)
                                            ).then_inc(self.s[f"gathered{c % 2}"], 16)


def normalise_sum(nc, g):
    with ExitStack() as ctx:
        pr = Prog(nc, ctx, "n2_")
        norm = Normalise(nc, pr, g, g["x1"], g["x2"], g["slot"])
        block = ctx.enter_context(nc.Block())
        block.sync(norm.sync)
        block.vector(norm.vector)
        block.scalar(norm.scalar)
        block.tensor(norm.tensor)
        block.gpsimd(norm.gpsimd)


def first_block(nc, io, g):
    with ExitStack() as ctx:
        pr = Prog(nc, ctx, "n1_")
        norm = Normalise(nc, pr, g, io["x"])
        zero = pr.sb("zero", [P, 8 * D], F32)
        zero_ready, zero_out, ident_ready, pool_chain = (pr.sem("zero_ready"), pr.sem("zero_out"),
                                                         pr.sem("ident_ready"), pr.sem("pool_chain"))
        dt = pr.sb("w_dst", [P, EG, P], I32)
        dn = pr.sb("w_next", [P, EG, P], I32)
        key = pr.sb("w_key", [P, WINS * VIS, 2], F16)
        low7 = pr.sb("w_low7", [P, WINS * VIS, 2], F16)
        wi = pr.sb("w_iota", [P, WG * P], I32)
        wlo = pr.sb("w_lo", [P, WG * P], F32)
        whi = pr.sb("w_hi", [P, WG * P], F32)
        first = pr.sb("w_first", [P, EG], F32)
        gt = pr.sb("w_gt", [P, EG * P], F32)
        below = pr.sb("w_below", [P, 2, EG, WG * P], F16)
        ones16 = pr.sb("w_ones16", [P, 1], F16)
        ones = pr.sb("w_ones", [P, 1], F32)
        m = pr.sb("w_m", [P, 2, WG], F32)
        lo = pr.sb("w_lotile", [P, 2, WG], F32)
        over = pr.sb("w_over", [P, WG + 1], F32)
        bad = pr.sb("w_bad", [P, 1], F32)
        idx = pr.sb("w_idx", [P, VIS, WG], I32)
        gd = pr.sb("w_gd", [P, WG, VIS, P], I32)
        gs = pr.sb("w_gs", [P, WG, VIS, P], I32)
        ints = pr.sb("w_ints", [P, 2, WG * VIS * P], I32)
        fl = pr.sb("w_fl", [P, 3, WG, VIS, P], F32)
        tr = pr.sb("w_tr", [P, 3, WG * P, VIS], F32)
        pm = pr.ps("w_pm", [P, 2 * WG])
        pt = [pr.ps(f"w_pt{i}", [P, VIS, P]) for i in range(2)]
        pf = pr.ps("w_pf", [P, 1])
        dst_in, iota_ready, below_ready = pr.sem("dst_in"), pr.sem("iota_ready"), pr.sem("below_ready")
        chain, counted, idx_ready, gathered = (pr.sem("vector_chain"), pr.sem("counted"), pr.sem("idx_ready"),
                                               pr.sem("gathered"))
        fl_ready, turned, taken, bad_ready, summed = (pr.sem("fl_ready"), pr.sem("turned"), pr.sem("taken"),
                                                      pr.sem("bad_ready"), pr.sem("bad_summed"))
        keys_ready, keys_out = pr.sem("keys_ready"), pr.sem("keys_out")
        block = ctx.enter_context(nc.Block())
        N = WG * VIS * P

        @block.sync
        def _(sp):
            sp.dma_start(dt[:, :, :], io["dst"][0:EG * P * P].rearrange("(g p e) -> p g e", p=P, e=P)).then_inc(dst_in, 16)
            sp.dma_start(dn[:, :, :], io["dst"][1:EG * P * P + 1].rearrange("(g p e) -> p g e", p=P, e=P)).then_inc(dst_in, 16)
            norm.sync(sp)
            sp.wait_ge(keys_ready, 2)
            sp.dma_start(g["keys"][0], key[:, :, :]).then_inc(keys_out, 16)
            sp.dma_start(g["keys"][1], low7[:, :, :]).then_inc(keys_out, 16)
            sp.wait_ge(keys_out, 32)

        block.scalar(norm.scalar)

        @block.gpsimd
        def _(pool):
            nc.gpsimd.memset(g["ident"][:, :], 0.0).then_inc(pool_chain, 1)
            pool.wait_ge(pool_chain, 1)
            nc.gpsimd.affine_select(out=g["ident"][:, :], in_=g["ident"][:, :], compare_op=ALU.not_equal, fill=1.0,
                                    base=0, pattern=[[-1, P]], channel_multiplier=1).then_inc(ident_ready, 1)
            nc.gpsimd.iota(wi[:, :], pattern=[[W, WG * P]], base=0, channel_multiplier=0).then_inc(iota_ready, 1)
            pool.wait_ge(idx_ready, 1)
            for w in range(WG):
                for i in range(VIS):
                    for rows, to in ((io["dst"], gd), (io["src"], gs)):
                        pool.indirect_dma_start(out=to[:, w, i, :], out_offset=None, in_=rows.rearrange("(t e) -> t e", e=P),
                                                in_offset=bass.IndirectOffsetOnAxis(ap=idx[:, i, w:w + 1], axis=0)
                                                ).then_inc(gathered, 16)
            pool.wait_ge(zero_ready, 1)
            for n in range(SLOTS // (8 * P)):
                pool.dma_start(g["slots_in"][n * 8 * P:(n + 1) * 8 * P, :].rearrange("(p r) d -> p (r d)", r=8),
                               zero[:, :]).then_inc(zero_out, 16)
            sure = 2 * ROWS // ST * ST
            half = (SLOTS - sure) // 2
            for n in range(2):
                pool.dma_start(g["slots_out"][sure + n * half:sure + (n + 1) * half, :].rearrange("(p r) d -> p (r d)", p=P),
                               zero[:, 0:half // P * D]).then_inc(zero_out, 16)
            pool.wait_ge(zero_out, 16 * (SLOTS // (8 * P) + 2))

        @block.vector
        def _(dve):
            ch = Chain(dve, chain)
            nc.vector.memset(zero[:, :], 0.0).then_inc(zero_ready, 1)
            ch.mark(nc.vector.memset(ones16[:, :], 1.0))
            ch.mark(nc.vector.memset(ones[:, :], 1.0))
            dve.wait_ge(iota_ready, 1)
            ch.mark(nc.vector.tensor_copy(wlo[:, :], wi[:, :]))
            ch.mark(nc.vector.tensor_scalar(whi[:, :], wi[:, :], float(W), None, ALU.add))
            dve.wait_ge(dst_in, 32)
            ch.mark(nc.vector.tensor_copy(first[:, :], dt[:, :, 0]))
            ch.done(nc.vector.tensor_tensor(gt[:, :], dt[:, :, :].rearrange("p g e -> p (g e)"),
                                            dn[:, :, :].rearrange("p g e -> p (g e)"), ALU.is_gt))
            ch.mark(nc.vector.reduce_sum(over[:, WG:WG + 1], gt[:, :], AX.X))
            for n, edge in ((0, wlo), (1, whi)):
                for q in range(EG):
                    last = nc.vector.tensor_scalar(below[:, n, q, :], edge[:, :], first[:, q:q + 1], None, ALU.is_gt)
            last.then_inc(below_ready, 1)
            dve.wait_ge(counted, 1)
            ch.done(nc.vector.tensor_copy(m[:, :, :], pm[:, :].rearrange("p (n w) -> p n w", n=2)))
            ch.done(nc.vector.tensor_scalar(lo[:, 0, :], m[:, 0, :], -1.0, 0.0, ALU.add, ALU.max))
            for i in range(VIS):
                last = nc.vector.tensor_scalar(idx[:, i, :], lo[:, 0, :], float(i), None, ALU.add)
            last.then_inc(idx_ready, 1)
            ch.done(nc.vector.tensor_tensor(lo[:, 1, :], m[:, 1, :], lo[:, 0, :], ALU.subtract))
            ch.done(nc.vector.tensor_scalar(over[:, 0:WG], lo[:, 1, :], float(VIS), None, ALU.is_gt))
            nc.vector.reduce_sum(bad[:, :], over[:, :], AX.X).then_inc(bad_ready, 1)
            dve.wait_ge(summed, 1)
            ch.mark(nc.vector.tensor_copy(g["flag"][0:1, 0:1], pf[0:1, 0:1]))
            norm.vector(dve)
            dve.wait_ge(gathered, 16 * 2 * WG * VIS)
            src = gs[:, :, :, :].rearrange("p w i e -> p (w i e)")
            dst = gd[:, :, :, :].rearrange("p w i e -> p (w i e)")
            flat = fl[:, :, :, :, :].rearrange("p a w i e -> p a (w i e)")
            ch.mark(nc.vector.tensor_scalar(ints[:, 0, :], src, 7, None, ALU.logical_shift_right))
            ch.done(nc.vector.tensor_scalar(ints[:, 1, :], src, P - 1, None, ALU.bitwise_and))
            ch.mark(nc.vector.tensor_copy(flat[:, 0, :], dst))
            ch.mark(nc.vector.scalar_tensor_tensor(flat[:, 1, :], ints[:, 0, :], float(W), dst, ALU.mult, ALU.add))
            nc.vector.tensor_copy(flat[:, 2, :], ints[:, 1, :]).then_inc(fl_ready, 1)
            dve.wait_ge(fl_ready, 1)
            for n in range(3 * WG):
                a, w = divmod(n, WG)
                dve.wait_ge(turned, n + 1)
                nc.vector.tensor_copy(tr[:, a, w * P:(w + 1) * P, :].rearrange("p v i -> p i v"),
                                      pt[n % 2][:, :, :]).then_inc(taken, 1)
            dve.wait_ge(taken, 3 * WG)
            base = wlo[:, :].unsqueeze(2).broadcast_to([P, WG * P, VIS])
            t1, t2 = fl[:, 0, :, :, :].rearrange("p w i e -> p (w i e)"), fl[:, 1, :, :, :].rearrange("p w i e -> p (w i e)")
            u = fl[:, 2, :, :, :].rearrange("p w i e -> p (w i e)")
            three = lambda ap: ap.rearrange("p (v i) -> p v i", i=VIS)
            ch.mark(nc.vector.tensor_tensor(three(t1), tr[:, 0, :, :], base, ALU.subtract))
            ch.done(nc.vector.tensor_tensor(three(t2), tr[:, 1, :, :], base, ALU.subtract))
            ch.done(nc.vector.tensor_scalar(t2, t2, 1.0, None, ALU.add))
            ch.done(nc.vector.scalar_tensor_tensor(u, t1, 0.0, t2, ALU.is_ge, ALU.mult))
            n = WINS * VIS
            twice = lambda ap: ap.unsqueeze(2).broadcast_to([P, n, 2])
            nc.vector.scalar_tensor_tensor(key[:, :, :], twice(t1[:, 0:n]), float(W), twice(u[:, 0:n]),
                                           ALU.is_lt, ALU.mult).then_inc(keys_ready, 1)
            nc.vector.tensor_copy(low7[:, :, :],
                                  twice(tr[:, 2, :, :].rearrange("p v i -> p (v i)")[:, 0:n])).then_inc(keys_ready, 1)

        @block.tensor
        def _(pe):
            pe.wait_ge(below_ready, 1)
            for n in range(2):
                for w in range(WG):
                    for q in range(EG):
                        last = nc.tensor.matmul(pm[:, n * WG + w:n * WG + w + 1], below[:, n, q, w * P:(w + 1) * P],
                                                ones16[:, :], start=(q == 0), stop=(q == EG - 1))
            last.then_inc(counted, 1)
            pe.wait_ge(bad_ready, 1)
            nc.tensor.matmul(pf[0:1, 0:1], bad[:, :], ones[:, :], start=True, stop=True).then_inc(summed, 1)
            pe.wait_ge(ident_ready, 1)
            norm.tensor(pe)
            pe.wait_ge(fl_ready, 1)
            for n in range(3 * WG):
                a, w = divmod(n, WG)
                if n >= 2:
                    pe.wait_ge(taken, n - 1)
                for i in range(VIS):
                    last = nc.tensor.transpose(pt[n % 2][:, i, :], fl[:, a, w, i, :], g["ident"][:, :])
                last.then_inc(turned, 1)


def aggregate(nc, pe, flag, adj, at, stationary, bank, hib, hi_in, hi_used, n, before=None):
    def tile(k, moving, first=False, last=False):
        if before and isinstance(k, int):
            before(k)
        seen = set()
        ops = stationary(k)
        for j, (f, operand) in enumerate(ops):
            ins = nc.tensor.matmul(bank[f], operand, moving, start=first and f not in seen,
                                   stop=last and f not in [x for x, _ in ops[j + 1:]])
            seen.add(f)
        return ins

    def upper_counts():
        if before:
            before(TILES - 1)
        with pe.Fori(0, TILES) as k:
            pe.wait_ge(hi_in, 16 * (n * TILES + k + 1))
            tile(k, hib[:, :])
            tile(k, hib[:, :]).then_inc(hi_used, 1)

    tile(0, adj[:, 0, at], first=True)
    if flag is None:
        upper_counts()
    else:
        with pe.If(flag != 0):
            upper_counts()
        with pe.Else():
            pe.nop()
    for k in range(1, TILES):
        ins = tile(k, adj[:, k, at], last=(k == TILES - 1))
    return ins


def feed_upper_counts(sp, g, flag, hib, hi_in, hi_used):
    def feed():
        with sp.Fori(0, 2 * CHUNKS) as n:
            with sp.Fori(0, TILES) as k:
                sp.wait_ge(hi_used, n * TILES + k)
                sp.dma_start(hib[:, :], g["upper"][ds(k * P, P), ds(n * SUB, SUB)]).then_inc(hi_in, 16)

    if flag is None:
        feed()
    else:
        with sp.If(flag != 0):
            feed()
        with sp.Else():
            sp.nop()


def build_counts(nc, io, g, adj):
    with ExitStack() as ctx:
        pr = Prog(nc, ctx)
        key = pr.sb("b_key", [P, WINS * VIS, 2], F16)
        low7 = pr.sb("b_low7", [P, WINS * VIS, 2], F16)
        it = pr.sb("b_it", [P, WG * P], I32)
        it16 = pr.sb("b_it16", [P, NW], F16)
        ib16 = pr.sb("b_ib16", [P, P], F16)
        ones = pr.sb("b_ones", [P, 1], F16)
        sel = pr.sb("b_sel", [P, SLOT * GW * VIS, NW], F16)
        low = pr.sb("b_low", [P, SLOT * GW * VIS, P], F16)
        degree = pr.sb("b_degree", [1, ROWS], F32)
        by_part = pr.sb("b_by_part", [P, 3, TILES], F32)
        win = pr.sb("b_win", [P, WINS], F32)
        gst = pr.sb("g_st", [P, 2, SG], I32)
        gi = pr.sb("g_int", [P, 2, SG], I32)
        gf = pr.sb("g_fl", [P, 3, SG], F32)
        gk = pr.sb("g_key", [P, SG, 2], F16)
        gl = pr.sb("g_low", [P, SG, 2], F16)
        gc = pr.sb("g_count", [P, 3, NW], I32)
        ghi = pr.sb("g_hi", [P, NW], F16)
        hib = pr.sb("g_hib", [P, SUB], F16)
        pw = [pr.ps(f"b_pw{i}", [P, 512]) for i in range(SLOT)]
        pd = pr.ps("b_pd", [P, SUB])
        s = {n: pr.sem("b_" + n) for n in (
            "const", "chain", "ready", "sel_ready", "multiplied", "copied", "g_in", "g_sel", "g_mult", "g_win",
            "g_split", "g_copied", "g_hi_out", "g_edge", "hi_in", "hi_used", "deg", "deg_taken", "deg_out", "deg_in", "by_part", "inv_done", "inv_out", "adj_done", "keys_in")}
        block = ctx.enter_context(nc.Block())
        NWIN = WINS * W

        def one_hot(out, values, names, width):
            r = values.shape[1]
            shape = [P, r, width // 2, 2]
            return nc.vector.tensor_tensor(
                out.rearrange("p r (h two) -> p r h two", two=2),
                names[:, 0:width].rearrange("p (h two) -> p h two", two=2).unsqueeze(1).broadcast_to(shape),
                values.unsqueeze(2).broadcast_to(shape), ALU.is_equal)

        @block.gpsimd
        def _(pool):
            nc.gpsimd.iota(it[:, :], pattern=[[1, WG * P]], base=0, channel_multiplier=0).then_inc(s["const"], 1)

        @block.vector
        def _(dve):
            ch = Chain(dve, s["chain"])
            dve.wait_ge(s["const"], 1)
            ch.mark(nc.vector.tensor_copy(it16[:, :], it[:, 1:NW + 1]))
            ch.mark(nc.vector.tensor_copy(ib16[:, :], it[:, 0:P]))
            ch.mark(nc.vector.memset(ones[:, :], 1.0))
            ch.mark(nc.vector.tensor_scalar(win[:, :], it[:, 0:WINS], float(W), None, ALU.mult))
            ch.mark(nc.vector.memset(adj[:, :, NWIN:ROWS], 0.0))
            ch.mark(nc.vector.memset(degree[:, NWIN:ROWS], 0.0))
            ch.wait()
            nc.vector.memset(gf[:, 0, :], 0.0).then_inc(s["ready"], 1)
            dve.wait_ge(s["ready"], 1)
            flag = dve.value_load(g["flag"][0:1, 0:1])
            with dve.If(flag != 0):
                with dve.Fori(0, WINS) as v:
                    with dve.Fori(0, SSTEPS) as u:
                        n = v * SSTEPS + u
                        gch = Chain(dve, s["g_edge"])
                        gch.base = (n * 6) + v * 3
                        dve.wait_ge(s["g_in"], 32 * (n + 1))
                        gch.mark(nc.vector.tensor_scalar(gi[:, 0, :], gst[:, 1, :], 7, None, ALU.logical_shift_right))
                        gch.mark(nc.vector.tensor_scalar(gi[:, 1, :], gst[:, 1, :], P - 1, None, ALU.bitwise_and))
                        gch.done(nc.vector.tensor_scalar(gf[:, 0, :], gst[:, 0, :], win[:, ds(v, 1)], None, ALU.subtract))
                        gch.done(nc.vector.scalar_tensor_tensor(gf[:, 1, :], gi[:, 0, :], float(W), gf[:, 0, :],
                                                                ALU.mult, ALU.add))
                        gch.done(nc.vector.tensor_scalar(gf[:, 2, :], gf[:, 1, :], 1.0, None, ALU.add))
                        dve.wait_ge(s["g_mult"], n)
                        gch.done(nc.vector.scalar_tensor_tensor(gf[:, 1, :], gf[:, 0, :], 0.0, gf[:, 2, :],
                                                                ALU.is_ge, ALU.mult))
                        two = lambda ap: ap.unsqueeze(2).broadcast_to([P, SG, 2])
                        nc.vector.scalar_tensor_tensor(gk[:, :, :], two(gf[:, 0, :]), float(W), two(gf[:, 1, :]),
                                                       ALU.is_lt, ALU.mult).then_inc(s["g_split"], 1)
                        nc.vector.tensor_copy(gl[:, :, :], two(gi[:, 1, :])).then_inc(s["g_split"], 1)
                        dve.wait_ge(s["g_split"], 2 * (n + 1))
                        one_hot(sel[:, 0:SG, :], gk[:, :, :], it16, NW)
                        one_hot(low[:, 0:SG, :], gl[:, :, :], ib16, P).then_inc(s["g_sel"], 1)
                    gch = Chain(dve, s["g_edge"])
                    gch.base = (v + 1) * SSTEPS * 6 + v * 3
                    dve.wait_ge(s["g_win"], v + 1)
                    gch.done(nc.vector.tensor_copy(gc[:, 0, :], pw[0][:, 0:NW]))
                    gch.mark(nc.vector.tensor_scalar(gc[:, 1, :], gc[:, 0, :], 11, None, ALU.logical_shift_right))
                    gch.done(nc.vector.tensor_scalar(gc[:, 2, :], gc[:, 0, :], int(SPLIT) - 1, None, ALU.bitwise_and))
                    dve.wait_ge(s["g_hi_out"], 16 * (v + 1))
                    nc.vector.tensor_copy(adj[:, :, ds(v * W, W)], gc[:, 2, :].rearrange("p (k j) -> p k j", j=W))
                    nc.vector.tensor_scalar(ghi[:, :], gc[:, 1, :], SPLIT / 2, None, ALU.mult).then_inc(s["g_copied"], 1)
                dve.wait_ge(s["g_copied"], WINS)
                nc.vector.memset(gf[:, 0, :], 0.0).then_inc(s["adj_done"], 1)
            with dve.Else():
                dve.wait_ge(s["keys_in"], 32)
                with dve.Fori(0, BODIES) as body:
                    for u in range(UNROLL):
                        group = body * UNROLL + u
                        at, slot = ds(group * GW * VIS, GW * VIS), slice(u % SLOT * GW * VIS, (u % SLOT + 1) * GW * VIS)
                        dve.wait_ge(s["multiplied"], group)
                        one_hot(sel[:, slot, :], key[:, at, :], it16, NW)
                        one_hot(low[:, slot, :], low7[:, at, :], ib16, P).then_inc(s["sel_ready"], 1)
            dve.wait_ge(s["deg_in"], 16)
            nc.vector.tensor_scalar(by_part[:, 1, :], by_part[:, 0, :], 1.0, XS, ALU.max, ALU.mult).then_inc(s["by_part"], 1)
            dve.wait_ge(s["by_part"], 1)
            nc.vector.reciprocal(by_part[:, 2, :], by_part[:, 1, :]).then_inc(s["inv_done"], 1)

        @block.scalar
        def _(act):
            act.wait_ge(s["ready"], 1)
            flag = act.value_load(g["flag"][0:1, 0:1])
            with act.If(flag != 0):
                with act.Fori(0, 2 * CHUNKS) as n:
                    act.wait_ge(s["deg"], n + 1)
                    nc.scalar.activation(degree[:, ds(n * SUB, SUB)], pd[0:1, 0:SUB], ACT.Copy).then_inc(s["deg_taken"], 1)
                act.wait_ge(s["deg_taken"], 2 * CHUNKS)
            with act.Else():
                act.sem_inc(s["copied"], SLOT - 1)

                def take_degrees(body):
                    act.wait_ge(s["deg"], body + 1)
                    nc.scalar.activation(degree[:, ds(body * BW, BW)], pd[0:1, 0:BW], ACT.Copy).then_inc(s["deg_taken"], 1)

                def take_counts(body, u):
                    group = body * UNROLL + u
                    act.wait_ge(s["multiplied"], group + SLOT)
                    nc.scalar.activation(
                        adj[:, :, ds(group * GW * W, GW * W)].rearrange("p k (w j) -> p w k j", j=W),
                        pw[u % SLOT][:, 0:GW * NW].rearrange("p (w k j) -> p w k j", w=GW, j=W), ACT.Copy).then_inc(s["copied"], 1)

                for u in range(UNROLL):
                    take_counts(0, u)
                with act.Fori(1, BODIES) as body:
                    for u in range(UNROLL):
                        take_counts(body, u)
                        if u == 4:
                            take_degrees(body - 1)
                take_degrees(BODIES - 1)
                act.wait_ge(s["deg_taken"], BODIES)
            act.dma_start(g["degree"], degree[:, :]).then_inc(s["deg_out"], 16)
            act.wait_ge(s["deg_out"], 16)
            spread = lambda ap: ap.rearrange("a (p t) -> (a p) t", p=P)
            act.dma_start(by_part[:, 0, :], spread(g["degree"])).then_inc(s["deg_in"], 16)
            act.wait_ge(s["inv_done"], 1)
            act.dma_start(spread(g["inv"]), by_part[:, 2, :]).then_inc(s["inv_out"], 16)
            act.wait_ge(s["inv_out"], 16)

        @block.tensor
        def _(pe):
            pe.wait_ge(s["ready"], 1)
            pe.sem_inc(s["multiplied"], SLOT - 1)
            flag = pe.value_load(g["flag"][0:1, 0:1])
            with pe.If(flag != 0):
                with pe.Fori(0, WINS) as v:
                    def step(n, first):
                        pe.wait_ge(s["g_sel"], n + 1)
                        for i in range(SG):
                            ins = nc.tensor.matmul(pw[0][:, 0:NW], low[:, i, :], sel[:, i, 0:NW],
                                                   start=first and i == 0, stop=i == SG - 1)
                        ins.then_inc(s["g_mult"], 1)
                    pe.wait_ge(s["g_copied"], v)
                    step(v * SSTEPS, True)
                    with pe.Fori(1, SSTEPS) as u:
                        step(v * SSTEPS + u, False)
                    pe.wait_ge(s["g_mult"], (v + 1) * SSTEPS)
                    pe.sem_inc(s["g_win"], 1)
                pe.wait_ge(s["adj_done"], 1)
                with pe.Fori(0, 2 * CHUNKS) as n:
                    pe.wait_ge(s["deg_taken"], n)
                    aggregate(nc, pe, None, adj, ds(n * SUB, SUB), lambda k: [(0, ones[:, :])], [pd[0:1, 0:SUB]],
                              hib, s["hi_in"], s["hi_used"], n).then_inc(s["deg"], 1)
            with pe.Else():
                def count(body, u):
                    group = body * UNROLL + u
                    pe.wait_ge(s["sel_ready"], group + 1)
                    pe.wait_ge(s["copied"], group)
                    for w in range(GW):
                        for i in range(VIS):
                            n = (u % SLOT * GW + w) * VIS + i
                            ins = nc.tensor.matmul(pw[u % SLOT][:, w * NW:(w + 1) * NW], low[:, n, :], sel[:, n, :],
                                                   start=i == 0, stop=i == VIS - 1)
                    ins.then_inc(s["multiplied"], 1)

                def degrees(body, tiles=range(TILES)):
                    if 0 in tiles:
                        pe.wait_ge(s["copied"], (body + 1) * UNROLL + SLOT - 1)
                        pe.wait_ge(s["deg_taken"], body)
                    for k in tiles:
                        ins = nc.tensor.matmul(pd[0:1, 0:BW], ones[:, :], adj[:, k, ds(body * BW, BW)],
                                               start=k == 0, stop=k == TILES - 1)
                    if TILES - 1 in tiles:
                        ins.then_inc(s["deg"], 1)

                for u in range(UNROLL):
                    count(0, u)
                with pe.Fori(1, BODIES) as body:
                    for u in range(UNROLL):
                        count(body, u)
                        if u in (1, 2, 3):
                            degrees(body - 1, range(TILES * (u - 1) // 3, TILES * u // 3))
                degrees(BODIES - 1)

        @block.sync
        def _(sp):
            sp.dma_start(key[:, :, :], g["keys"][0]).then_inc(s["keys_in"], 16)
            sp.dma_start(low7[:, :, :], g["keys"][1]).then_inc(s["keys_in"], 16)
            sp.wait_ge(s["ready"], 1)
            flag = sp.value_load(g["flag"][0:1, 0:1])
            with sp.If(flag != 0):
                sp.dma_start(g["upper"].rearrange("(k p) n -> p k n", p=P)[:, :, NWIN:ROWS],
                             adj[:, :, NWIN:ROWS]).then_inc(s["g_hi_out"], 16)
                with sp.Fori(0, WINS) as v:
                    with sp.Fori(0, SSTEPS) as u:
                        sp.wait_ge(s["g_sel"], v * SSTEPS + u)
                        for n, rows in enumerate((io["dst"], io["src"])):
                            sp.dma_start(gst[:, n, :], rows.rearrange("(t e) -> e t", e=P)[:, ds(u * SG, SG)],
                                         allow_slow_non_contiguous=True).then_inc(s["g_in"], 16)
                    sp.wait_ge(s["g_copied"], v + 1)
                    sp.dma_start(g["upper"].rearrange("(k p) n -> p k n", p=P)[:, :, ds(v * W, W)],
                                 ghi[:, :].rearrange("p (k j) -> p k j", j=W)).then_inc(s["g_hi_out"], 16)
                sp.wait_ge(s["g_hi_out"], 16 * (WINS + 1))
                feed_upper_counts(sp, g, None, hib, s["hi_in"], s["hi_used"])
            with sp.Else():
                sp.nop()


BT = -(-CT // 2)


def in_bank(banks, n):
    count = min(2, CT - 2 * n)
    return slice(2 * n, 2 * n + count), banks[n][:, 0:count * D].rearrange("p (t d) -> p t d", d=D)


def conv_tensors(pr, parts):
    t = {
        "parts": parts,
        "inv": pr.sb("c_inv", [P, CH], F32),
        "mean": pr.sb("c_mean", [P, KD, CH], F32),
        "own": pr.sb("c_own", [P, KD, CH], F32),
        "wl": pr.sb("c_wl", [P, KD, D], F32),
        "wr": pr.sb("c_wr", [P, KD, D], F32),
        "hib": pr.sb("c_hib", [P, SUB], F16),
        "agg": [[pr.ps(f"c_agg{h}{f}", [P, SUB]) for f in range(KD)] for h in range(2)],
        "bank": [pr.ps(f"c_bank{i}", [P, 512]) for i in range(4)],
    }
    return t


def conv_tensor_engine(nc, g, adj, t, s, dense, turn, turn_at, score=None, loading=False):
    def agg(pe, flag, c, h, before=None):
        def parts_loaded(k):
            if k % CT == 0 or k == TILES - 1:
                for i in range(0 if k == TILES - 1 else k // CT, k // CT + 1):
                    pe.wait_ge(s[f"parts_in{i}"], 16)
        pe.wait_ge(s["mean_done"], 4 * c - 2 + 2 * h) if not isinstance(c, int) else None
        aggregate(nc, pe, flag, adj, ds(c * CH + h * SUB, SUB),
                  lambda k: [(f, t["parts"][:, k, a, f * P:(f + 1) * P]) for a in range(2) for f in range(KD)],
                  [t["agg"][h][f][:, :] for f in range(KD)], t["hib"], s["hi_in"], s["hi_used"], 2 * c + h,
                  parts_loaded if loading and isinstance(c, int) and h == 0 else before).then_inc(s["agg_done"], 1)

    def run(pe):
        flag = pe.value_load(g["flag"][0:1, 0:1])
        agg(pe, flag, 0, 0)
        agg(pe, flag, 0, 1)
        with pe.Fori(1, CHUNKS) as c:
            agg(pe, flag, c, 0)
            dense(pe, c - 1)
            agg(pe, flag, c, 1, lambda k: turn(pe, c - 1) if k == turn_at else None)
            if score:
                score(pe, c - 1)
        dense(pe, CHUNKS - 1)
        turn(pe, CHUNKS - 1)
        if score:
            score(pe, CHUNKS - 1)
    return run


def mean_half(nc, dve, t, s, c, h):
    dve.wait_ge(s["agg_done"], 2 * c + h + 1)
    if h == 0:
        dve.wait_ge(s["inv_in"], 16 * (c + 1))
        dve.wait_ge(s["dense_done"], c)
    for f in range(KD):
        at = slice(h * SUB, (h + 1) * SUB)
        nc.vector.tensor_tensor(t["mean"][:, f, at], t["agg"][h][f][:, :], t["inv"][:, at], ALU.mult
                                ).then_inc(s["mean_done"], 1)


def load_parts(sp, g, t, i, sem):
    sp.dma_start(t["parts"][:, i * CT:(i + 1) * CT, :, :].rearrange("p t a d -> p (t a d)"),
                 g["parts"][:, i * CT * 2 * D:(i + 1) * CT * 2 * D]).then_inc(sem, 16)


def load_chunk_inv(sp, g, t, s, c, at):
    sp.wait_ge(s["mean_done"], 4 * c)
    sp.dma_start(t["inv"][:, :], g["inv"][:, ds(at, CH)].broadcast_to([P, CH])).then_inc(s["inv_in"], 16)


CONV_SEMS = ("weights_in", "inv_in", "own_in", "agg_done", "mean_done", "dense_done", "hi_in",
             "hi_used", "chain", "ready", "turned", "stored")


def first_conv(nc, io, g, adj, parts, tag, names):
    wl, b, wr = names
    with ExitStack() as ctx:
        pr = Prog(nc, ctx, tag)
        t = conv_tensors(pr, parts)
        h = pr.sb("c_h", [P, KD, CH], F32)
        bias = pr.sb("c_bias", [P, KD], F32)
        small = pr.sb("c_small", [P, 6, KD], F32)
        part = t["own"][:, :, :].bitcast(F16).rearrange("p f n -> p (f n)").rearrange("p (t a d) -> p t a d", t=CT, a=2)
        s = {n: pr.sem("f_" + n) for n in CONV_SEMS + tuple(f"parts_in{i}" for i in range(CHUNKS)) + ("norms_in", "group_done", "h_done", "h_out", "high_done",
                                                       "low_done", "part_out", "scale_done", "next_in")}
        block = ctx.enter_context(nc.Block())

        @block.sync
        def _(sp):
            for i in range(CHUNKS):
                load_parts(sp, g, t, i, s[f"parts_in{i}"])
            sp.dma_start(bias[:, :], io[b].rearrange("(f p) -> p f", p=P), allow_slow_non_contiguous=True).then_inc(s["norms_in"], 16)
            sp.dma_start(t["mean"][:, :, 0:D], io[wl].rearrange("(f p) k -> p f k", p=P)).then_inc(s["norms_in"], 16)
            sp.dma_start(t["mean"][:, :, D:2 * D], io[wr].rearrange("(f p) k -> p f k", p=P)).then_inc(s["norms_in"], 16)
            sp.dma_start(t["wl"][:, :, :], io[wl + "_T"].rearrange("(k p) f -> p k f", p=P)).then_inc(s["weights_in"], 16)
            sp.dma_start(t["wr"][:, :, :], io[wr + "_T"].rearrange("(k p) f -> p k f", p=P)).then_inc(s["weights_in"], 16)

            with sp.Fori(0, CHUNKS) as c:
                at = sp.snap(c * CH)
                load_chunk_inv(sp, g, t, s, c, at)
                sp.wait_ge(s["part_out"], 16 * c)
                sp.dma_start(t["own"][:, :, :], g["xt"][:, :, ds(at, CH)]).then_inc(s["own_in"], 16)
            sp.wait_ge(s["agg_done"], 2 * CHUNKS)
            for i in range(CHUNKS):
                if i == CHUNKS - 1:
                    sp.wait_ge(s["part_out"], 16 * CHUNKS)
                load_parts(sp, g, t, i, s["next_in"])
            sp.wait_ge(s["next_in"], 16 * CHUNKS)

        @block.gpsimd
        def _(pool):
            flag = pool.value_load(g["flag"][0:1, 0:1])
            feed_upper_counts(pool, g, flag, t["hib"], s["hi_in"], s["hi_used"])

        @block.vector
        def _(dve):
            ch = Chain(dve, s["chain"])
            dve.wait_ge(s["norms_in"], 48)
            for f in range(KD):
                ch.mark(nc.vector.tensor_reduce(small[:, 0, f:f + 1], t["mean"][:, f, 0:2 * D], AX.X, ALU.add,
                                                apply_absolute_value=True))
                ch.mark(nc.vector.tensor_reduce(small[:, 1, f:f + 1], bias[:, f:f + 1], AX.X, ALU.add,
                                                apply_absolute_value=True))
            ch.wait()
            ch.done(nc.vector.scalar_tensor_tensor(small[:, 2, :], small[:, 0, :], 16.0, small[:, 1, :], ALU.mult, ALU.add))
            ch.done(nc.vector.tensor_scalar(small[:, 3, :], small[:, 2, :], 1e-20, None, ALU.max))
            ch.done(nc.vector.tensor_scalar(small[:, 4, :].bitcast(I32), small[:, 3, :].bitcast(I32), 0x7F800000, None,
                                            ALU.bitwise_and))
            ch.done(nc.vector.tensor_scalar(g["unscale"][:, :], small[:, 4, :], 2.0 ** -14, None, ALU.mult))
            ch.done(nc.vector.reciprocal(g["scale"][:, :], g["unscale"][:, :]))
            nc.vector.tensor_tensor(small[:, 5, :], bias[:, :], g["scale"][:, :], ALU.mult).then_inc(s["scale_done"], 1)

            def low_parts(c):
                for n in range(BT):
                    dve.wait_ge(s["high_done"], BT * c + n + 1)
                    tiles, bank = in_bank(t["bank"], n)
                    nc.vector.tensor_tensor(part[:, tiles, 1, :], bank, part[:, tiles, 0, :], ALU.subtract
                                            ).then_inc(s["low_done"], 1)

            mean_half(nc, dve, t, s, 0, 0)
            mean_half(nc, dve, t, s, 0, 1)
            with dve.Fori(1, CHUNKS) as c:
                mean_half(nc, dve, t, s, c, 0)
                low_parts(c - 1)
                mean_half(nc, dve, t, s, c, 1)
            low_parts(CHUNKS - 1)

        @block.scalar
        def _(act):
            act.wait_ge(s["scale_done"], 1)
            with act.Fori(0, CHUNKS) as c:
                act.wait_ge(s["h_out"], 16 * c)
                act.wait_ge(s["turned"], BT * c)
                for n in range(4):
                    f, half = n % 2, n // 2
                    act.wait_ge(s["group_done"], 4 * c + n + 1)
                    nc.scalar.activation(h[:, f, half * SUB:(half + 1) * SUB], t["bank"][n][:, 0:SUB], ACT.Relu,
                                         bias=small[:, 5, f:f + 1], scale=g["scale"][:, f:f + 1]).then_inc(s["h_done"], 1)
                act.wait_ge(s["h_done"], 4 * (c + 1))
                act.dma_start(g["ht"][:, :, ds(c * CH, CH)], h[:, :, :]).then_inc(s["h_out"], 16)
                for n in range(BT):
                    act.wait_ge(s["turned"], BT * c + n + 1)
                    tiles, bank = in_bank(t["bank"], n)
                    nc.scalar.activation(part[:, tiles, 0, :], bank, ACT.Copy).then_inc(s["high_done"], 1)
                act.wait_ge(s["low_done"], BT * (c + 1))
                act.dma_start(g["parts"][:, ds(c * CT * 2 * D, CT * 2 * D)],
                              part.rearrange("p t a d -> p (t a d)")).then_inc(s["part_out"], 16)
            act.wait_ge(s["h_out"], 16 * CHUNKS)
            act.wait_ge(s["part_out"], 16 * CHUNKS)

        def dense(pe, c):
            pe.wait_ge(s["weights_in"], 32)
            pe.wait_ge(s["mean_done"], 4 * (c + 1))
            pe.wait_ge(s["own_in"], 16 * (c + 1))
            pe.wait_ge(s["low_done"], BT * c)
            for n in range(4):
                f, at = n % 2, slice(n // 2 * SUB, (n // 2 + 1) * SUB)
                for k in range(KD):
                    nc.tensor.matmul(t["bank"][n][:, 0:SUB], t["wl"][:, k, f * P:(f + 1) * P], t["mean"][:, k, at],
                                     start=k == 0, stop=False)
                for k in range(KD):
                    ins = nc.tensor.matmul(t["bank"][n][:, 0:SUB], t["wr"][:, k, f * P:(f + 1) * P], t["own"][:, k, at],
                                           start=False, stop=k == KD - 1)
                ins.then_inc(s["group_done"], 1)
            pe.wait_ge(s["group_done"], 4 * (c + 1))
            pe.sem_inc(s["dense_done"], 1)

        def turn(pe, c):
            pe.wait_ge(s["h_done"], 4 * (c + 1))
            for n in range(CT):
                for f in range(KD):
                    ins = nc.tensor.transpose(t["bank"][n // 2][:, n % 2 * D + f * P:n % 2 * D + (f + 1) * P],
                                              h[:, f, n * P:(n + 1) * P], g["ident"][:, :])
                if n % 2 or n == CT - 1:
                    ins.then_inc(s["turned"], 1)

        block.tensor(conv_tensor_engine(nc, g, adj, t, s, dense, turn, 10, loading=True))


def second_conv(nc, io, g, adj, parts, tag, names, gate, rows_from, rows_to, keep_norm):
    wl, b, wr = names
    with ExitStack() as ctx:
        pr = Prog(nc, ctx, tag)
        t = conv_tensors(pr, parts)
        xr = pr.sb("s_rows", [P, CT, D], F32)
        bias = pr.sb("s_bias", [P, D], F32)
        gate_w, gate_b = io[gate[0]], io[gate[1]]
        E = gate_w.shape[1]
        wg = pr.sb("s_gate_w", [P, KD, E], F32)
        bg = pr.sb("s_gate_b", [P, E], F32)
        st = pr.sb("s_st", [P, CT, 6], F32)
        mv = pr.sb("s_mv", [P, CT, 2], F32)
        tmp = pr.sb("s_tmp", [P, 6, CT], F32)
        rstd = pr.sb("s_rstd", [P, CT], F32)
        s = {n: pr.sem("s_" + n) for n in CONV_SEMS + ("bias_in", "rows_in", "tile_done", "sum_done", "x_out",
                                                       "var_ready", "root_done", "norm_done", "xt_ready", "xt_out",
                                                       "norm_out", "scaled", "gate_in", "scored", "score_done")}
        block = ctx.enter_context(nc.Block())
        chunk_of = lambda ap, c: ap.rearrange("(t p) d -> p t d", p=P)[:, ds(c * CT, CT), :]

        @block.sync
        def _(sp):
            sp.dma_start(t["wl"][:, :, :], io[wl + "_T"].rearrange("(k p) f -> p k f", p=P)).then_inc(s["weights_in"], 16)
            sp.dma_start(t["wr"][:, :, :], io[wr + "_T"].rearrange("(k p) f -> p k f", p=P)).then_inc(s["weights_in"], 16)
            sp.dma_start(bias[:, :], io[b].rearrange("(a n) -> a n", a=1).broadcast_to([P, D])).then_inc(s["bias_in"], 16)
            sp.dma_start(wg[:, :, :], gate_w.rearrange("(k p) e -> p k e", p=P)).then_inc(s["gate_in"], 16)
            sp.dma_start(bg[:, :], gate_b.rearrange("(a e) -> a e", a=1).broadcast_to([P, E])).then_inc(s["gate_in"], 16)
            with sp.Fori(0, CHUNKS) as c:
                at = sp.snap(c * CH)
                load_chunk_inv(sp, g, t, s, c, at)
                if keep_norm:
                    sp.wait_ge(s["norm_out"], 16 * c)
                sp.wait_ge(s["turned"], c)
                sp.dma_start(xr[:, :, :], chunk_of(rows_from, c)).then_inc(s["rows_in"], 16)
                sp.wait_ge(s["xt_out"], 16 * c)
                sp.wait_ge(s["scored"], c)
                sp.dma_start(t["own"][:, :, :], g["ht"][:, :, ds(at, CH)]).then_inc(s["own_in"], 16)

        @block.gpsimd
        def _(pool):
            flag = pool.value_load(g["flag"][0:1, 0:1])
            feed_upper_counts(pool, g, flag, t["hib"], s["hi_in"], s["hi_used"])

        @block.vector
        def _(dve):
            ch = Chain(dve, s["chain"])
            dve.wait_ge(s["weights_in"], 32)
            for k in range(KD):
                ch.mark(nc.vector.tensor_scalar(t["wl"][:, k, :], t["wl"][:, k, :], g["unscale"][:, k:k + 1], XS,
                                                ALU.mult, ALU.mult))
                ch.mark(nc.vector.tensor_scalar(t["wr"][:, k, :], t["wr"][:, k, :], g["unscale"][:, k:k + 1], None,
                                                ALU.mult))
            ch.wait()
            nc.vector.memset(tmp[:, :, :], 0.0).then_inc(s["scaled"], 1)
            dve.wait_ge(s["scaled"], 1)
            dve.wait_ge(s["bias_in"], 16)
            start = ch.n
            per = 1 + NORM_MARKS

            def finish(c):
                ch.base, ch.n = start + c * per, 0
                dve.wait_ge(s["rows_in"], 16 * (c + 1))
                ch.done(nc.vector.tensor_tensor(xr[:, :, :], xr[:, :, :], bias[:, :].unsqueeze(1).broadcast_to([P, CT, D]),
                                                ALU.add))
                for n in range(BT):
                    dve.wait_ge(s["tile_done"], BT * c + n + 1)
                    tiles, bank = in_bank(t["bank"], n)
                    nc.vector.tensor_tensor(xr[:, tiles, :], bank, xr[:, tiles, :], ALU.add).then_inc(s["sum_done"], 1)
                dve.wait_ge(s["sum_done"], BT * (c + 1))
                norm_stats(nc, ch, xr, st, mv, s["var_ready"], s["root_done"], c + 1, rstd, tmp)
                assert ch.n == per, ch.n
                dve.wait_ge(s["x_out"], 16 * (c + 1))
                for n in range(CT):
                    nc.vector.tensor_scalar(xr[:, n, :], xr[:, n, :], mv[:, n, 0:1], rstd[:, n:n + 1],
                                            ALU.subtract, ALU.mult).then_inc(s["norm_done"], 1)

            def take_scores(c):
                dve.wait_ge(s["scored"], c + 1)
                nc.vector.tensor_tensor(g["scores"][:, ds(c * CT, CT), 0:E],
                                        t["bank"][3][:, 0:CT * E].rearrange("p (t e) -> p t e", e=E),
                                        bg[:, :].unsqueeze(1).broadcast_to([P, CT, E]), ALU.add).then_inc(s["score_done"], 1)

            dve.wait_ge(s["gate_in"], 32)
            mean_half(nc, dve, t, s, 0, 0)
            mean_half(nc, dve, t, s, 0, 1)
            with dve.Fori(1, CHUNKS) as c:
                mean_half(nc, dve, t, s, c, 0)
                finish(c - 1)
                mean_half(nc, dve, t, s, c, 1)
                take_scores(c - 1)
            finish(CHUNKS - 1)
            take_scores(CHUNKS - 1)

        @block.scalar
        def _(act):
            with act.Fori(0, CHUNKS) as c:
                act.wait_ge(s["sum_done"], BT * (c + 1))
                act.dma_start(chunk_of(rows_to, c), xr[:, :, :]).then_inc(s["x_out"], 16)
                root(nc, act, tmp, s["var_ready"], s["root_done"], c + 1)
                if keep_norm:
                    act.wait_ge(s["norm_done"], CT * (c + 1))
                    act.dma_start(chunk_of(g["norm"], c), xr[:, :, :]).then_inc(s["norm_out"], 16)
                act.wait_ge(s["turned"], c + 1)
                evacuate_transposed(nc, t["bank"], t["own"]).then_inc(s["xt_ready"], 1)
                act.wait_ge(s["xt_ready"], c + 1)
                act.dma_start(g["xt"][:, :, ds(c * CH, CH)], t["own"][:, :, :]).then_inc(s["xt_out"], 16)
            act.wait_ge(s["x_out"], 16 * CHUNKS)
            act.wait_ge(s["xt_out"], 16 * CHUNKS)
            if keep_norm:
                act.wait_ge(s["norm_out"], 16 * CHUNKS)

        def dense(pe, c):
            pe.wait_ge(s["scaled"], 1)
            pe.wait_ge(s["mean_done"], 4 * (c + 1))
            pe.wait_ge(s["own_in"], 16 * (c + 1))
            pe.wait_ge(s["xt_ready"], c)
            for n in range(CT):
                at, to = slice(n * P, (n + 1) * P), t["bank"][n // 2][:, n % 2 * D:(n % 2 + 1) * D]
                for k in range(KD):
                    nc.tensor.matmul(to, t["mean"][:, k, at], t["wl"][:, k, :], start=k == 0, stop=False)
                for k in range(KD):
                    ins = nc.tensor.matmul(to, t["own"][:, k, at], t["wr"][:, k, :], start=False, stop=k == KD - 1)
                if n % 2 or n == CT - 1:
                    ins.then_inc(s["tile_done"], 1)
            pe.wait_ge(s["tile_done"], BT * (c + 1))
            pe.sem_inc(s["dense_done"], 1)

        def turn(pe, c):
            pe.wait_ge(s["norm_done"], CT * (c + 1))
            transpose_chunk(nc, pe, t["bank"], xr, g["ident"]).then_inc(s["turned"], 1)

        def score(pe, c):
            pe.wait_ge(s["xt_ready"], c + 1)
            pe.wait_ge(s["score_done"], c)
            pe.wait_ge(s["gate_in"], 32)
            for n in range(CT):
                for k in range(KD):
                    ins = nc.tensor.matmul(t["bank"][3][:, n * E:(n + 1) * E], t["own"][:, k, n * P:(n + 1) * P], wg[:, k, :],
                                           start=k == 0, stop=k == KD - 1)
            ins.then_inc(s["scored"], 1)

        block.tensor(conv_tensor_engine(nc, g, adj, t, s, dense, turn, 18, score))


def first_of_largest(nc, ch, sc, m, eq, rank, mv, one, down, shape):
    bc = lambda ap: ap.unsqueeze(2).broadcast_to(shape)
    ch.done(nc.vector.reduce_max(m, sc, AX.X))
    ch.done(nc.vector.tensor_tensor(eq, sc, bc(m), ALU.is_equal))
    ch.done(nc.vector.tensor_tensor(rank, eq, down.unsqueeze(1).broadcast_to(shape), ALU.mult))
    ch.done(nc.vector.reduce_max(mv, rank, AX.X))
    ch.done(nc.vector.tensor_tensor(one, rank, bc(mv), ALU.is_equal))


def route(nc, io, g):
    with ExitStack() as ctx:
        pr = Prog(nc, ctx, "r_")
        rows = pr.sb("rows", [P, TILES, D], F32)
        S3 = [P, TILES, E0]
        f = {n: pr.sb(n, S3, F32) for n in ("sc", "eq", "rank", "o1", "o2", "sl")}
        f2 = {n: pr.sb(n, [P, TILES], F32) for n in ("m", "mv", "pick")}
        mask = pr.sb("mask", S3, F16)
        pre = pr.sb("pre", [P, TILES + 1, E0], F32)
        ones = pr.sb("ones", [P, TILES], F32)
        down_i = pr.sb("down_i", [P, E0], I32)
        down = pr.sb("down", [P, E0], F32)
        tri32 = pr.sb("tri32", [P, P], F32)
        tri = pr.sb("tri", [P, P], F16)
        all1 = pr.sb("all1", [P, P], F16)
        cnt_i = pr.sb("cnt_i", [P, 2, E0], I32)
        cnt = pr.sb("cnt", [P, 5, E0], F32)
        ps_rank = pr.ps("ps_rank", S3)
        ps_tot = pr.ps("ps_tot", S3)
        s = {n: pr.sem(n) for n in ("rows_in", "iotas", "chain", "mask_ready",
                                    "ranked", "idx_ready", "scattered", "const")}
        block = ctx.enter_context(nc.Block())

        @block.sync
        def _(sp):
            sp.dma_start(rows[:, :, :], g["norm"].rearrange("(t p) d -> p t d", p=P)).then_inc(s["rows_in"], 16)

        @block.tensor
        def _(pe):
            pe.wait_ge(s["mask_ready"], 1)
            nc.tensor.matmul(ps_rank[:, :, :], tri[:, :], mask[:, :, :], start=True, stop=True)
            nc.tensor.matmul(ps_tot[:, :, :], all1[:, :], mask[:, :, :], start=True, stop=True).then_inc(s["ranked"], 1)

        @block.vector
        def _(dve):
            ch = Chain(dve, s["chain"])
            ch.mark(nc.vector.memset(all1[:, :], 1.0))
            ch.mark(nc.vector.memset(ones[:, :], 1.0))
            ch.mark(nc.vector.memset(pre[:, 0, :], 0.0))
            dve.wait_ge(s["iotas"], 2)
            ch.mark(nc.vector.tensor_copy(down[:, :], down_i[:, :]))
            ch.mark(nc.vector.tensor_copy(tri[:, :], tri32[:, :]))
            ch.done(nc.vector.tensor_copy(f["sc"][:, :, :], g["scores"][:, :, :]))
            a = {n: v[:, :, :] for n, v in f.items()}
            first_of_largest(nc, ch, a["sc"], f2["m"][:, :], a["eq"], a["rank"], f2["mv"][:, :], a["o1"], down[:, :], S3)
            ch.done(nc.vector.scalar_tensor_tensor(a["sc"], a["o1"], -3e38, a["sc"], ALU.mult, ALU.add))
            first_of_largest(nc, ch, a["sc"], f2["m"][:, :], a["eq"], a["rank"], f2["mv"][:, :], a["o2"], down[:, :], S3)
            nc.vector.tensor_tensor(mask[:, :, :], a["o1"], a["o2"], ALU.add).then_inc(s["mask_ready"], 1)
            dve.wait_ge(s["ranked"], 1)
            ch.mark(nc.vector.tensor_copy(a["sc"], ps_tot[:, :, :]))
            ch.done(nc.vector.tensor_copy(a["sl"], ps_rank[:, :, :]))
            for e in range(E0):
                ch.mark(nc.vector.tensor_tensor_scan(pre[:, 1:TILES + 1, e], ones[:, :], f["sc"][:, :, e], 0.0,
                                                     ALU.mult, ALU.add))
            ch.wait()
            ch.done(nc.vector.tensor_scalar(cnt[:, 0, :], pre[:, TILES, :], 1.0, float(ST - 1), ALU.max, ALU.add))
            ch.done(nc.vector.tensor_copy(cnt_i[:, 0, :], cnt[:, 0, :]))
            ch.done(nc.vector.tensor_scalar(cnt_i[:, 1, :], cnt_i[:, 0, :], ST.bit_length() - 1, None, ALU.logical_shift_right))
            ch.done(nc.vector.tensor_copy(cnt[:, 1, :], cnt_i[:, 1, :]))
            ch.done(nc.vector.tensor_tensor_scan(cnt[:, 2, :], ones[:, 0:E0], cnt[:, 1, :], 0.0, ALU.mult, ALU.add))
            ch.done(nc.vector.tensor_tensor(cnt[:, 3, :], cnt[:, 2, :], cnt[:, 1, :], ALU.subtract))
            ch.mark(nc.vector.tensor_scalar(cnt[:, 4, :], cnt[:, 3, :], float(ST), None, ALU.mult))
            ch.done(nc.vector.tensor_tensor(a["sl"], a["sl"], pre[:, 0:TILES, :], ALU.add))
            ch.done(nc.vector.tensor_tensor(a["sl"], a["sl"], cnt[:, 4, :].unsqueeze(1).broadcast_to(S3), ALU.add))
            for n, one in ((0, "o1"), (1, "o2")):
                ch.done(nc.vector.tensor_tensor(a["eq"], a[one], a["sl"], ALU.mult))
                ch.done(nc.vector.reduce_sum(f2["pick"][:, :], a["eq"], AX.X))
                ins = nc.vector.tensor_copy(g["slot"][:, n, :], f2["pick"][:, :])
                ch.done(ins)
            nc.vector.memset(f2["m"][:, :], 0.0).then_inc(s["idx_ready"], 1)
            ch.mark(nc.vector.tensor_copy(g["tiles"][:, 0, :], cnt[:, 1, :]))
            ch.mark(nc.vector.tensor_copy(g["tiles"][:, 1, :], cnt[:, 3, :]))
            ch.done(nc.vector.tensor_copy(g["tiles"][:, 2, 0:1], cnt[:, 2, E0 - 1:E0]))

        @block.gpsimd
        def _(pool):
            nc.gpsimd.iota(down_i[:, :], pattern=[[-1, E0]], base=E0, channel_multiplier=0).then_inc(s["iotas"], 1)
            nc.gpsimd.memset(tri32[:, :], 1.0).then_inc(s["const"], 1)
            pool.wait_ge(s["const"], 1)
            nc.gpsimd.affine_select(out=tri32[:, :], in_=tri32[:, :], compare_op=ALU.is_gt, fill=0.0, base=0,
                                    pattern=[[1, P]], channel_multiplier=-1).then_inc(s["iotas"], 1)
            pool.wait_ge(s["rows_in"], 16)
            pool.wait_ge(s["idx_ready"], 1)
            for n in range(2):
                for t in range(TILES):
                    pool.indirect_dma_start(out=g["slots_in"], in_=rows[:, t, :], in_offset=None,
                                            out_offset=bass.IndirectOffsetOnAxis(ap=g["slot"][:, n, t:t + 1], axis=0)
                                            ).then_inc(s["scattered"], 16)
            pool.wait_ge(s["scattered"], 16 * 2 * TILES)


def experts(nc, io, g):
    with ExitStack() as ctx:
        pr = Prog(nc, ctx, "e_")
        NT = ST // P
        w1 = pr.sb("w1", [P, 2, KD, H0], F32)
        w2 = pr.sb("w2", [P, 2, HB, D], F32)
        b1 = pr.sb("b1", [P, 2, HB], F32)
        b2 = pr.sb("b2", [P, 2, D], F32)
        xr = pr.sb("xr", [P, NT, D], F32)
        xt = pr.sb("xt", [P, KD, ST], F32)
        h = pr.sb("h", [P, HB, ST], F32)
        y = pr.sb("y", [P, NT, D], F32)
        px = pr.ps("px", [P, KD, ST])
        ph = [pr.ps(f"ph{n}", [P, ST]) for n in range(HB)]
        py = pr.ps("py", [P, NT, D])
        s = {n: pr.sem(n) for n in ("w_in0", "w_in1", "w_free0", "w_free1", "rows_in", "turned", "xt_ready", "h_mm",
                                    "h_done", "y_mm", "y_done", "y_out")}
        LOADS = 4 * 16
        block = ctx.enter_context(nc.Block())
        total_on = lambda eng: eng.value_load(g["tiles"][0:1, 2, 0:1], min_val=E0, max_val=STMAX)

        def tiles_on(eng, e):
            return (eng.value_load(g["tiles"][0:1, 0, ds(e, 1)], min_val=1, max_val=STMAX),
                    eng.value_load(g["tiles"][0:1, 1, ds(e, 1)], min_val=0, max_val=STMAX))

        @block.sync
        def _(sp):
            total = total_on(sp)
            tile_of = lambda ap, j: ap.rearrange("(t p) d -> p t d", p=P)[:, ds(j * NT, NT), :]

            def load(j):
                sp.wait_ge(s["turned"], j)
                sp.dma_start(xr[:, :, :], tile_of(g["slots_in"], j)).then_inc(s["rows_in"], 16)

            def store(j, count):
                sp.wait_ge(s["y_done"], count)
                sp.dma_start(tile_of(g["slots_out"], j), y[:, :, :]).then_inc(s["y_out"], 16)

            load(0)
            load(1)
            with sp.Fori(2, total) as j:
                load(j)
                store(sp.snap(j - 2), j)
            store(total - 2, total)
            store(total - 1, total + 1)

        @block.tensor
        def _(pe):
            def turn(j):
                pe.wait_ge(s["rows_in"], 16 * (j + 1))
                for k in range(KD):
                    for t in range(NT):
                        ins = nc.tensor.transpose(px[:, k, t * P:(t + 1) * P], xr[:, t, k * P:(k + 1) * P], g["ident"][:, :])
                ins.then_inc(s["turned"], 1)

            def first_product(j, u):
                pe.wait_ge(s["xt_ready"], j + 1)
                for n in range(HB):
                    for k in range(KD):
                        ins = nc.tensor.matmul(ph[n][:, :], w1[:, u, k, n * P:(n + 1) * P], xt[:, k, :],
                                               start=k == 0, stop=k == KD - 1)
                    ins.then_inc(s["h_mm"], 1)

            def second_product(before, u):
                pe.wait_ge(s["h_done"], HB * before)
                pe.wait_ge(s["y_done"], before)
                for t in range(NT):
                    for n in range(HB):
                        ins = nc.tensor.matmul(py[:, t, :], h[:, n, t * P:(t + 1) * P], w2[:, u, n, :],
                                               start=n == 0, stop=n == HB - 1)
                ins.then_inc(s["y_mm"], 1)

            def expert(e, u, uses):
                tiles, at = tiles_on(pe, e)
                if not isinstance(e, int) or e > 0:
                    turn(at)
                    second_product(at, 1 - u)
                else:
                    at = 0
                    turn(at)
                pe.wait_ge(s[f"w_in{u}"], LOADS * (uses + 1))
                first_product(at, u)
                with pe.Fori(1, tiles) as i:
                    j = pe.snap(at + i)
                    turn(j)
                    second_product(j, u)
                    first_product(j, u)

            expert(0, 0, 0)
            with pe.Fori(0, E0 // 2 - 1) as k:
                expert(k * 2 + 1, 1, k)
                expert(k * 2 + 2, 0, k + 1)
            expert(E0 - 1, 1, E0 // 2 - 1)
            total = total_on(pe)
            second_product(total, 1)

        @block.scalar
        def _(act):
            def expert(e, u):
                tiles, at = tiles_on(act, e)
                with act.Fori(0, tiles) as i:
                    j = act.snap(at + i)
                    act.wait_ge(s["turned"], j + 1)
                    nc.scalar.activation(xt[:, :, :], px[:, :, :], ACT.Identity).then_inc(s["xt_ready"], 1)
                    for n in range(HB):
                        act.wait_ge(s["h_mm"], HB * j + n + 1)
                        nc.scalar.activation(h[:, n, :], ph[n][:, :], ACT.Gelu, bias=b1[:, u, n:n + 1]
                                             ).then_inc(s["h_done"], 1)

            with act.Fori(0, E0 // 2) as k:
                expert(k * 2, 0)
                expert(k * 2 + 1, 1)

        @block.vector
        def _(dve):
            def expert(e, u):
                tiles, at = tiles_on(dve, e)
                with dve.Fori(0, tiles) as i:
                    j = dve.snap(at + i)
                    dve.wait_ge(s["y_out"], 16 * j)
                    dve.wait_ge(s["y_mm"], j + 1)
                    nc.vector.tensor_tensor(y[:, :, :], py[:, :, :], b2[:, u, :].unsqueeze(1).broadcast_to([P, NT, D]),
                                            ALU.add).then_inc(s["y_done"], 1)
                dve.wait_ge(s["y_done"], at + tiles + 1)
                dve.sem_inc(s[f"w_free{u}"], 1)

            dve.sem_inc(s["y_done"], 1)
            with dve.Fori(0, E0 // 2) as k:
                expert(k * 2, 0)
                expert(k * 2 + 1, 1)

        @block.gpsimd
        def _(pool):
            def load(e, u, uses):
                pool.wait_ge(s[f"w_free{u}"], uses)
                for to, fr in ((w1[:, u, :, :], io["L0_ffn_W1"].rearrange("e (k p) h -> p (e k) h", p=P)[:, ds(e * KD, KD), :]),
                               (w2[:, u, :, :], io["L0_ffn_W2"].rearrange("e (k p) d -> p (e k) d", p=P)[:, ds(e * HB, HB), :]),
                               (b1[:, u, :], io["L0_ffn_b1"].rearrange("e (k p) -> p (e k)", p=P)[:, ds(e * HB, HB)]),
                               (b2[:, u, :], io["L0_ffn_b2"][ds(e, 1), :].broadcast_to([P, D]))):
                    pool.dma_start(to, fr, allow_slow_non_contiguous=True).then_inc(s[f"w_in{u}"], 16)

            with pool.Fori(0, E0 // 2) as k:
                load(k * 2, 0, k)
                load(k * 2 + 1, 1, k)
            pool.wait_ge(s["y_out"], 16 * total_on(pool))


def last_experts(nc, io, g, rows_from, out):
    with ExitStack() as ctx:
        pr = Prog(nc, ctx, "m_")
        F = "L1_ffn_"
        sw1 = pr.sb("sw1", [P, KD, SH1], F32)
        sw2 = pr.sb("sw2", [P, SH1 // P, SH2], F32)
        sw3 = pr.sb("sw3", [P, D], F32)
        ew1 = pr.sb("ew1", [P, KD, E1, EH1], F32)
        ew2 = pr.sb("ew2", [P, E1, EH2], F32)
        ew3 = pr.sb("ew3", [EH2 + 1, E1, D], F32)
        sb1 = pr.sb("sb1", [P, SH1 // P], F32)
        sb2 = pr.sb("sb2", [P, 1], F32)
        sb3 = pr.sb("sb3", [P, D], F32)
        eb1 = pr.sb("eb1", [P, E1], F32)
        eb2 = pr.sb("eb2", [EH2, E1], F32)
        xt = pr.sb("xt", [P, KD, ROWS], F32)
        h1 = pr.sb("h1", [P, SH1 // P, CH], F32)
        h2 = pr.sb("h2", [P, CH], F32)
        eh1 = pr.sb("eh1", [P, 2, CH], F32)
        eh2 = pr.sb("eh2", [EH2 + 1, 2, CH], F32)
        acc = pr.sb("acc", [P, TILES, D], F32)
        weight = pr.sb("weight", [P, CT, E1], F32)
        down_i = pr.sb("down_i", [P, E1], I32)
        down = pr.sb("down", [P, E1], F32)
        S3 = [P, TILES, E1]
        f = {n: pr.sb(n, S3, F32) for n in ("sc", "d", "ex", "gate", "eq", "rank", "o1", "o2", "w1", "w2", "wt")}
        f2 = {n: pr.sb(n, [P, TILES], F32) for n in ("mx", "sm", "rs", "m1", "m2", "mv", "dd", "t", "t1", "r2", "v2")}
        bank = [pr.ps(f"bank{i}", [P, 512]) for i in range(7)]
        s = {n: pr.sem(n) for n in ("w_in", "xt_in", "acc_in", "down_ready", "chain", "exp_in1", "exp_in2",
                                    "exp1", "exp2", "mm", "act_took", "dve_took", "ready", "out_done")}
        block = ctx.enter_context(nc.Block())
        NB = len(bank)
        LOADS = 13
        ORDER = ["S1", "E1.0", "S2", "E2.0", "E1.1", "S3", "E3.0", "E2.1", "E1.2", "E3.1", "E2.2", "E1.3", "E3.2",
                 "E2.3", "E3.3"]
        GROUPS = {"S1": 4, "S2": 2, "S3": BT, "E1": 2, "E2": 2, "E3": BT}
        first, n = {}, 0
        for name in ORDER:
            first[name] = n
            n += GROUPS[name[:2]]
        TOTAL = n
        by_dve = [x[:2] in ("S3", "E3") for x in ORDER for _ in range(GROUPS[x[:2]])]
        taken = [sum(1 for b in by_dve[:i + 1] if b == by_dve[i]) for i in range(TOTAL)]
        ACT_N, DVE_N = by_dve.count(False), by_dve.count(True)

        def group_taken(eng, c, i):
            if by_dve[i]:
                eng.wait_ge(s["dve_took"], (c + 1) * DVE_N + taken[i])
            else:
                eng.wait_ge(s["act_took"], (c + 1) * ACT_N + taken[i])

        @block.sync
        def _(sp):
            for c in range(CHUNKS):
                if c:
                    sp.wait_ge(s["xt_in"], 16 * c)
                    sp.wait_ge(s["acc_in"], 16 * c)
                sp.dma_start(xt[:, :, c * CH:(c + 1) * CH], g["xt"][:, :, c * CH:(c + 1) * CH]).then_inc(s["xt_in"], 16)
                sp.dma_start(acc[:, c * CT:(c + 1) * CT, :],
                             rows_from.rearrange("(t p) d -> p t d", p=P)[:, c * CT:(c + 1) * CT, :]).then_inc(s["acc_in"], 16)

        @block.gpsimd
        def _(pool):
            nc.gpsimd.iota(down_i[:, :], pattern=[[-1, E1]], base=E1, channel_multiplier=0).then_inc(s["down_ready"], 1)
            with pool.Fori(0, CHUNKS - 1) as c:
                pool.wait_ge(s["dve_took"], DVE_N * (c + 2))
                pool.dma_start(out[ds(c * CH, CH), :].rearrange("(t p) d -> p t d", p=P), acc[:, ds(c * CT, CT), :]).then_inc(s["out_done"], 16)
            pool.wait_ge(s["dve_took"], DVE_N * (CHUNKS + 1))
            at = (CHUNKS - 1) * CH
            full = (NODES - at) // P
            pool.dma_start(out[at:at + full * P, :].rearrange("(t p) d -> p t d", p=P), acc[:, TILES - CT:TILES - CT + full, :]).then_inc(s["out_done"], 16)
            rest = NODES - at - full * P
            pool.dma_start(out[NODES - rest:NODES, :], acc[0:rest, TILES - CT + full, :]).then_inc(s["out_done"], 16)
            pool.wait_ge(s["out_done"], 16 * (CHUNKS + 1))

        @block.tensor
        def _(pe):
            pe.wait_ge(s["w_in"], 16 * LOADS)
            pe.wait_ge(s["ready"], 1)
            with pe.Fori(0, CHUNKS) as c:
                pe.wait_ge(s["xt_in"], 16 * (c + 1))
                for name in ORDER:
                    kind, e = name[:2], int(name[3:] or 0)
                    need = {"S2": "S1", "S3": "S2", "E2": f"E1.{e}", "E3": f"E2.{e}"}.get(kind)
                    if need:
                        group_taken(pe, c, first[need] + GROUPS[need[:2]] - 1)
                    for n in range(GROUPS[kind]):
                        i = first[name] + n
                        if i >= NB:
                            group_taken(pe, c, i - NB)
                        else:
                            group_taken(pe, c - 1, max(j for j in range(TOTAL) if j % NB == i))
                        b = bank[i % NB]
                        half = slice((n if kind != "S1" else n // 2) * SUB, ((n if kind != "S1" else n // 2) + 1) * SUB)
                        if kind == "S1":
                            for k in range(KD):
                                ins = nc.tensor.matmul(b[:, 0:SUB], sw1[:, k, n % 2 * P:(n % 2 + 1) * P], xt[:, k, ds(c * CH + half.start, SUB)],
                                                       start=k == 0, stop=k == KD - 1)
                        elif kind == "E1":
                            for k in range(KD):
                                ins = nc.tensor.matmul(b[:, 0:SUB], ew1[:, k, e, :], xt[:, k, ds(c * CH + half.start, SUB)], start=k == 0, stop=k == KD - 1)
                        elif kind == "S2":
                            for k in range(SH1 // P):
                                ins = nc.tensor.matmul(b[:, 0:SUB], sw2[:, k, :], h1[:, k, half], start=k == 0, stop=k == SH1 // P - 1)
                        elif kind == "E2":
                            ins = nc.tensor.matmul(b[0:EH2, 0:SUB], ew2[:, e, :], eh1[:, e % 2, half], start=True, stop=True)
                        else:
                            for t in range(2 * n, min(2 * n + 2, CT)):
                                to = b[:, t % 2 * D:(t % 2 + 1) * D]
                                if kind == "S3":
                                    ins = nc.tensor.matmul(to, h2[:, t * P:(t + 1) * P], sw3[:, :], start=True, stop=True)
                                else:
                                    ins = nc.tensor.matmul(to, eh2[:, e % 2, t * P:(t + 1) * P], ew3[:, e, :], start=True, stop=True)
                        ins.then_inc(s["mm"], 1)

        @block.scalar
        def _(act):
            loads = [
                (sw1[:, :, :], io[F + "sW1"].rearrange("(k p) n -> p k n", p=P)),
                (sw2[:, :, :], io[F + "sW2"].rearrange("(k p) n -> p k n", p=P)),
                (sw3[:, :], io[F + "sW3"]),
                (sb1[:, :], io[F + "sb1"].rearrange("(k p) -> p k", p=P)),
                (sb2[:, :], io[F + "sb2"].rearrange("(p a) -> p a", a=1)),
                (sb3[:, :], io[F + "sb3"].rearrange("(a n) -> a n", a=1).broadcast_to([P, D])),
                (eb1[:, :], io[F + "eb1"].rearrange("e p -> p e")),
                (eb2[:, :], io[F + "eb2"].rearrange("e p -> p e")),
                (ew3[EH2:EH2 + 1, :, :], io[F + "eb3"].rearrange("(a e) n -> a e n", a=1)),
                (ew2[:, :, :], io[F + "eW2"].rearrange("e p n -> p e n")),
                (ew3[0:EH2, :, :], io[F + "eW3"].rearrange("e p n -> p e n")),
            ] + [(ew1[:, k, :, :], io[F + "eW1"][:, k * P:(k + 1) * P, :].rearrange("e p n -> p e n")) for k in range(KD)]
            assert len(loads) == LOADS
            for to, fr in loads:
                act.dma_start(to, fr, allow_slow_non_contiguous=True).then_inc(s["w_in"], 16)
            act.sem_inc(s["act_took"], ACT_N)
            act.wait_ge(s["exp_in1"], 1)
            nc.scalar.activation(f["ex"][:, :, :], f["d"][:, :, :], ACT.Exp).then_inc(s["exp1"], 1)
            act.wait_ge(s["exp_in2"], 1)
            nc.scalar.activation(f2["t"][:, :], f2["dd"][:, :], ACT.Exp).then_inc(s["exp2"], 1)
            act.wait_ge(s["w_in"], 16 * LOADS)
            with act.Fori(0, CHUNKS) as c:
                for name in ORDER:
                    kind, e = name[:2], int(name[3:] or 0)
                    if kind in ("S3", "E3"):
                        continue
                    for n in range(GROUPS[kind]):
                        i = first[name] + n
                        b = bank[i % NB]
                        half = slice((n if kind != "S1" else n // 2) * SUB, ((n if kind != "S1" else n // 2) + 1) * SUB)
                        act.wait_ge(s["mm"], c * TOTAL + i + 1)
                        if kind == "S1":
                            to, fr, bias = h1[:, n % 2, half], b[:, 0:SUB], sb1[:, n % 2:n % 2 + 1]
                        elif kind == "E1":
                            to, fr, bias = eh1[:, e % 2, half], b[:, 0:SUB], eb1[:, e:e + 1]
                        elif kind == "S2":
                            to, fr, bias = h2[:, half], b[:, 0:SUB], sb2[:, 0:1]
                        else:
                            to, fr, bias = eh2[0:EH2, e % 2, half], b[0:EH2, 0:SUB], eb2[:, e:e + 1]
                        nc.scalar.activation(to, fr, ACT.Relu, bias=bias).then_inc(s["act_took"], 1)

        @block.vector
        def _(dve):
            ch = Chain(dve, s["chain"])
            dve.sem_inc(s["dve_took"], DVE_N)
            dve.wait_ge(s["down_ready"], 1)
            ch.mark(nc.vector.tensor_copy(down[:, :], down_i[:, :]))
            ch.done(nc.vector.memset(eh2[EH2:EH2 + 1, :, :], 1.0))
            nc.vector.memset(f2["sm"][:, :], 1.0).then_inc(s["ready"], 1)
            dve.wait_ge(s["ready"], 1)
            a = {n: v[:, :, :] for n, v in f.items()}
            a2 = {n: v[:, :] for n, v in f2.items()}
            bc = lambda ap: ap.unsqueeze(2).broadcast_to(S3)
            ch.done(nc.vector.tensor_copy(a["sc"], g["scores"][:, :, 0:E1]))
            ch.done(nc.vector.reduce_max(a2["mx"], a["sc"], AX.X))
            nc.vector.tensor_tensor(a["d"], a["sc"], bc(a2["mx"]), ALU.subtract).then_inc(s["exp_in1"], 1)
            dve.wait_ge(s["exp1"], 1)
            ch.done(nc.vector.reduce_sum(a2["sm"], a["ex"], AX.X))
            ch.done(nc.vector.reciprocal(a2["rs"], a2["sm"]))
            ch.done(nc.vector.tensor_tensor(a["gate"], a["ex"], bc(a2["rs"]), ALU.mult))
            first_of_largest(nc, ch, a["gate"], a2["m1"], a["eq"], a["rank"], a2["mv"], a["o1"], down[:, :], S3)
            ch.done(nc.vector.scalar_tensor_tensor(a["gate"], a["o1"], -2.0, a["gate"], ALU.mult, ALU.add))
            first_of_largest(nc, ch, a["gate"], a2["m2"], a["eq"], a["rank"], a2["mv"], a["o2"], down[:, :], S3)
            nc.vector.tensor_tensor(a2["dd"], a2["m2"], a2["m1"], ALU.subtract).then_inc(s["exp_in2"], 1)
            dve.wait_ge(s["exp2"], 1)
            ch.done(nc.vector.tensor_scalar(a2["t1"], a2["t"], 1.0, None, ALU.add))
            ch.done(nc.vector.reciprocal(a2["r2"], a2["t1"]))
            ch.mark(nc.vector.tensor_tensor(a2["v2"], a2["t"], a2["r2"], ALU.mult))
            ch.done(nc.vector.tensor_tensor(a["w1"], a["o1"], bc(a2["r2"]), ALU.mult))
            ch.done(nc.vector.tensor_tensor(a["w2"], a["o2"], bc(a2["v2"]), ALU.mult))
            ch.done(nc.vector.tensor_tensor(a["wt"], a["w1"], a["w2"], ALU.add))
            dve.wait_ge(s["w_in"], 16 * LOADS)
            with ch.loop(0, CHUNKS, 2) as c:
                dve.wait_ge(s["acc_in"], 16 * (c + 1))
                dve.wait_ge(s["dve_took"], DVE_N * (c + 1))
                ch.mark(nc.vector.tensor_copy(weight[:, :, :], f["wt"][:, ds(c * CT, CT), :]))
                rows = acc[:, ds(c * CT, CT), :]
                ch.done(nc.vector.tensor_tensor(rows, rows, sb3[:, :].unsqueeze(1).broadcast_to([P, CT, D]), ALU.add))
                for name in ORDER:
                    kind, e = name[:2], int(name[3:] or 0)
                    if kind not in ("S3", "E3"):
                        continue
                    for n in range(GROUPS[kind]):
                        i = first[name] + n
                        dve.wait_ge(s["mm"], c * TOTAL + i + 1)
                        tiles, b = in_bank([bank[i % NB]] * BT, n)
                        if kind == "S3":
                            rows = acc[:, ds(c * CT + tiles.start, tiles.stop - tiles.start), :]
                            ins = nc.vector.tensor_tensor(rows, b, rows, ALU.add)
                        else:
                            dve.wait_ge(s["dve_took"], (c + 1) * DVE_N + taken[i] - BT)
                            for t in range(tiles.start, tiles.stop):
                                row = acc[:, ds(c * CT + t, 1), :].rearrange("p a d -> p (a d)")
                                ins = nc.vector.scalar_tensor_tensor(row, b[:, t - tiles.start, :], weight[:, t, e:e + 1],
                                                                     row, ALU.mult, ALU.add)
                        ins.then_inc(s["dve_took"], 1)


def program(nc, io, out):
    dram = lambda name, shape, dt: nc.dram_tensor(name, shape, dt).ap()
    g = {
        "parts": dram("parts", (P, TILES * 2 * D), F16),
        "xt": dram("xt", (P, KD, ROWS), F32),
        "ht": dram("ht", (P, KD, ROWS), F32),
        "slots_in": dram("slots_in", (SLOTS, D), F32),
        "slots_out": dram("slots_out", (SLOTS, D), F32),
        "norm": dram("norm", (ROWS, D), F32),
        "x1": dram("x1", (ROWS, D), F32),
        "x2": dram("x2", (ROWS, D), F32),
        "x3": dram("x3", (ROWS, D), F32),
        "upper": dram("upper", (ROWS, ROWS), F16),
        "degree": dram("degree", (1, ROWS), F32),
        "inv": dram("inv", (1, ROWS), F32),
        "keys": dram("keys", (2, P, WINS * VIS, 2), F16),
    }
    with ExitStack() as ctx:
        pr = Prog(nc, ctx)
        g["ident"] = pr.sb("ident", [P, P], F32)
        g["flag"] = pr.sb("flag", [1, 1], I32)
        g["scale"] = pr.sb("scale", [P, KD], F32)
        g["unscale"] = pr.sb("unscale", [P, KD], F32)
        g["slot"] = pr.sb("slot", [P, 2, TILES], I32)
        g["tiles"] = pr.sb("tiles", [P, 3, E0], I32)
        g["scores"] = pr.sb("scores", [P, TILES, E0], F32)
        first_block(nc, io, g)
        held = ctx.enter_context(ExitStack())
        adj = held.enter_context(nc.sbuf_tensor("adj", [P, TILES, ROWS], F16))
        build_counts(nc, io, g, adj)
        with nc.sbuf_tensor("l0_parts", [P, TILES, 2, D], F16) as parts:
            first_conv(nc, io, g, adj, parts, "l0a_", ("L0_gnn_W1l", "L0_gnn_b1", "L0_gnn_W1r"))
            second_conv(nc, io, g, adj, parts, "l0b_", ("L0_gnn_W2l", "L0_gnn_b2", "L0_gnn_W2r"),
                        ("L0_ffn_Wg", "L0_ffn_bg"), io["x"], g["x1"], True)
        route(nc, io, g)
        experts(nc, io, g)
        normalise_sum(nc, g)
        with nc.sbuf_tensor("l1_parts", [P, TILES, 2, D], F16) as parts:
            first_conv(nc, io, g, adj, parts, "l1a_", ("L1_gnn_w1_l", "L1_gnn_b1", "L1_gnn_w1_r"))
            second_conv(nc, io, g, adj, parts, "l1b_", ("L1_gnn_w2_l", "L1_gnn_b2", "L1_gnn_w2_r"),
                        ("L1_ffn_gW", "L1_ffn_gb"), g["x2"], g["x3"], False)
        held.close()
        last_experts(nc, io, g, g["x3"], out)


GNN_WEIGHTS = ("L0_gnn_W1l", "L0_gnn_W1r", "L0_gnn_W2l", "L0_gnn_W2r",
               "L1_gnn_w1_l", "L1_gnn_w1_r", "L1_gnn_w2_l", "L1_gnn_w2_r")


def layout(inputs):
    import numpy as np

    def padded(a, rows, value):
        return np.concatenate([a, np.full((rows - a.shape[0],) + a.shape[1:], value, a.dtype)])

    arrays = {n: np.ascontiguousarray(a) for n, a in inputs.items()}
    arrays["x"] = padded(arrays["x"], ROWS, 0)
    arrays["src"] = padded(arrays["src"], EPAD, 0)
    arrays["dst"] = padded(arrays["dst"], EPAD, FAR)
    for n in GNN_WEIGHTS:
        arrays[n + "_T"] = np.ascontiguousarray(arrays[n].T)
    return arrays


def kernel(**inputs):
    import concourse.bacc as bacc
    from concourse.bass_utils import run_bass_kernel_spmd

    nc = bacc.Bacc("TRN2", target_bir_lowering=False, num_devices=1)
    arrays = layout(inputs)
    io = {n: nc.dram_tensor("in_" + n, a.shape, mybir.dt.from_np(a.dtype), kind="ExternalInput").ap()
          for n, a in arrays.items()}
    out = nc.dram_tensor("out", (NODES, D), F32, kind="ExternalOutput").ap()
    program(nc, io, out)
    r = run_bass_kernel_spmd(nc, [{"in_" + n: a for n, a in arrays.items()}], core_ids=[0])
    return r.results[0]["out"]
```

```python
from contextlib import ExitStack, contextmanager

import concourse.bass as bass
from concourse import mybir

F32, F16, I32 = mybir.dt.float32, mybir.dt.float16, mybir.dt.int32
ALU = mybir.AluOpType
ACT = mybir.ActivationFunctionType
AX = mybir.AxisListType
ds = bass.ds

P = 128
D = 256
KD = D // P
NODES = 3125
TILES = -(-NODES // P)
ROWS = TILES * P
CT = 5
CHUNKS = TILES // CT
CH = CT * P
SUB = CH // 2
EDGES = 103125
ETILES = -(-EDGES // P)
W = 6
VIS = 3
WINS = 528
GW = 3
GROUPS = WINS // GW
UNROLL = 16
SLOT = 2
BODIES = GROUPS // UNROLL
BW = UNROLL * GW * W
WG = -(-WINS // P)
NW = TILES * W
EG = 7
EPAD = (EG * P + 1) * P
SG = 13
SSTEPS = ETILES // SG
FAR = 4096
SPLIT = 2048.0
XS = 1024.0
EPS = 1e-5
E0, H0 = 8, 512
HB = H0 // P
ST = 256
STMAX = (2 * ROWS + E0 * (ST - 1)) // ST
SLOTS = STMAX * ST
CAP = ROWS + ST
E1, SH1, SH2, EH1, EH2 = 4, 256, 128, 128, 64

assert W * WINS >= NODES and SSTEPS * SG == ETILES and CHUNKS * CT == TILES
assert BODIES * UNROLL * GW == WINS and UNROLL % SLOT == 0 and NW % 2 == 0 and STMAX % 2 == 0


class Chain:

    def __init__(self, eng, sem):
        self.eng, self.sem, self.base, self.n = eng, sem, 0, 0

    def mark(self, ins):
        ins.then_inc(self.sem, 1)
        self.n += 1
        return self.base + self.n

    def wait(self):
        self.eng.wait_ge(self.sem, self.base + self.n)

    def done(self, ins):
        self.mark(ins)
        self.wait()

    @contextmanager
    def loop(self, start, end, per):
        before = self.n
        with self.eng.Fori(start, end) as i:
            self.base, self.n = before + (i - start) * per, 0
            yield i
            assert self.n == per, (self.n, per)
        self.base, self.n = 0, before + (end - start) * per


class Prog:

    def __init__(self, nc, ctx, tag=""):
        self.nc, self.ctx, self.tag, self.sems = nc, ctx, tag, []
        ctx.callback(self.clear)

    def clear(self):
        if self.sems:
            self.nc.clear_and_free_semaphores(self.sems)
            self.nc.all_engine_barrier(sem_only=True)

    def sb(self, name, shape, dt):
        return self.ctx.enter_context(self.nc.sbuf_tensor(self.tag + name, shape, dt))

    def ps(self, name, shape, dt=F32):
        return self.ctx.enter_context(self.nc.psum_tensor(self.tag + name, shape, dt))

    def sem(self, name):
        self.sems.append(self.nc.alloc_semaphore(self.tag + name))
        return self.sems[-1]


NORM_MARKS = 2 * CT + 5


def norm_stats(nc, ch, rows, st, mv, var_ready, rstd_from, n, rstd, tmp):
    for t in range(CT):
        ch.mark(nc.vector.bn_stats(st[:, t, :], rows[:, t, :]))
    ch.wait()
    nc.vector.memset(tmp[:, 3, :], 0.0)
    for t in range(CT):
        ch.mark(nc.vector.bn_aggr(mv[:, t, :], st[:, t, :]))
    ch.wait()
    ins = nc.vector.tensor_scalar(tmp[:, 0, :], mv[:, :, 1], EPS, None, ALU.add)
    ins.then_inc(var_ready, 1)
    ch.eng.wait_ge(rstd_from, n)
    ch.done(nc.vector.reciprocal(tmp[:, 1, :], tmp[:, 2, :]))
    ch.done(nc.vector.tensor_tensor(tmp[:, 3, :], tmp[:, 1, :], tmp[:, 1, :], ALU.mult))
    ch.done(nc.vector.tensor_tensor(tmp[:, 4, :], tmp[:, 3, :], tmp[:, 0, :], ALU.mult))
    ch.done(nc.vector.tensor_scalar(tmp[:, 5, :], tmp[:, 4, :], -0.5, 1.5, ALU.mult, ALU.add))
    ch.done(nc.vector.tensor_tensor(rstd[:, :], tmp[:, 1, :], tmp[:, 5, :], ALU.mult))


def norm_apply(nc, ch, out, rows, mv, rstd):
    for t in range(CT):
        ch.mark(nc.vector.tensor_scalar(out[:, t, :], rows[:, t, :], mv[:, t, 0:1], rstd[:, t:t + 1],
                                        ALU.subtract, ALU.mult))


def root(nc, act, tmp, var_ready, root_done, n):
    act.wait_ge(var_ready, n)
    nc.scalar.activation(tmp[:, 2, :], tmp[:, 0, :], ACT.Sqrt).then_inc(root_done, 1)


def transposed_place(bank, f, t):
    return bank[f][:, t * P:(t + 1) * P] if t < CT - 1 else bank[2][:, f * P:(f + 1) * P]


def transpose_chunk(nc, pe, bank, rows, ident):
    for t in range(CT):
        for f in range(KD):
            last = nc.tensor.transpose(transposed_place(bank, f, t), rows[:, t, f * P:(f + 1) * P], ident[:, :])
    return last


def evacuate_transposed(nc, bank, out):
    four = (CT - 1) * P
    nc.scalar.activation(out[:, 0, 0:four], bank[0][:, 0:four], ACT.Copy)
    nc.scalar.activation(out[:, 1, 0:four], bank[1][:, 0:four], ACT.Copy)
    return nc.scalar.activation(out[:, :, four:CH], bank[2][:, 0:2 * P].rearrange("p (f n) -> p f n", f=KD), ACT.Copy)


def over_chunks(eng, body):
    with eng.Fori(0, CHUNKS // 2) as i:
        body(i * 2, 0, i)
        body(i * 2 + 1, 1, i)
    assert CHUNKS % 2 == 1
    body(CHUNKS - 1, 0, CHUNKS // 2)


class Normalise:

    def __init__(self, nc, pr, g, rows_from, rows_to=None, idx=None):
        self.nc, self.g, self.rows_from, self.rows_to, self.idx = nc, g, rows_from, rows_to, idx
        self.xr = pr.sb("rows", [P, 2, CT, D], F32)
        self.xn = pr.sb("norm", [P, CT, D], F32)
        self.part = pr.sb("part", [P, CT, 2, D], F16)
        self.xt = pr.sb("xt", [P, KD, CH], F32)
        self.st = pr.sb("st", [P, CT, 6], F32)
        self.mv = pr.sb("mv", [P, CT, 2], F32)
        self.tmp = pr.sb("tmp", [P, 6, CT], F32)
        self.rstd = pr.sb("rstd", [P, CT], F32)
        if idx is not None:
            self.chosen = pr.sb("chosen", [P, 2, 2, CT, D], F32)
        self.bank = [pr.ps(f"ps{i}", [P, 512]) for i in range(3)]
        self.s = {n: pr.sem(n) for n in ("rows_in0", "rows_in1", "var_ready", "root_done", "norm_done", "rows_free0",
                                         "rows_free1", "high_done", "parts_done", "n_chain", "n_turned", "xt_ready",
                                         "part_out", "xt_out", "gathered0", "gathered1", "summed", "sum_out0",
                                         "sum_out1")}

    def chunk_of(self, ap, c):
        return ap.rearrange("(t p) d -> p t d", p=P)[:, ds(c * CT, CT), :]

    def sync(self, sp):
        s = self.s

        def body(c, u, i):
            at, to = (sp.snap(c * CT), sp.snap(c * (CT * 2 * D))) if not isinstance(c, int) else (c * CT, c * CT * 2 * D)
            rows = self.rows_from.rearrange("(t p) d -> p t d", p=P)[:, ds(at, CT), :]
            if self.idx is not None:
                sp.wait_ge(s[f"sum_out{u}"], 16 * i)
            sp.wait_ge(s[f"rows_free{u}"], i)
            sp.dma_start(self.xr[:, u, :, :], rows).then_inc(s[f"rows_in{u}"], 16)

        over_chunks(sp, body)

    def vector(self, dve):
        nc, s, part, xn = self.nc, self.s, self.part, self.xn
        ch = Chain(dve, s["n_chain"])
        per = NORM_MARKS + CT + (2 if self.idx is not None else 0)

        def body(c, u, i):
            xr = self.xr[:, u, :, :]
            ch.base, ch.n = c * per, 0
            dve.wait_ge(s[f"rows_in{u}"], 16 * (i + 1))
            if self.idx is not None:
                dve.wait_ge(s[f"gathered{u}"], 16 * 2 * CT * (i + 1))
                for n in range(2):
                    ch.done(nc.vector.tensor_tensor(xr, xr, self.chosen[:, u, n, :, :], ALU.add))
                dve.sem_inc(s["summed"], 1)
            norm_stats(nc, ch, xr, self.st, self.mv, s["var_ready"], s["root_done"], c + 1, self.rstd, self.tmp)
            dve.wait_ge(s["n_turned"], c)
            norm_apply(nc, ch, xn, xr, self.mv, self.rstd)
            ch.wait()
            dve.sem_inc(s["norm_done"], 1)
            assert ch.n == per, ch.n
            dve.wait_ge(s["part_out"], 16 * c)
            nc.vector.tensor_scalar(part[:, :, 0, :], xn[:, :, :], XS, None, ALU.mult).then_inc(s["high_done"], 1)
            dve.wait_ge(s["high_done"], c + 1)
            nc.vector.scalar_tensor_tensor(part[:, :, 1, :], xn[:, :, :], XS, part[:, :, 0, :],
                                           ALU.mult, ALU.subtract).then_inc(s["parts_done"], 1)

        over_chunks(dve, body)

    def scalar(self, act):
        nc, s = self.nc, self.s

        def body(c, u, i):
            if self.idx is not None:
                act.wait_ge(s["summed"], c + 1)
                act.dma_start(self.chunk_of(self.rows_to, c), self.xr[:, u, :, :]).then_inc(s[f"sum_out{u}"], 16)
            root(nc, act, self.tmp, s["var_ready"], s["root_done"], c + 1)
            act.wait_ge(s["norm_done"], c + 1)
            act.sem_inc(s[f"rows_free{u}"], 1)
            act.wait_ge(s["n_turned"], c + 1)
            act.wait_ge(s["xt_out"], 16 * c)
            evacuate_transposed(nc, self.bank, self.xt).then_inc(s["xt_ready"], 1)
            act.wait_ge(s["xt_ready"], c + 1)
            act.dma_start(self.g["xt"][:, :, ds(c * CH, CH)], self.xt[:, :, :]).then_inc(s["xt_out"], 16)
            act.wait_ge(s["parts_done"], c + 1)
            act.dma_start(self.g["parts"][:, ds(c * (CT * 2 * D), CT * 2 * D)],
                          self.part[:, :, :, :].rearrange("p t a d -> p (t a d)")).then_inc(s["part_out"], 16)

        over_chunks(act, body)
        act.wait_ge(s["part_out"], 16 * CHUNKS)
        act.wait_ge(s["xt_out"], 16 * CHUNKS)
        if self.idx is not None:
            act.wait_ge(s["sum_out0"], 16 * (CHUNKS // 2 + 1))
            act.wait_ge(s["sum_out1"], 16 * (CHUNKS // 2))

    def tensor(self, pe):
        s = self.s

        def body(c, u, i):
            pe.wait_ge(s["norm_done"], c + 1)
            pe.wait_ge(s["xt_ready"], c)
            transpose_chunk(self.nc, pe, self.bank, self.xn, self.g["ident"]).then_inc(s["n_turned"], 1)

        over_chunks(pe, body)

    def gpsimd(self, pool):
        for c in range(CHUNKS):
            if c >= 2:
                pool.wait_ge(self.s["summed"], c - 1)
            for n in range(2):
                for t in range(CT):
                    at = c * CT + t
                    pool.indirect_dma_start(out=self.chosen[:, c % 2, n, t, :], out_offset=None, in_=self.g["slots_out"],
                                            in_offset=bass.IndirectOffsetOnAxis(ap=self.idx[:, n, at:at + 1], axis=0)
                                            ).then_inc(self.s[f"gathered{c % 2}"], 16)


def normalise_sum(nc, g):
    with ExitStack() as ctx:
        pr = Prog(nc, ctx, "n2_")
        norm = Normalise(nc, pr, g, g["x1"], g["x2"], g["slot"])
        block = ctx.enter_context(nc.Block())
        block.sync(norm.sync)
        block.vector(norm.vector)
        block.scalar(norm.scalar)
        block.tensor(norm.tensor)
        block.gpsimd(norm.gpsimd)


def first_block(nc, io, g):
    with ExitStack() as ctx:
        pr = Prog(nc, ctx, "n1_")
        norm = Normalise(nc, pr, g, io["x"])
        dst_ready, act_taken, low_ready, act_sums = (pr.sem("dst_ready"), pr.sem("act_taken"), pr.sem("low_ready"),
                                                     pr.sem("act_sums"))
        sure = 2 * ROWS // ST * ST
        half = (SLOTS - sure) // 2
        zero = pr.sb("zero", [P, half // P * D], F32)
        zero_ready, zero_out, ident_ready, pool_chain = (pr.sem("zero_ready"), pr.sem("zero_out"),
                                                         pr.sem("ident_ready"), pr.sem("pool_chain"))
        dt = pr.sb("w_dst", [P, EG, P], I32)
        dn = pr.sb("w_next", [P, EG, P], I32)
        key = pr.sb("w_key", [P, WINS * VIS, 2], F16)
        low7 = pr.sb("w_low7", [P, WINS * VIS, 2], F16)
        wi = pr.sb("w_iota", [P, WG * P], I32)
        wlo = pr.sb("w_lo", [P, WG * P], F32)
        whi = pr.sb("w_hi", [P, WG * P], F32)
        first = pr.sb("w_first", [P, EG], F32)
        gt = pr.sb("w_gt", [P, EG * P], F32)
        below = pr.sb("w_below", [P, 2, EG, WG * P], F16)
        ones16 = pr.sb("w_ones16", [P, 1], F16)
        ones = pr.sb("w_ones", [P, 1], F32)
        m = pr.sb("w_m", [P, 2, WG], F32)
        lo = pr.sb("w_lotile", [P, 2, WG], F32)
        over = pr.sb("w_over", [P, WG + 1], F32)
        bad = pr.sb("w_bad", [P, 1], F32)
        idx = pr.sb("w_idx", [P, VIS, WG], I32)
        gd = pr.sb("w_gd", [P, WG, VIS, P], I32)
        gs = pr.sb("w_gs", [P, WG, VIS, P], I32)
        ints = pr.sb("w_ints", [P, 2, WG * VIS * P], I32)
        fl = pr.sb("w_fl", [P, 3, WG, VIS, P], F32)
        tr = pr.sb("w_tr", [P, 3, WG * P, VIS], F32)
        pm = pr.ps("w_pm", [P, 512])
        pt = [pr.ps(f"w_pt{i}", [P, VIS, P]) for i in range(2)]
        pf = pr.ps("w_pf", [P, 1])
        here_bank = norm.bank + [pm]
        here = pr.sb("w_here", [P, W, WINS * VIS], F16)
        degree = pr.sb("w_degree", [1, ROWS], F32)
        here_ready, summed, sums_taken, degree_out = (pr.sem("here_ready"), pr.sem("deg_summed"), pr.sem("sums_taken"),
                                                      pr.sem("degree_out"))
        dst_in, iota_ready, below_ready = pr.sem("dst_in"), pr.sem("iota_ready"), pr.sem("below_ready")
        chain, counted, idx_ready, gathered = (pr.sem("vector_chain"), pr.sem("counted"), pr.sem("idx_ready"),
                                               pr.sem("gathered"))
        fl_ready, turned, taken, bad_ready, bad_summed = (pr.sem("fl_ready"), pr.sem("turned"), pr.sem("taken"),
                                                          pr.sem("bad_ready"), pr.sem("bad_summed"))
        keys_ready, keys_out = pr.sem("keys_ready"), pr.sem("keys_out")
        block = ctx.enter_context(nc.Block())
        NWIN = WINS * W
        HV = WINS // 2

        def degree_place(q):
            j, half = q // 2, q % 2
            return degree[:, 0:NWIN].rearrange("a (v j) -> a j v", j=W)[:, j, half * HV:(half + 1) * HV]

        @block.sync
        def _(sp):
            sp.dma_start(dt[:, :, :], io["dst"][0:EG * P * P].rearrange("(g p e) -> p g e", p=P, e=P)).then_inc(dst_in, 16)
            sp.dma_start(dn[:, :, :], io["dst"][1:EG * P * P + 1].rearrange("(g p e) -> p g e", p=P, e=P)).then_inc(dst_in, 16)
            norm.sync(sp)
            sp.wait_ge(keys_ready, 1)
            sp.dma_start(g["keys"][0], key[:, :, :]).then_inc(keys_out, 16)
            sp.wait_ge(low_ready, 1)
            sp.dma_start(g["keys"][1], low7[:, :, :]).then_inc(keys_out, 16)
            sp.wait_ge(sums_taken, W + 1)
            sp.wait_ge(act_sums, W)
            sp.dma_start(g["degree"], degree[:, :]).then_inc(degree_out, 16)
            sp.wait_ge(keys_out, 32)
            sp.wait_ge(degree_out, 16)

        def turned_place(n):
            a, w = divmod(n, WG)
            return tr[:, a, w * P:(w + 1) * P, :].rearrange("p v i -> p i v")

        @block.scalar
        def _(act):
            norm.scalar(act)
            act.wait_ge(gathered, 16 * 2 * WG * VIS)
            nc.scalar.activation(fl[:, 0, :, :, :].rearrange("p w i e -> p (w i e)"),
                                 gd[:, :, :, :].rearrange("p w i e -> p (w i e)"), ACT.Copy).then_inc(dst_ready, 1)
            for n in range(1, 3 * WG, 2):
                act.wait_ge(turned, n + 1)
                nc.scalar.activation(turned_place(n), pt[1][:, :, :], ACT.Copy).then_inc(act_taken, 1)
            act.wait_ge(taken, len(range(0, 3 * WG, 2)))
            act.wait_ge(act_taken, 3 * WG // 2)
            n = WINS * VIS
            nc.scalar.activation(low7[:, :, :], tr[:, 2, :, :].rearrange("p v i -> p (v i)")[:, 0:n]
                                 .unsqueeze(2).broadcast_to([P, n, 2]), ACT.Copy).then_inc(low_ready, 1)
            for q in range(1, 2 * W, 2):
                act.wait_ge(summed, q + 1)
                nc.scalar.activation(degree_place(q), here_bank[q % 4][0:1, 0:HV], ACT.Copy).then_inc(act_sums, 1)

        @block.gpsimd
        def _(pool):
            nc.gpsimd.memset(g["ident"][:, :], 0.0).then_inc(pool_chain, 1)
            pool.wait_ge(pool_chain, 1)
            nc.gpsimd.affine_select(out=g["ident"][:, :], in_=g["ident"][:, :], compare_op=ALU.not_equal, fill=1.0,
                                    base=0, pattern=[[-1, P]], channel_multiplier=1).then_inc(ident_ready, 1)
            nc.gpsimd.iota(wi[:, :], pattern=[[W, WG * P]], base=0, channel_multiplier=0).then_inc(iota_ready, 1)
            nc.gpsimd.memset(zero[:, :], 0.0).then_inc(zero_ready, 1)
            pool.wait_ge(idx_ready, 1)
            for w in range(WG):
                for i in range(VIS):
                    for rows, to in ((io["dst"], gd), (io["src"], gs)):
                        pool.indirect_dma_start(out=to[:, w, i, :], out_offset=None, in_=rows.rearrange("(t e) -> t e", e=P),
                                                in_offset=bass.IndirectOffsetOnAxis(ap=idx[:, i, w:w + 1], axis=0)
                                                ).then_inc(gathered, 16)
            pool.wait_ge(zero_ready, 1)
            for n in range(2):
                pool.dma_start(g["slots_out"][sure + n * half:sure + (n + 1) * half, :].rearrange("(p r) d -> p (r d)", p=P),
                               zero[:, 0:half // P * D]).then_inc(zero_out, 16)
            pool.wait_ge(zero_out, 16 * 2)

        @block.vector
        def _(dve):
            ch = Chain(dve, chain)
            ch.mark(nc.vector.memset(ones16[:, :], 1.0))
            ch.mark(nc.vector.memset(ones[:, :], 1.0))
            dve.wait_ge(iota_ready, 1)
            ch.mark(nc.vector.tensor_copy(wlo[:, :], wi[:, :]))
            ch.mark(nc.vector.tensor_scalar(whi[:, :], wi[:, :], float(W), None, ALU.add))
            dve.wait_ge(dst_in, 32)
            ch.mark(nc.vector.tensor_copy(first[:, :], dt[:, :, 0]))
            ch.done(nc.vector.tensor_tensor(gt[:, :], dt[:, :, :].rearrange("p g e -> p (g e)"),
                                            dn[:, :, :].rearrange("p g e -> p (g e)"), ALU.is_gt))
            ch.mark(nc.vector.reduce_sum(over[:, WG:WG + 1], gt[:, :], AX.X))
            for n, edge in ((0, wlo), (1, whi)):
                for q in range(EG):
                    last = nc.vector.tensor_scalar(below[:, n, q, :], edge[:, :], first[:, q:q + 1], None, ALU.is_gt)
            last.then_inc(below_ready, 1)
            dve.wait_ge(counted, 1)
            ch.done(nc.vector.tensor_copy(m[:, :, :], pm[:, 0:2 * WG].rearrange("p (n w) -> p n w", n=2)))
            ch.done(nc.vector.tensor_scalar(lo[:, 0, :], m[:, 0, :], -1.0, 0.0, ALU.add, ALU.max))
            for i in range(VIS):
                last = nc.vector.tensor_scalar(idx[:, i, :], lo[:, 0, :], float(i), None, ALU.add)
            last.then_inc(idx_ready, 1)
            ch.done(nc.vector.tensor_tensor(lo[:, 1, :], m[:, 1, :], lo[:, 0, :], ALU.subtract))
            ch.done(nc.vector.tensor_scalar(over[:, 0:WG], lo[:, 1, :], float(VIS), None, ALU.is_gt))
            nc.vector.reduce_sum(bad[:, :], over[:, :], AX.X).then_inc(bad_ready, 1)
            dve.wait_ge(bad_summed, 1)
            ch.mark(nc.vector.tensor_copy(g["flag"][0:1, 0:1], pf[0:1, 0:1]))
            norm.vector(dve)
            dve.wait_ge(gathered, 16 * 2 * WG * VIS)
            src = gs[:, :, :, :].rearrange("p w i e -> p (w i e)")
            dst = gd[:, :, :, :].rearrange("p w i e -> p (w i e)")
            flat = fl[:, :, :, :, :].rearrange("p a w i e -> p a (w i e)")
            ch.mark(nc.vector.tensor_scalar(ints[:, 0, :], src, 7, None, ALU.logical_shift_right))
            ch.done(nc.vector.tensor_scalar(ints[:, 1, :], src, P - 1, None, ALU.bitwise_and))
            ch.mark(nc.vector.scalar_tensor_tensor(flat[:, 1, :], ints[:, 0, :], float(W), dst, ALU.mult, ALU.add))
            nc.vector.tensor_copy(flat[:, 2, :], ints[:, 1, :]).then_inc(fl_ready, 1)
            dve.wait_ge(fl_ready, 1)
            for n in range(0, 3 * WG, 2):
                dve.wait_ge(turned, n + 1)
                nc.vector.tensor_copy(turned_place(n), pt[0][:, :, :]).then_inc(taken, 1)
            dve.wait_ge(taken, len(range(0, 3 * WG, 2)))
            dve.wait_ge(act_taken, 3 * WG // 2)
            base = wlo[:, :].unsqueeze(2).broadcast_to([P, WG * P, VIS])
            t1, t2 = fl[:, 0, :, :, :].rearrange("p w i e -> p (w i e)"), fl[:, 1, :, :, :].rearrange("p w i e -> p (w i e)")
            u = fl[:, 2, :, :, :].rearrange("p w i e -> p (w i e)")
            three = lambda ap: ap.rearrange("p (v i) -> p v i", i=VIS)
            ch.mark(nc.vector.tensor_tensor(three(t1), tr[:, 0, :, :], base, ALU.subtract))
            ch.done(nc.vector.tensor_tensor(three(t2), tr[:, 1, :, :], base, ALU.subtract))
            ch.done(nc.vector.tensor_scalar(t2, t2, 1.0, None, ALU.add))
            ch.done(nc.vector.scalar_tensor_tensor(u, t1, 0.0, t2, ALU.is_ge, ALU.mult))
            n = WINS * VIS
            twice = lambda ap: ap.unsqueeze(2).broadcast_to([P, n, 2])
            nc.vector.scalar_tensor_tensor(key[:, :, :], twice(t1[:, 0:n]), float(W), twice(u[:, 0:n]),
                                           ALU.is_lt, ALU.mult).then_inc(keys_ready, 1)
            nc.vector.memset(degree[:, NWIN:ROWS], 0.0).then_inc(sums_taken, 1)
            for j in range(W):
                nc.vector.tensor_scalar(here[:, j, :], t1[:, 0:n], float(j), None, ALU.is_equal).then_inc(here_ready, 1)
            for q in range(0, 2 * W, 2):
                dve.wait_ge(summed, q + 1)
                nc.vector.tensor_copy(degree_place(q), here_bank[q % 4][0:1, 0:HV]).then_inc(sums_taken, 1)

        @block.tensor
        def _(pe):
            pe.wait_ge(below_ready, 1)
            for n in range(2):
                for w in range(WG):
                    for q in range(EG):
                        last = nc.tensor.matmul(pm[:, n * WG + w:n * WG + w + 1], below[:, n, q, w * P:(w + 1) * P],
                                                ones16[:, :], start=(q == 0), stop=(q == EG - 1))
            last.then_inc(counted, 1)
            pe.wait_ge(bad_ready, 1)
            nc.tensor.matmul(pf[0:1, 0:1], bad[:, :], ones[:, :], start=True, stop=True).then_inc(bad_summed, 1)
            pe.wait_ge(ident_ready, 1)
            norm.tensor(pe)
            pe.wait_ge(dst_ready, 1)
            pe.wait_ge(fl_ready, 1)
            for n in range(3 * WG):
                a, w = divmod(n, WG)
                if n >= 2:
                    pe.wait_ge(act_taken if n % 2 else taken, n // 2)
                for i in range(VIS):
                    last = nc.tensor.transpose(pt[n % 2][:, i, :], fl[:, a, w, i, :], g["ident"][:, :])
                last.then_inc(turned, 1)
            pe.wait_ge(norm.s["xt_ready"], CHUNKS)
            for q in range(2 * W):
                j, half = q // 2, q % 2
                pe.wait_ge(here_ready, j + 1)
                if q >= 4:
                    pe.wait_ge(act_sums if q % 2 else sums_taken, (q - 4) // 2 + (1 if q % 2 else 2))
                for i in range(VIS):
                    last = nc.tensor.matmul(here_bank[q % 4][0:1, 0:HV], ones16[:, :],
                                            here[:, j, :].rearrange("p (v i) -> p i v", i=VIS)[:, i, half * HV:(half + 1) * HV],
                                            start=i == 0, stop=i == VIS - 1)
                last.then_inc(summed, 1)


def aggregate(nc, pe, flag, adj, at, stationary, bank, hib, hi_in, hi_used, n, before=None):
    def tile(k, moving, first=False, last=False):
        if before and isinstance(k, int):
            before(k)
        seen = set()
        ops = stationary(k)
        for j, (f, operand) in enumerate(ops):
            ins = nc.tensor.matmul(bank[f], operand, moving, start=first and f not in seen,
                                   stop=last and f not in [x for x, _ in ops[j + 1:]])
            seen.add(f)
        return ins

    def upper_counts():
        if before:
            before(TILES - 1)
        with pe.Fori(0, TILES) as k:
            pe.wait_ge(hi_in, 16 * (n * TILES + k + 1))
            tile(k, hib[:, :])
            tile(k, hib[:, :]).then_inc(hi_used, 1)

    tile(0, adj[:, 0, at], first=True)
    if flag is None:
        upper_counts()
    else:
        with pe.If(flag != 0):
            upper_counts()
        with pe.Else():
            pe.nop()
    for k in range(1, TILES):
        ins = tile(k, adj[:, k, at], last=(k == TILES - 1))
    return ins


def feed_upper_counts(sp, g, flag, hib, hi_in, hi_used):
    def feed():
        with sp.Fori(0, 2 * CHUNKS) as n:
            with sp.Fori(0, TILES) as k:
                sp.wait_ge(hi_used, n * TILES + k)
                sp.dma_start(hib[:, :], g["upper"][ds(k * P, P), ds(n * SUB, SUB)]).then_inc(hi_in, 16)

    if flag is None:
        feed()
    else:
        with sp.If(flag != 0):
            feed()
        with sp.Else():
            sp.nop()


def build_counts(nc, io, g, adj):
    with ExitStack() as ctx:
        pr = Prog(nc, ctx)
        key = pr.sb("b_key", [P, WINS * VIS, 2], F16)
        low7 = pr.sb("b_low7", [P, WINS * VIS, 2], F16)
        it16 = pr.sb("b_it16", [P, NW], F16)
        ib16 = pr.sb("b_ib16", [P, P], F16)
        ones = pr.sb("b_ones", [P, 1], F16)
        sel = pr.sb("b_sel", [P, SLOT * GW * VIS, NW], F16)
        low = pr.sb("b_low", [P, SLOT * GW * VIS, P], F16)
        parts = pr.sb("b_parts", [P, TILES, 2, D], F16)
        sums = pr.sb("b_sums", [P, KD, BW], F32)
        by_part = pr.sb("b_by_part", [P, 3, TILES], F32)
        place, used = parts[:, :, :, :].rearrange("p t a d -> p (t a d)"), [0]

        def before_parts(count, dt):
            size = count * (2 if dt == F32 or dt == I32 else 1)
            at, used[0] = used[0], used[0] + size
            assert used[0] <= TILES * 2 * D
            return place[:, at:at + size].bitcast(dt) if dt != F16 else place[:, at:at + size]

        it = before_parts(WG * P, I32)
        win = before_parts(WINS, F32)
        split = lambda ap, n: ap.rearrange("p (a n) -> p a n", a=n)
        gst, gi, gf = (split(before_parts(n * SG, dt), n) for n, dt in ((2, I32), (2, I32), (3, F32)))
        gk, gl = split(before_parts(SG * 2, F16), SG), split(before_parts(SG * 2, F16), SG)
        gc, ghi = split(before_parts(3 * NW, I32), 3), before_parts(NW, F16)
        hib = sel[:, 0:2, :].rearrange("p r n -> p (r n)")[:, 0:BW]
        deg = key[:, :, :].rearrange("p n two -> p (n two)")[0:1, 0:2 * BW].bitcast(F32)
        pw = [pr.ps(f"b_pw{i}", [P, 512]) for i in range(SLOT)]
        pa = [pr.ps(f"b_pa{f}", [P, BW]) for f in range(KD)]
        pd = pr.ps("b_pd", [P, BW])
        s = {n: pr.sem("b_" + n) for n in (
            "const", "chain", "ready", "sel_ready", "multiplied", "copied", "g_in", "g_sel", "g_mult", "g_win",
            "g_split", "g_copied", "g_hi_out", "g_edge", "hi_in", "hi_used", "summed", "sums_ready", "sums_out",
            "deg_ready", "deg_out", "deg_in", "by_part", "inv_done", "inv_out", "adj_done", "first_keys_in", "keys_in", "parts_in",
            "rest_out", "degrees_out")}
        block = ctx.enter_context(nc.Block())
        NWIN = WINS * W
        EARLY = UNROLL // 2 * GW * VIS

        def one_hot(out, values, names, width):
            r = values.shape[1]
            shape = [P, r, width // 2, 2]
            return nc.vector.tensor_tensor(
                out.rearrange("p r (h two) -> p r h two", two=2),
                names[:, 0:width].rearrange("p (h two) -> p h two", two=2).unsqueeze(1).broadcast_to(shape),
                values.unsqueeze(2).broadcast_to(shape), ALU.is_equal)

        @block.gpsimd
        def _(pool):
            nc.gpsimd.iota(it, pattern=[[1, WG * P]], base=0, channel_multiplier=0).then_inc(s["const"], 1)
            spread = lambda ap: ap.rearrange("a (p t) -> (a p) t", p=P)
            pool.wait_ge(s["degrees_out"], 1)
            pool.dma_start(by_part[:, 0, :], spread(g["degree"])).then_inc(s["deg_in"], 16)
            pool.wait_ge(s["inv_done"], 1)
            pool.dma_start(spread(g["inv"]), by_part[:, 2, :]).then_inc(s["inv_out"], 16)
            pool.wait_ge(s["inv_out"], 16)

        @block.vector
        def _(dve):
            ch = Chain(dve, s["chain"])
            dve.wait_ge(s["const"], 1)
            ch.mark(nc.vector.tensor_copy(it16[:, :], it[:, 1:NW + 1]))
            ch.mark(nc.vector.tensor_copy(ib16[:, :], it[:, 0:P]))
            ch.mark(nc.vector.memset(ones[:, :], 1.0))
            ch.mark(nc.vector.tensor_scalar(win, it[:, 0:WINS], float(W), None, ALU.mult))
            ch.mark(nc.vector.memset(adj[:, :, NWIN:ROWS], 0.0))
            ch.mark(nc.vector.memset(sums[:, :, 0:ROWS - NWIN], 0.0))
            ch.wait()
            dve.sem_inc(s["ready"], 1)

            def invert():
                dve.wait_ge(s["deg_in"], 16)
                nc.vector.tensor_scalar(by_part[:, 1, :], by_part[:, 0, :], 1.0, XS, ALU.max, ALU.mult).then_inc(s["by_part"], 1)
                dve.wait_ge(s["by_part"], 1)
                nc.vector.reciprocal(by_part[:, 2, :], by_part[:, 1, :]).then_inc(s["inv_done"], 1)

            flag = dve.value_load(g["flag"][0:1, 0:1])
            with dve.If(flag != 0):
                with dve.Fori(0, WINS) as v:
                    with dve.Fori(0, SSTEPS) as u:
                        n = v * SSTEPS + u
                        gch = Chain(dve, s["g_edge"])
                        gch.base = (n * 6) + v * 3
                        dve.wait_ge(s["g_in"], 32 * (n + 1))
                        gch.mark(nc.vector.tensor_scalar(gi[:, 0, :], gst[:, 1, :], 7, None, ALU.logical_shift_right))
                        gch.mark(nc.vector.tensor_scalar(gi[:, 1, :], gst[:, 1, :], P - 1, None, ALU.bitwise_and))
                        gch.done(nc.vector.tensor_scalar(gf[:, 0, :], gst[:, 0, :], win[:, ds(v, 1)], None, ALU.subtract))
                        gch.done(nc.vector.scalar_tensor_tensor(gf[:, 1, :], gi[:, 0, :], float(W), gf[:, 0, :],
                                                                ALU.mult, ALU.add))
                        gch.done(nc.vector.tensor_scalar(gf[:, 2, :], gf[:, 1, :], 1.0, None, ALU.add))
                        dve.wait_ge(s["g_mult"], n)
                        gch.done(nc.vector.scalar_tensor_tensor(gf[:, 1, :], gf[:, 0, :], 0.0, gf[:, 2, :],
                                                                ALU.is_ge, ALU.mult))
                        two = lambda ap: ap.unsqueeze(2).broadcast_to([P, SG, 2])
                        nc.vector.scalar_tensor_tensor(gk[:, :, :], two(gf[:, 0, :]), float(W), two(gf[:, 1, :]),
                                                       ALU.is_lt, ALU.mult).then_inc(s["g_split"], 1)
                        nc.vector.tensor_copy(gl[:, :, :], two(gi[:, 1, :])).then_inc(s["g_split"], 1)
                        dve.wait_ge(s["g_split"], 2 * (n + 1))
                        one_hot(sel[:, 0:SG, :], gk[:, :, :], it16, NW)
                        one_hot(low[:, 0:SG, :], gl[:, :, :], ib16, P).then_inc(s["g_sel"], 1)
                    gch = Chain(dve, s["g_edge"])
                    gch.base = (v + 1) * SSTEPS * 6 + v * 3
                    dve.wait_ge(s["g_win"], v + 1)
                    gch.done(nc.vector.tensor_copy(gc[:, 0, :], pw[0][:, 0:NW]))
                    gch.mark(nc.vector.tensor_scalar(gc[:, 1, :], gc[:, 0, :], 11, None, ALU.logical_shift_right))
                    gch.done(nc.vector.tensor_scalar(gc[:, 2, :], gc[:, 0, :], int(SPLIT) - 1, None, ALU.bitwise_and))
                    dve.wait_ge(s["g_hi_out"], 16 * (v + 1))
                    nc.vector.tensor_copy(adj[:, :, ds(v * W, W)], gc[:, 2, :].rearrange("p (k j) -> p k j", j=W))
                    nc.vector.tensor_scalar(ghi, gc[:, 1, :], SPLIT / 2, None, ALU.mult).then_inc(s["g_copied"], 1)
                dve.wait_ge(s["g_copied"], WINS)
                dve.sem_inc(s["adj_done"], 1)
                invert()
            with dve.Else():
                dve.wait_ge(s["first_keys_in"], 32)
                with dve.Fori(0, BODIES) as body:
                    for u in range(UNROLL):
                        group = body * UNROLL + u
                        if u == UNROLL // 2:
                            dve.wait_ge(s["keys_in"], 32)
                        at, slot = ds(group * GW * VIS, GW * VIS), slice(u % SLOT * GW * VIS, (u % SLOT + 1) * GW * VIS)
                        dve.wait_ge(s["multiplied"], group)
                        one_hot(sel[:, slot, :], key[:, at, :], it16, NW)
                        one_hot(low[:, slot, :], low7[:, at, :], ib16, P).then_inc(s["sel_ready"], 1)
                invert()
        @block.scalar
        def _(act):
            act.wait_ge(s["ready"], 1)
            flag = act.value_load(g["flag"][0:1, 0:1])
            def take_sums(r):
                act.wait_ge(s["summed"], r + 1)
                act.wait_ge(s["sums_out"], 16 * r)
                for f in range(KD):
                    nc.scalar.activation(sums[:, f, :], pa[f][:, :], ACT.Copy).then_inc(s["sums_ready"], 1)

            with act.If(flag != 0):
                act.wait_ge(s["rest_out"], 16)
                with act.Fori(0, BODIES) as r:
                    take_sums(r)
                    act.wait_ge(s["deg_out"], 16 * r)
                    nc.scalar.activation(deg, pd[0:1, :], ACT.Copy).then_inc(s["deg_ready"], 1)
            with act.Else():
                act.sem_inc(s["copied"], SLOT - 1)

                def take_counts(body, u):
                    group = body * UNROLL + u
                    act.wait_ge(s["multiplied"], group + SLOT)
                    nc.scalar.activation(
                        adj[:, :, ds(group * GW * W, GW * W)].rearrange("p k (w j) -> p w k j", j=W),
                        pw[u % SLOT][:, 0:GW * NW].rearrange("p (w k j) -> p w k j", w=GW, j=W), ACT.Copy).then_inc(s["copied"], 1)

                for u in range(UNROLL):
                    take_counts(0, u)
                act.wait_ge(s["rest_out"], 16)
                with act.Fori(1, BODIES) as body:
                    for u in range(UNROLL):
                        take_counts(body, u)
                    take_sums(body - 1)
                take_sums(BODIES - 1)

        @block.tensor
        def _(pe):
            pe.wait_ge(s["ready"], 1)
            pe.sem_inc(s["multiplied"], SLOT - 1)
            flag = pe.value_load(g["flag"][0:1, 0:1])
            with pe.If(flag != 0):
                with pe.Fori(0, WINS) as v:
                    def step(n, first=False, last=False):
                        pe.wait_ge(s["g_sel"], n + 1)
                        for i in range(SG):
                            ins = nc.tensor.matmul(pw[0][:, 0:NW], low[:, i, :], sel[:, i, 0:NW],
                                                   start=first and i == 0, stop=last and i == SG - 1)
                        ins.then_inc(s["g_mult"], 1)
                    pe.wait_ge(s["g_copied"], v)
                    step(v * SSTEPS, first=True)
                    with pe.Fori(1, SSTEPS - 1) as u:
                        step(v * SSTEPS + u)
                    step(v * SSTEPS + SSTEPS - 1, last=True)
                    pe.wait_ge(s["g_mult"], (v + 1) * SSTEPS)
                    pe.sem_inc(s["g_win"], 1)
                pe.wait_ge(s["adj_done"], 1)
                pe.wait_ge(s["parts_in"], 16 * CHUNKS)
                with pe.Fori(0, BODIES) as r:
                    pe.wait_ge(s["sums_ready"], KD * r)
                    pe.wait_ge(s["deg_ready"], r)
                    aggregate(nc, pe, None, adj, ds(r * BW, BW),
                              lambda k: [(f, parts[:, k, a, f * P:(f + 1) * P]) for a in range(2) for f in range(KD)]
                              + [(KD, ones[:, :])], [pa[f][:, :] for f in range(KD)] + [pd[0:1, :]],
                              hib, s["hi_in"], s["hi_used"], r).then_inc(s["summed"], 1)
            with pe.Else():
                def count(body, u):
                    group = body * UNROLL + u
                    pe.wait_ge(s["sel_ready"], group + 1)
                    pe.wait_ge(s["copied"], group)
                    for w in range(GW):
                        for i in range(VIS):
                            n = (u % SLOT * GW + w) * VIS + i
                            ins = nc.tensor.matmul(pw[u % SLOT][:, w * NW:(w + 1) * NW], low[:, n, :], sel[:, n, :],
                                                   start=i == 0, stop=i == VIS - 1)
                    ins.then_inc(s["multiplied"], 1)

                def add_up(r, tiles):
                    if 0 in tiles:
                        pe.wait_ge(s["copied"], (r + 1) * UNROLL + SLOT - 1)
                        pe.wait_ge(s["sums_ready"], KD * r)
                    for k in tiles:
                        for a in range(2):
                            for f in range(KD):
                                ins = nc.tensor.matmul(pa[f][:, :], parts[:, k, a, f * P:(f + 1) * P],
                                                       adj[:, k, ds(r * BW, BW)], start=k == 0 and a == 0,
                                                       stop=k == TILES - 1 and a == 1)
                    if TILES - 1 in tiles:
                        ins.then_inc(s["summed"], 1)

                for u in range(UNROLL):
                    count(0, u)
                pe.wait_ge(s["parts_in"], 16 * CHUNKS)
                with pe.Fori(1, BODIES) as body:
                    for u in range(UNROLL):
                        count(body, u)
                        if 1 <= u < UNROLL - 1:
                            add_up(body - 1, range(TILES * (u - 1) // (UNROLL - 2), TILES * u // (UNROLL - 2)))
                add_up(BODIES - 1, range(TILES))

        @block.sync
        def _(sp):
            for at, sem in ((slice(0, EARLY), s["first_keys_in"]), (slice(EARLY, WINS * VIS), s["keys_in"])):
                sp.dma_start(key[:, at, :], g["keys"][0][:, at, :]).then_inc(sem, 16)
                sp.dma_start(low7[:, at, :], g["keys"][1][:, at, :]).then_inc(sem, 16)
            sp.wait_ge(s["ready"], 1)
            sp.dma_start(g["sums"][:, :, NWIN:ROWS], sums[:, :, 0:ROWS - NWIN]).then_inc(s["rest_out"], 16)
            flag = sp.value_load(g["flag"][0:1, 0:1])

            def load_all_parts():
                for i in range(CHUNKS):
                    load_parts(sp, g, {"parts": parts}, i, s["parts_in"])

            def store_sums(r):
                sp.wait_ge(s["sums_ready"], KD * (r + 1))
                sp.dma_start(g["sums"][:, :, ds(r * BW, BW)], sums[:, :, :]).then_inc(s["sums_out"], 16)

            with sp.If(flag != 0):
                sp.dma_start(g["upper"].rearrange("(k p) n -> p k n", p=P)[:, :, NWIN:ROWS],
                             adj[:, :, NWIN:ROWS]).then_inc(s["g_hi_out"], 16)
                with sp.Fori(0, WINS) as v:
                    with sp.Fori(0, SSTEPS) as u:
                        sp.wait_ge(s["g_sel"], v * SSTEPS + u)
                        for n, rows in enumerate((io["dst"], io["src"])):
                            sp.dma_start(gst[:, n, :], rows.rearrange("(t e) -> e t", e=P)[:, ds(u * SG, SG)],
                                         allow_slow_non_contiguous=True).then_inc(s["g_in"], 16)
                    sp.wait_ge(s["g_copied"], v + 1)
                    sp.dma_start(g["upper"].rearrange("(k p) n -> p k n", p=P)[:, :, ds(v * W, W)],
                                 ghi.rearrange("p (k j) -> p k j", j=W)).then_inc(s["g_hi_out"], 16)
                sp.wait_ge(s["g_hi_out"], 16 * (WINS + 1))
                load_all_parts()
                with sp.Fori(0, BODIES) as r:
                    with sp.Fori(0, TILES) as k:
                        sp.wait_ge(s["hi_used"], r * TILES + k)
                        sp.dma_start(hib, g["upper"][ds(k * P, P), ds(r * BW, BW)]).then_inc(s["hi_in"], 16)
                    store_sums(r)
                    sp.wait_ge(s["deg_ready"], r + 1)
                    sp.dma_start(g["degree"][:, ds(r * BW, BW)], deg).then_inc(s["deg_out"], 16)
                sp.wait_ge(s["deg_out"], 16 * BODIES)
                sp.sem_inc(s["degrees_out"], 1)
            with sp.Else():
                sp.sem_inc(s["degrees_out"], 1)
                load_all_parts()
                with sp.Fori(0, BODIES) as r:
                    store_sums(r)
            sp.wait_ge(s["sums_out"], 16 * BODIES)
            sp.wait_ge(s["rest_out"], 16)


BT = -(-CT // 2)


def in_bank(banks, n):
    count = min(2, CT - 2 * n)
    return slice(2 * n, 2 * n + count), banks[n][:, 0:count * D].rearrange("p (t d) -> p t d", d=D)


def conv_tensors(pr, parts):
    t = {
        "parts": parts,
        "inv": pr.sb("c_inv", [P, CH], F32),
        "mean": pr.sb("c_mean", [P, KD, CH], F32),
        "own": pr.sb("c_own", [P, KD, CH], F32),
        "wl": pr.sb("c_wl", [P, KD, D], F32),
        "wr": pr.sb("c_wr", [P, KD, D], F32),
        "hib": pr.sb("c_hib", [P, SUB], F16),
        "agg": [[pr.ps(f"c_agg{h}{f}", [P, SUB]) for f in range(KD)] for h in range(2)],
        "bank": [pr.ps(f"c_bank{i}", [P, 512]) for i in range(4)],
    }
    return t


def conv_tensor_engine(nc, g, adj, t, s, dense, turn, turn_at, score=None, rank=None, loading=False):
    def agg(pe, flag, c, h, before=None):
        def parts_loaded(k):
            if k % CT == 0 or k == TILES - 1:
                for i in range(0 if k == TILES - 1 else k // CT, k // CT + 1):
                    pe.wait_ge(s[f"parts_in{i}"], 16)
        first = isinstance(c, int) and c == 0
        if not first:
            pe.wait_ge(s["mean_done"], 4 * c - 2 + 2 * h)
        aggregate(nc, pe, flag, adj, ds(c * CH + h * SUB, SUB),
                  lambda k: [(f, t["parts"][:, k, a, f * P:(f + 1) * P]) for a in range(2) for f in range(KD)],
                  [t["agg"][h][f][:, :] for f in range(KD)], t["hib"], s["hi_in"], s["hi_used"], 2 * c + h,
                  parts_loaded if loading and first and h == 0 else before).then_inc(s["agg_done"], 1)

    def run(pe):
        flag = pe.value_load(g["flag"][0:1, 0:1])
        agg(pe, flag, 0, 0)
        agg(pe, flag, 0, 1)

        def chunk(c, ranks):
            agg(pe, flag, c, 0, lambda k: rank(pe, c - 2) if ranks and k == 8 else None)
            dense(pe, c - 1)
            agg(pe, flag, c, 1, lambda k: turn(pe, c - 1) if k == turn_at else None)
            if score:
                score(pe, c - 1)

        if rank:
            chunk(1, False)
            with pe.Fori(2, CHUNKS) as c:
                chunk(c, True)
            rank(pe, CHUNKS - 2)
        else:
            with pe.Fori(1, CHUNKS) as c:
                chunk(c, False)
        dense(pe, CHUNKS - 1)
        turn(pe, CHUNKS - 1)
        if score:
            score(pe, CHUNKS - 1)
        if rank:
            rank(pe, CHUNKS - 1)
    return run


def mean_half(nc, dve, t, s, c, h):
    dve.wait_ge(s["agg_done"], 2 * c + h + 1)
    if h == 0:
        dve.wait_ge(s["inv_in"], 16 * (c + 1))
        dve.wait_ge(s["dense_done"], c)
    for f in range(KD):
        at = slice(h * SUB, (h + 1) * SUB)
        nc.vector.tensor_tensor(t["mean"][:, f, at], t["agg"][h][f][:, :], t["inv"][:, at], ALU.mult
                                ).then_inc(s["mean_done"], 1)


def load_parts(sp, g, t, i, sem):
    sp.dma_start(t["parts"][:, i * CT:(i + 1) * CT, :, :].rearrange("p t a d -> p (t a d)"),
                 g["parts"][:, i * CT * 2 * D:(i + 1) * CT * 2 * D]).then_inc(sem, 16)


def load_chunk_inv(sp, g, t, s, c, at):
    sp.wait_ge(s["mean_done"], 4 * c)
    sp.dma_start(t["inv"][:, :], g["inv"][:, ds(at, CH)].broadcast_to([P, CH])).then_inc(s["inv_in"], 16)


CONV_SEMS = ("weights_in", "inv_in", "own_in", "agg_done", "mean_done", "dense_done", "hi_in",
             "hi_used", "chain", "ready", "turned", "stored")


def scale_of_h(nc, ch, g, weights, bias, small, scale_done):
    for f in range(KD):
        ch.mark(nc.vector.tensor_reduce(small[:, 0, f:f + 1], weights[:, f, 0:2 * D], AX.X, ALU.add,
                                        apply_absolute_value=True))
        ch.mark(nc.vector.tensor_reduce(small[:, 1, f:f + 1], bias[:, f:f + 1], AX.X, ALU.add,
                                        apply_absolute_value=True))
    ch.wait()
    ch.done(nc.vector.scalar_tensor_tensor(small[:, 2, :], small[:, 0, :], 16.0, small[:, 1, :], ALU.mult, ALU.add))
    ch.done(nc.vector.tensor_scalar(small[:, 3, :], small[:, 2, :], 1e-20, None, ALU.max))
    ch.done(nc.vector.tensor_scalar(small[:, 4, :].bitcast(I32), small[:, 3, :].bitcast(I32), 0x7F800000, None,
                                    ALU.bitwise_and))
    ch.done(nc.vector.tensor_scalar(g["unscale"][:, :], small[:, 4, :], 2.0 ** -14, None, ALU.mult))
    ch.done(nc.vector.reciprocal(g["scale"][:, :], g["unscale"][:, :]))
    nc.vector.tensor_tensor(small[:, 5, :], bias[:, :], g["scale"][:, :], ALU.mult).then_inc(scale_done, 1)


def lagged(eng, first, second):
    first(0, 0, 0)
    with eng.Fori(0, CHUNKS // 2) as i:
        first(i * 2 + 1, 1, i)
        second(i * 2, 0, i)
        first(i * 2 + 2, 0, i + 1)
        second(i * 2 + 1, 1, i)
    assert CHUNKS % 2 == 1
    second(CHUNKS - 1, 0, CHUNKS // 2)


def summed_conv(nc, io, g, tag, names):
    wl, b, wr = names
    with ExitStack() as ctx:
        pr = Prog(nc, ctx, tag)
        mean = pr.sb("mean", [P, 2, KD, CH], F32)
        own = pr.sb("own", [P, 2, KD, CH], F32)
        inv = pr.sb("inv", [P, 2, CH], F32)
        h = pr.sb("h", [P, 2, KD, CH], F32)
        part = pr.sb("part", [P, CT, 2, D], F16)
        w_l = pr.sb("wl", [P, KD, D], F32)
        w_r = pr.sb("wr", [P, KD, D], F32)
        bias = pr.sb("bias", [P, KD], F32)
        small = pr.sb("small", [P, 6, KD], F32)
        bank = [pr.ps(f"bank{i}", [P, 512]) for i in range(4)]
        turned_bank = [pr.ps(f"turned{i}", [P, 512]) for i in range(BT)]
        weights = part[:, :, :, :].rearrange("p t a d -> p (t a d)").bitcast(F32)[:, 0:2 * KD * D].rearrange(
            "p (f n) -> p f n", f=KD)
        s = {n: pr.sem(n) for n in ("norms_in", "weights_in", "in0", "in1", "mean_done", "group_done", "free0", "free1",
                                    "h_done", "h_out0", "h_out1", "turned", "high_done", "low_done", "part_out",
                                    "scale_done", "chain")}
        block = ctx.enter_context(nc.Block())

        @block.sync
        def _(sp):
            def load(c, u, i):
                at = sp.snap(c * CH) if not isinstance(c, int) else c * CH
                sp.wait_ge(s[f"free{u}"], i)
                got = s[f"in{u}"]
                sp.dma_start(mean[:, u, :, :], g["sums"][:, :, ds(at, CH)]).then_inc(got, 16)
                sp.dma_start(inv[:, u, :], g["inv"][:, ds(at, CH)].broadcast_to([P, CH])).then_inc(got, 16)
                sp.dma_start(own[:, u, :, :], g["xt"][:, :, ds(at, CH)]).then_inc(got, 16)

            over_chunks(sp, load)

        @block.gpsimd
        def _(pool):
            pool.dma_start(w_l[:, :, :], io[wl + "_T"].rearrange("(k p) f -> p k f", p=P)).then_inc(s["weights_in"], 16)
            pool.dma_start(w_r[:, :, :], io[wr + "_T"].rearrange("(k p) f -> p k f", p=P)).then_inc(s["weights_in"], 16)

            def mean_of(c, u, i):
                pool.wait_ge(s[f"in{u}"], 48 * (i + 1))
                for half in range(2):
                    at = slice(half * SUB, (half + 1) * SUB)
                    nc.gpsimd.tensor_tensor(mean[:, u, :, at], mean[:, u, :, at],
                                            inv[:, u, at].unsqueeze(1).broadcast_to([P, KD, SUB]), ALU.mult
                                            ).then_inc(s["mean_done"], 1)

            over_chunks(pool, mean_of)

        @block.vector
        def _(dve):
            ch = Chain(dve, s["chain"])
            dve.wait_ge(s["norms_in"], 48)
            scale_of_h(nc, ch, g, weights, bias, small, s["scale_done"])

            def low_parts(c, u, i):
                for n in range(BT):
                    dve.wait_ge(s["high_done"], BT * c + n + 1)
                    tiles, turned = in_bank(turned_bank, n)
                    nc.vector.tensor_tensor(part[:, tiles, 1, :], turned, part[:, tiles, 0, :], ALU.subtract
                                            ).then_inc(s["low_done"], 1)

            over_chunks(dve, low_parts)

        @block.scalar
        def _(act):
            act.dma_start(bias[:, :], io[b].rearrange("(f p) -> p f", p=P), allow_slow_non_contiguous=True).then_inc(s["norms_in"], 16)
            act.dma_start(weights[:, :, 0:D], io[wl].rearrange("(f p) k -> p f k", p=P)).then_inc(s["norms_in"], 16)
            act.dma_start(weights[:, :, D:2 * D], io[wr].rearrange("(f p) k -> p f k", p=P)).then_inc(s["norms_in"], 16)
            act.wait_ge(s["scale_done"], 1)

            def relu(c, u, i):
                act.wait_ge(s[f"h_out{u}"], 16 * i)
                for n in range(4):
                    f, half = n % 2, n // 2
                    act.wait_ge(s["group_done"], 4 * c + n + 1)
                    nc.scalar.activation(h[:, u, f, half * SUB:(half + 1) * SUB], bank[n][:, 0:SUB], ACT.Relu,
                                         bias=small[:, 5, f:f + 1], scale=g["scale"][:, f:f + 1]).then_inc(s["h_done"], 1)
                act.wait_ge(s["h_done"], 4 * (c + 1))
                act.dma_start(g["ht"][:, :, ds(c * CH, CH)], h[:, u, :, :]).then_inc(s[f"h_out{u}"], 16)

            def high_parts(c, u, i):
                act.wait_ge(s["part_out"], 16 * c)
                for n in range(BT):
                    act.wait_ge(s["turned"], BT * c + n + 1)
                    tiles, turned = in_bank(turned_bank, n)
                    nc.scalar.activation(part[:, tiles, 0, :], turned, ACT.Copy).then_inc(s["high_done"], 1)
                act.wait_ge(s["low_done"], BT * (c + 1))
                act.dma_start(g["parts"][:, ds(c * (CT * 2 * D), CT * 2 * D)],
                              part[:, :, :, :].rearrange("p t a d -> p (t a d)")).then_inc(s["part_out"], 16)

            lagged(act, relu, high_parts)
            act.wait_ge(s["h_out0"], 16 * (CHUNKS // 2 + 1))
            act.wait_ge(s["h_out1"], 16 * (CHUNKS // 2))
            act.wait_ge(s["part_out"], 16 * CHUNKS)

        @block.tensor
        def _(pe):
            pe.wait_ge(s["weights_in"], 32)

            def dense(c, u, i):
                for n in range(4):
                    f, at = n % 2, slice(n // 2 * SUB, (n // 2 + 1) * SUB)
                    if not isinstance(c, int) or c > 0:
                        pe.wait_ge(s["h_done"], 4 * (c - 1) + n + 1)
                    if f == 0:
                        pe.wait_ge(s["mean_done"], 2 * c + n // 2 + 1)
                    for k in range(KD):
                        nc.tensor.matmul(bank[n][:, 0:SUB], w_l[:, k, f * P:(f + 1) * P], mean[:, u, k, at],
                                         start=k == 0, stop=False)
                    for k in range(KD):
                        ins = nc.tensor.matmul(bank[n][:, 0:SUB], w_r[:, k, f * P:(f + 1) * P], own[:, u, k, at],
                                               start=False, stop=k == KD - 1)
                    ins.then_inc(s["group_done"], 1)
                pe.wait_ge(s["group_done"], 4 * (c + 1))
                pe.sem_inc(s[f"free{u}"], 1)

            def turn(c, u, i):
                pe.wait_ge(s["h_done"], 4 * (c + 1))
                pe.wait_ge(s["low_done"], BT * c)
                for n in range(CT):
                    for f in range(KD):
                        ins = nc.tensor.transpose(turned_bank[n // 2][:, n % 2 * D + f * P:n % 2 * D + (f + 1) * P],
                                                  h[:, u, f, n * P:(n + 1) * P], g["ident"][:, :])
                    if n % 2 or n == CT - 1:
                        ins.then_inc(s["turned"], 1)

            lagged(pe, dense, turn)


def first_conv(nc, io, g, adj, parts, tag, names):
    wl, b, wr = names
    with ExitStack() as ctx:
        pr = Prog(nc, ctx, tag)
        t = conv_tensors(pr, parts)
        h = pr.sb("c_h", [P, KD, CH], F32)
        bias = pr.sb("c_bias", [P, KD], F32)
        small = pr.sb("c_small", [P, 6, KD], F32)
        part = t["own"][:, :, :].bitcast(F16).rearrange("p f n -> p (f n)").rearrange("p (t a d) -> p t a d", t=CT, a=2)
        last_part = parts[:, TILES - CT:TILES, :, :]
        part_of = lambda c: last_part if isinstance(c, int) and c == CHUNKS - 1 else part
        s = {n: pr.sem("f_" + n) for n in CONV_SEMS + tuple(f"parts_in{i}" for i in range(CHUNKS)) + ("norms_in", "group_done", "h_done", "h_out", "high_done",
                                                       "low_done", "part_out", "scale_done", "next_in")}
        block = ctx.enter_context(nc.Block())

        @block.sync
        def _(sp):
            for i in range(CHUNKS):
                load_parts(sp, g, t, i, s[f"parts_in{i}"])
            sp.dma_start(bias[:, :], io[b].rearrange("(f p) -> p f", p=P), allow_slow_non_contiguous=True).then_inc(s["norms_in"], 16)
            sp.dma_start(t["mean"][:, :, 0:D], io[wl].rearrange("(f p) k -> p f k", p=P)).then_inc(s["norms_in"], 16)
            sp.dma_start(t["mean"][:, :, D:2 * D], io[wr].rearrange("(f p) k -> p f k", p=P)).then_inc(s["norms_in"], 16)
            sp.dma_start(t["wl"][:, :, :], io[wl + "_T"].rearrange("(k p) f -> p k f", p=P)).then_inc(s["weights_in"], 16)
            sp.dma_start(t["wr"][:, :, :], io[wr + "_T"].rearrange("(k p) f -> p k f", p=P)).then_inc(s["weights_in"], 16)

            with sp.Fori(0, CHUNKS) as c:
                at = sp.snap(c * CH)
                load_chunk_inv(sp, g, t, s, c, at)
                sp.wait_ge(s["part_out"], 16 * c)
                sp.dma_start(t["own"][:, :, :], g["xt"][:, :, ds(at, CH)]).then_inc(s["own_in"], 16)
            sp.wait_ge(s["agg_done"], 2 * CHUNKS)
            for i in range(CHUNKS - 1):
                load_parts(sp, g, t, i, s["next_in"])
            sp.wait_ge(s["next_in"], 16 * (CHUNKS - 1))

        @block.gpsimd
        def _(pool):
            flag = pool.value_load(g["flag"][0:1, 0:1])
            feed_upper_counts(pool, g, flag, t["hib"], s["hi_in"], s["hi_used"])

        @block.vector
        def _(dve):
            ch = Chain(dve, s["chain"])
            dve.wait_ge(s["norms_in"], 48)
            scale_of_h(nc, ch, g, t["mean"], bias, small, s["scale_done"])

            def low_parts(c):
                for n in range(BT):
                    dve.wait_ge(s["high_done"], BT * c + n + 1)
                    tiles, bank = in_bank(t["bank"], n)
                    nc.vector.tensor_tensor(part_of(c)[:, tiles, 1, :], bank, part_of(c)[:, tiles, 0, :], ALU.subtract
                                            ).then_inc(s["low_done"], 1)

            mean_half(nc, dve, t, s, 0, 0)
            mean_half(nc, dve, t, s, 0, 1)
            with dve.Fori(1, CHUNKS) as c:
                mean_half(nc, dve, t, s, c, 0)
                low_parts(c - 1)
                mean_half(nc, dve, t, s, c, 1)
            low_parts(CHUNKS - 1)

        @block.scalar
        def _(act):
            act.wait_ge(s["scale_done"], 1)

            def chunk(c):
                act.wait_ge(s["h_out"], 16 * c)
                act.wait_ge(s["turned"], BT * c)
                for n in range(4):
                    f, half = n % 2, n // 2
                    act.wait_ge(s["group_done"], 4 * c + n + 1)
                    nc.scalar.activation(h[:, f, half * SUB:(half + 1) * SUB], t["bank"][n][:, 0:SUB], ACT.Relu,
                                         bias=small[:, 5, f:f + 1], scale=g["scale"][:, f:f + 1]).then_inc(s["h_done"], 1)
                act.wait_ge(s["h_done"], 4 * (c + 1))
                act.dma_start(g["ht"][:, :, ds(c * CH, CH)], h[:, :, :]).then_inc(s["h_out"], 16)
                for n in range(BT):
                    act.wait_ge(s["turned"], BT * c + n + 1)
                    tiles, bank = in_bank(t["bank"], n)
                    nc.scalar.activation(part_of(c)[:, tiles, 0, :], bank, ACT.Copy).then_inc(s["high_done"], 1)

            with act.Fori(0, CHUNKS - 1) as c:
                chunk(c)
                act.wait_ge(s["low_done"], BT * (c + 1))
                act.dma_start(g["parts"][:, ds(c * (CT * 2 * D), CT * 2 * D)],
                              part.rearrange("p t a d -> p (t a d)")).then_inc(s["part_out"], 16)
            act.wait_ge(s["agg_done"], 2 * CHUNKS)
            chunk(CHUNKS - 1)
            act.wait_ge(s["h_out"], 16 * CHUNKS)
            act.wait_ge(s["part_out"], 16 * (CHUNKS - 1))

        def dense(pe, c):
            pe.wait_ge(s["weights_in"], 32)
            pe.wait_ge(s["mean_done"], 4 * (c + 1))
            pe.wait_ge(s["own_in"], 16 * (c + 1))
            pe.wait_ge(s["low_done"], BT * c)
            for n in range(4):
                f, at = n % 2, slice(n // 2 * SUB, (n // 2 + 1) * SUB)
                for k in range(KD):
                    nc.tensor.matmul(t["bank"][n][:, 0:SUB], t["wl"][:, k, f * P:(f + 1) * P], t["mean"][:, k, at],
                                     start=k == 0, stop=False)
                for k in range(KD):
                    ins = nc.tensor.matmul(t["bank"][n][:, 0:SUB], t["wr"][:, k, f * P:(f + 1) * P], t["own"][:, k, at],
                                           start=False, stop=k == KD - 1)
                ins.then_inc(s["group_done"], 1)
            pe.wait_ge(s["group_done"], 4 * (c + 1))
            pe.sem_inc(s["dense_done"], 1)

        def turn(pe, c):
            pe.wait_ge(s["h_done"], 4 * (c + 1))
            for n in range(CT):
                for f in range(KD):
                    ins = nc.tensor.transpose(t["bank"][n // 2][:, n % 2 * D + f * P:n % 2 * D + (f + 1) * P],
                                              h[:, f, n * P:(n + 1) * P], g["ident"][:, :])
                if n % 2 or n == CT - 1:
                    ins.then_inc(s["turned"], 1)

        block.tensor(conv_tensor_engine(nc, g, adj, t, s, dense, turn, 10, loading=True))


def second_conv(nc, io, g, adj, parts, tag, names, gate, rows_from, rows_to, routing=False, loading=False):
    wl, b, wr = names
    with ExitStack() as ctx:
        pr = Prog(nc, ctx, tag)
        t = conv_tensors(pr, parts)
        xr = pr.sb("s_rows", [P, CT, D], F32)
        last_rows = parts[:, 0:CT, :, :].rearrange("p t a d -> p t (a d)").bitcast(F32)
        rows_of = lambda c: last_rows if isinstance(c, int) and c == CHUNKS - 1 else xr[:, :, :]
        bias = pr.sb("s_bias", [P, D], F32)
        gate_w, gate_b = io[gate[0]], io[gate[1]]
        E = gate_w.shape[1]
        if routing:
            C3 = [P, CT, E]
            tri = pr.sb("s_tri", [P, P], F16)
            all1 = pr.sb("s_all1", [P, P], F16)
            mask = pr.sb("s_mask", C3, F16)
            sc, one1, one2, spare = (pr.sb("s_" + n, C3, F32) for n in ("sc", "one1", "one2", "spare"))
            most = pr.sb("s_most", [P, CT], F32)
            pre = pr.sb("s_pre", [P, CT + 1, E], F32)
            down_i = pr.sb("s_down_i", [P, E], I32)
            down = pr.sb("s_down", [P, E], F32)
            ranks_of = pr.sb("s_ranks_of", [P, CT], F32)
            place = g["place"]
        wg = pr.sb("s_gate_w", [P, KD, E], F32)
        bg = pr.sb("s_gate_b", [P, E], F32)
        st = pr.sb("s_st", [P, CT, 6], F32)
        mv = pr.sb("s_mv", [P, CT, 2], F32)
        tmp = pr.sb("s_tmp", [P, 6, CT], F32)
        rstd = pr.sb("s_rstd", [P, CT], F32)
        s = {n: pr.sem("s_" + n) for n in CONV_SEMS + ("bias_in", "rows_in", "tile_done", "sum_done", "x_out",
                                                       "var_ready", "root_done", "norm_done", "xt_ready", "xt_out",
                                                       "scattered", "consts", "mask_ready", "ranked", "placed", "place_ready",
                                                       "init",
                                                       "route_chain", "pool_chain", "scaled", "gate_in", "scored", "score_done") + tuple(f"parts_in{i}" for i in range(CHUNKS))}
        block = ctx.enter_context(nc.Block())
        chunk_of = lambda ap, c: ap.rearrange("(t p) d -> p t d", p=P)[:, ds(c * CT, CT), :]

        @block.sync
        def _(sp):
            if loading:
                for i in range(CHUNKS):
                    load_parts(sp, g, t, i, s[f"parts_in{i}"])
            sp.dma_start(t["wl"][:, :, :], io[wl + "_T"].rearrange("(k p) f -> p k f", p=P)).then_inc(s["weights_in"], 16)
            sp.dma_start(t["wr"][:, :, :], io[wr + "_T"].rearrange("(k p) f -> p k f", p=P)).then_inc(s["weights_in"], 16)
            sp.dma_start(bias[:, :], io[b].rearrange("(a n) -> a n", a=1).broadcast_to([P, D])).then_inc(s["bias_in"], 16)
            sp.dma_start(wg[:, :, :], gate_w.rearrange("(k p) e -> p k e", p=P)).then_inc(s["gate_in"], 16)
            sp.dma_start(bg[:, :], gate_b.rearrange("(a e) -> a e", a=1).broadcast_to([P, E])).then_inc(s["gate_in"], 16)

            def load(c, at):
                load_chunk_inv(sp, g, t, s, c, at)
                sp.wait_ge(s["xt_out"], 16 * c)
                sp.wait_ge(s["scored"], c)
                sp.dma_start(t["own"][:, :, :], g["ht"][:, :, ds(at, CH)]).then_inc(s["own_in"], 16)

            with sp.Fori(0, CHUNKS - 1) as c:
                load(c, sp.snap(c * CH))
                if routing:
                    sp.wait_ge(s["scattered"], 16 * 2 * CT * c)
                sp.wait_ge(s["turned"], c)
                sp.dma_start(xr[:, :, :], chunk_of(rows_from, c)).then_inc(s["rows_in"], 16)
            load(CHUNKS - 1, (CHUNKS - 1) * CH)
            sp.wait_ge(s["agg_done"], 2 * CHUNKS)
            sp.dma_start(last_rows, chunk_of(rows_from, CHUNKS - 1)).then_inc(s["rows_in"], 16)

        @block.gpsimd
        def _(pool):
            flag = pool.value_load(g["flag"][0:1, 0:1])
            if not routing:
                feed_upper_counts(pool, g, flag, t["hib"], s["hi_in"], s["hi_used"])
                return
            nc.gpsimd.iota(down_i[:, :], pattern=[[-1, E]], base=E, channel_multiplier=0).then_inc(s["consts"], 1)
            nc.gpsimd.memset(all1[:, :], 1.0).then_inc(s["consts"], 1)
            nc.gpsimd.memset(tri[:, :], 1.0).then_inc(s["pool_chain"], 1)
            pool.wait_ge(s["pool_chain"], 1)
            nc.gpsimd.affine_select(out=tri[:, :], in_=tri[:, :], compare_op=ALU.is_gt, fill=0.0, base=0,
                                    pattern=[[1, P]], channel_multiplier=-1).then_inc(s["consts"], 1)

            def feed(n):
                with pool.If(flag != 0):
                    with pool.Fori(0, TILES) as k:
                        pool.wait_ge(s["hi_used"], n * TILES + k)
                        pool.dma_start(t["hib"][:, :], g["upper"][ds(k * P, P), n * SUB:(n + 1) * SUB]).then_inc(s["hi_in"], 16)
                with pool.Else():
                    pool.nop()

            def scatter(c):
                pool.wait_ge(s["norm_done"], CT * (c + 1))
                pool.wait_ge(s["place_ready"], 2 * (c + 1))
                for n in range(2):
                    for i in range(CT):
                        at = c * CT + i
                        pool.indirect_dma_start(out=g["slots_in"], in_=rows_of(c)[:, i, :], in_offset=None,
                                                out_offset=bass.IndirectOffsetOnAxis(ap=place[:, n, at:at + 1], axis=0)
                                                ).then_inc(s["scattered"], 16)

            for c in range(CHUNKS):
                feed(2 * c)
                if c >= 2:
                    scatter(c - 2)
                feed(2 * c + 1)
            scatter(CHUNKS - 2)
            scatter(CHUNKS - 1)
            pool.wait_ge(s["scattered"], 16 * 2 * TILES)

        @block.vector
        def _(dve):
            ch = Chain(dve, s["chain"])
            dve.wait_ge(s["weights_in"], 32)
            for k in range(KD):
                ch.mark(nc.vector.tensor_scalar(t["wl"][:, k, :], t["wl"][:, k, :], g["unscale"][:, k:k + 1], XS,
                                                ALU.mult, ALU.mult))
                ch.mark(nc.vector.tensor_scalar(t["wr"][:, k, :], t["wr"][:, k, :], g["unscale"][:, k:k + 1], None,
                                                ALU.mult))
            ch.wait()
            nc.vector.memset(tmp[:, :, :], 0.0).then_inc(s["scaled"], 1)
            dve.wait_ge(s["scaled"], 1)
            dve.wait_ge(s["bias_in"], 16)
            start = ch.n
            per = 1 + NORM_MARKS

            def finish(c):
                xr = rows_of(c)
                ch.base, ch.n = start + c * per, 0
                dve.wait_ge(s["rows_in"], 16 * (c + 1))
                ch.done(nc.vector.tensor_tensor(xr, xr, bias[:, :].unsqueeze(1).broadcast_to([P, CT, D]),
                                                ALU.add))
                for n in range(BT):
                    dve.wait_ge(s["tile_done"], BT * c + n + 1)
                    tiles, bank = in_bank(t["bank"], n)
                    nc.vector.tensor_tensor(xr[:, tiles, :], bank, xr[:, tiles, :], ALU.add).then_inc(s["sum_done"], 1)
                dve.wait_ge(s["sum_done"], BT * (c + 1))
                norm_stats(nc, ch, xr, st, mv, s["var_ready"], s["root_done"], c + 1, rstd, tmp)
                assert ch.n == per, ch.n
                dve.wait_ge(s["x_out"], 16 * (c + 1))
                for n in range(CT):
                    nc.vector.tensor_scalar(xr[:, n, :], xr[:, n, :], mv[:, n, 0:1], rstd[:, n:n + 1],
                                            ALU.subtract, ALU.mult).then_inc(s["norm_done"], 1)

            def take_scores(c):
                dve.wait_ge(s["scored"], c + 1)
                nc.vector.tensor_tensor(g["scores"][:, ds(c * CT, CT), 0:E],
                                        t["bank"][3][:, 0:CT * E].rearrange("p (t e) -> p t e", e=E),
                                        bg[:, :].unsqueeze(1).broadcast_to([P, CT, E]), ALU.add).then_inc(s["score_done"], 1)

            dve.wait_ge(s["gate_in"], 32)
            if routing:
                rch = Chain(dve, s["route_chain"])
                CHOOSE, PLACE = 11, CT + 8

                def choose(c):
                    rch.base, rch.n = c * (CHOOSE + PLACE), 0
                    bc = lambda ap: ap.unsqueeze(2).broadcast_to(C3)
                    bdown = down[:, :].unsqueeze(1).broadcast_to(C3)
                    S, O1, O2, X = sc[:, :, :], one1[:, :, :], one2[:, :, :], spare[:, :, :]
                    V1, V2 = (g["choice"][:, n, ds(c * CT, CT)] for n in range(2))
                    dve.wait_ge(s["scored"], c + 1)
                    rch.done(nc.vector.tensor_tensor(S, t["bank"][3][:, 0:CT * E].rearrange("p (t e) -> p t e", e=E),
                                                     bg[:, :].unsqueeze(1).broadcast_to(C3), ALU.add))
                    rch.done(nc.vector.reduce_max(most[:, :], S, AX.X))
                    rch.done(nc.vector.tensor_tensor(O1, S, bc(most[:, :]), ALU.is_equal))
                    rch.done(nc.vector.tensor_tensor(X, O1, bdown, ALU.mult))
                    rch.done(nc.vector.reduce_max(V1, X, AX.X))
                    rch.done(nc.vector.tensor_tensor(O1, X, bc(V1), ALU.is_equal))
                    rch.done(nc.vector.scalar_tensor_tensor(S, O1, -3e38, S, ALU.mult, ALU.add))
                    rch.done(nc.vector.reduce_max(most[:, :], S, AX.X))
                    rch.done(nc.vector.tensor_tensor(O2, S, bc(most[:, :]), ALU.is_equal))
                    rch.done(nc.vector.tensor_tensor(X, O2, bdown, ALU.mult))
                    rch.done(nc.vector.reduce_max(V2, X, AX.X))
                    nc.vector.tensor_tensor(O2, X, bc(V2), ALU.is_equal).then_inc(s["score_done"], 1)
                    dve.wait_ge(s["score_done"], c + 1)
                    nc.vector.tensor_tensor(mask[:, :, :], O1, O2, ALU.add).then_inc(s["mask_ready"], 1)
                    assert rch.n == CHOOSE, rch.n

                def put(c):
                    rch.base, rch.n = c * (CHOOSE + PLACE) + CHOOSE, 0
                    ranks, totals = (t["bank"][3][:, at:at + CT * E].rearrange("p (t e) -> p t e", e=E) for at in (128, 256))
                    dve.wait_ge(s["ranked"], c + 1)
                    rch.done(nc.vector.tensor_copy(pre[:, 0, :], pre[:, CT, :]))
                    for i in range(CT):
                        rch.done(nc.vector.tensor_tensor(pre[:, i + 1, :], pre[:, i, :], totals[:, i, :], ALU.add))
                    rch.done(nc.vector.tensor_tensor(spare[:, :, :], ranks, pre[:, 0:CT, :], ALU.add))
                    dve.sem_inc(s["placed"], 1)
                    for n, one in enumerate((one1, one2)):
                        at = ds(c * CT, CT)
                        rch.done(nc.vector.tensor_tensor(sc[:, :, :], one[:, :, :], spare[:, :, :], ALU.mult))
                        rch.mark(nc.vector.reduce_sum(ranks_of[:, :], sc[:, :, :], AX.X))
                        rch.done(nc.vector.tensor_scalar(most[:, :], g["choice"][:, n, at], -float(CAP), float(E * CAP),
                                                         ALU.mult, ALU.add))
                        nc.vector.tensor_tensor(place[:, n, at], most[:, :], ranks_of[:, :], ALU.add
                                                ).then_inc(s["place_ready"], 1)
                        dve.wait_ge(s["place_ready"], 2 * c + n + 1)
                    assert rch.n == PLACE, rch.n

                dve.wait_ge(s["consts"], 3)
                nc.vector.memset(pre[:, CT, :], 0.0).then_inc(s["init"], 1)
                nc.vector.tensor_copy(down[:, :], down_i[:, :]).then_inc(s["init"], 1)
                dve.wait_ge(s["init"], 2)
            else:
                choose, put = take_scores, None
            mean_half(nc, dve, t, s, 0, 0)
            mean_half(nc, dve, t, s, 0, 1)

            def chunk(c, puts):
                if puts:
                    put(c - 2)
                mean_half(nc, dve, t, s, c, 0)
                finish(c - 1)
                mean_half(nc, dve, t, s, c, 1)
                choose(c - 1)

            if routing:
                chunk(1, False)
                with dve.Fori(2, CHUNKS) as c:
                    chunk(c, True)
                put(CHUNKS - 2)
            else:
                with dve.Fori(1, CHUNKS) as c:
                    chunk(c, False)
            finish(CHUNKS - 1)
            choose(CHUNKS - 1)
            if routing:
                put(CHUNKS - 1)
                nc.vector.tensor_copy(g["counts"][:, :], pre[:, CT, :]).then_inc(s["init"], 1)
                dve.wait_ge(s["init"], 3)

        @block.scalar
        def _(act):
            def chunk(c):
                act.wait_ge(s["sum_done"], BT * (c + 1))
                act.dma_start(chunk_of(rows_to, c), rows_of(c)).then_inc(s["x_out"], 16)
                root(nc, act, tmp, s["var_ready"], s["root_done"], c + 1)
                act.wait_ge(s["turned"], c + 1)
                evacuate_transposed(nc, t["bank"], t["own"]).then_inc(s["xt_ready"], 1)
                act.wait_ge(s["xt_ready"], c + 1)
                act.dma_start(g["xt"][:, :, ds(c * CH, CH)], t["own"][:, :, :]).then_inc(s["xt_out"], 16)

            with act.Fori(0, CHUNKS - 1) as c:
                chunk(c)
            chunk(CHUNKS - 1)
            act.wait_ge(s["x_out"], 16 * CHUNKS)
            act.wait_ge(s["xt_out"], 16 * CHUNKS)

        def dense(pe, c):
            pe.wait_ge(s["scaled"], 1)
            pe.wait_ge(s["mean_done"], 4 * (c + 1))
            pe.wait_ge(s["own_in"], 16 * (c + 1))
            pe.wait_ge(s["xt_ready"], c)
            for n in range(CT):
                at, to = slice(n * P, (n + 1) * P), t["bank"][n // 2][:, n % 2 * D:(n % 2 + 1) * D]
                for k in range(KD):
                    nc.tensor.matmul(to, t["mean"][:, k, at], t["wl"][:, k, :], start=k == 0, stop=False)
                for k in range(KD):
                    ins = nc.tensor.matmul(to, t["own"][:, k, at], t["wr"][:, k, :], start=False, stop=k == KD - 1)
                if n % 2 or n == CT - 1:
                    ins.then_inc(s["tile_done"], 1)
            pe.wait_ge(s["tile_done"], BT * (c + 1))
            pe.sem_inc(s["dense_done"], 1)

        def turn(pe, c):
            pe.wait_ge(s["norm_done"], CT * (c + 1))
            transpose_chunk(nc, pe, t["bank"], rows_of(c), g["ident"]).then_inc(s["turned"], 1)

        def score(pe, c):
            pe.wait_ge(s["xt_ready"], c + 1)
            pe.wait_ge(s["placed" if routing else "score_done"], c)
            pe.wait_ge(s["gate_in"], 32)
            for n in range(CT):
                for k in range(KD):
                    ins = nc.tensor.matmul(t["bank"][3][:, n * E:(n + 1) * E], t["own"][:, k, n * P:(n + 1) * P], wg[:, k, :],
                                           start=k == 0, stop=k == KD - 1)
            ins.then_inc(s["scored"], 1)

        def rank(pe, c):
            pe.wait_ge(s["mask_ready"], c + 1)
            nc.tensor.matmul(t["bank"][3][:, 128:128 + CT * E], tri[:, :], mask[:, :, :], start=True, stop=True)
            nc.tensor.matmul(t["bank"][3][:, 256:256 + CT * E], all1[:, :], mask[:, :, :], start=True, stop=True
                             ).then_inc(s["ranked"], 1)

        block.tensor(conv_tensor_engine(nc, g, adj, t, s, dense, turn, 21 if routing else 18, score, rank if routing else None, loading))


def first_of_largest(nc, ch, sc, m, eq, rank, mv, one, down, shape):
    bc = lambda ap: ap.unsqueeze(2).broadcast_to(shape)
    ch.done(nc.vector.reduce_max(m, sc, AX.X))
    ch.done(nc.vector.tensor_tensor(eq, sc, bc(m), ALU.is_equal))
    ch.done(nc.vector.tensor_tensor(rank, eq, down.unsqueeze(1).broadcast_to(shape), ALU.mult))
    ch.done(nc.vector.reduce_max(mv, rank, AX.X))
    ch.done(nc.vector.tensor_tensor(one, rank, bc(mv), ALU.is_equal))


def route(nc, pr, g):
    S3 = [P, TILES, E0]
    chosen = [pr.sb(f"chosen{n}", S3, F32) for n in range(2)]
    start = pr.sb("start", [P, 2, TILES], F32)
    rank = pr.sb("rank", [P, 3, 2, TILES], F32)
    ones = pr.sb("ones", [P, E0], F32)
    down_i = pr.sb("down_i", [P, E0], I32)
    down = pr.sb("down", [P, E0], F32)
    base_i = pr.sb("base_i", [P, E0], I32)
    step_i = pr.sb("step_i", [P, STMAX], I32)
    step = pr.sb("step", [P, STMAX], F32)
    cnt_i = pr.sb("cnt_i", [P, 2, E0], I32)
    cnt = pr.sb("cnt", [P, 6, E0], F32)
    past = pr.sb("past", [P, STMAX, E0], F32)
    moved = pr.sb("moved", [P, STMAX], F32)
    tail = pr.sb("tail", [P, E0], I32)
    zero = pr.sb("zero", [P, ST // P * D], F32)
    s = {n: pr.sem("r_" + n) for n in ("iotas", "chain", "zero_ready", "tail_ready", "cleared", "tables_ready")}

    def gpsimd():
        nc.gpsimd.iota(base_i[:, :], pattern=[[CAP, E0]], base=0, channel_multiplier=0).then_inc(s["iotas"], 1)
        nc.gpsimd.iota(down_i[:, :], pattern=[[-1, E0]], base=E0, channel_multiplier=0).then_inc(s["iotas"], 1)
        nc.gpsimd.iota(step_i[:, :], pattern=[[1, STMAX]], base=0, channel_multiplier=0).then_inc(s["iotas"], 1)

    def sync(sp):
        sp.wait_ge(s["zero_ready"], 1)
        sp.wait_ge(s["tail_ready"], 1)
        for e in range(E0):
            at = sp.value_load(tail[0:1, e:e + 1], min_val=0, max_val=E0 * CAP - ST)
            sp.dma_start(g["slots_in"][ds(at, ST), :].rearrange("(p r) d -> p (r d)", p=P), zero[:, :]).then_inc(s["cleared"], 16)
        sp.wait_ge(s["cleared"], 16 * E0)

    def vector(dve):
        ch = Chain(dve, s["chain"])
        nc.vector.memset(zero[:, :], 0.0).then_inc(s["zero_ready"], 1)
        ch.mark(nc.vector.memset(ones[:, :], 1.0))
        dve.wait_ge(s["iotas"], 3)
        nc.vector.tensor_tensor(tail[:, :], g["counts"][:, :], base_i[:, :], ALU.add).then_inc(s["tail_ready"], 1)
        ch.mark(nc.vector.tensor_copy(down[:, :], down_i[:, :]))
        ch.mark(nc.vector.tensor_copy(step[:, :], step_i[:, :]))
        ch.done(nc.vector.tensor_scalar(cnt[:, 0, :], g["counts"][:, :], 1.0, float(ST - 1), ALU.max, ALU.add))
        ch.done(nc.vector.tensor_copy(cnt_i[:, 0, :], cnt[:, 0, :]))
        ch.done(nc.vector.tensor_scalar(cnt_i[:, 1, :], cnt_i[:, 0, :], ST.bit_length() - 1, None, ALU.logical_shift_right))
        ch.done(nc.vector.tensor_copy(cnt[:, 1, :], cnt_i[:, 1, :]))
        ch.done(nc.vector.tensor_tensor_scan(cnt[:, 2, :], ones[:, :], cnt[:, 1, :], 0.0, ALU.mult, ALU.add))
        ch.done(nc.vector.tensor_tensor(cnt[:, 3, :], cnt[:, 2, :], cnt[:, 1, :], ALU.subtract))
        ch.mark(nc.vector.tensor_scalar(cnt[:, 4, :], cnt[:, 3, :], float(ST), None, ALU.mult))
        ch.mark(nc.vector.tensor_scalar(cnt[:, 5, :], cnt[:, 1, :], -float(ST // P), float(CAP // P), ALU.mult, ALU.add))
        ch.mark(nc.vector.tensor_copy(g["tiles"][:, 0, :], cnt[:, 1, :]))
        ch.mark(nc.vector.tensor_copy(g["tiles"][:, 1, :], cnt[:, 3, :]))
        ch.mark(nc.vector.tensor_copy(g["tiles"][:, 2, 0:1], cnt[:, 2, E0 - 1:E0]))
        ch.done(nc.vector.tensor_tensor(past[:, :, :], cnt[:, 2, :].unsqueeze(1).broadcast_to([P, STMAX, E0]),
                                        step[:, :].unsqueeze(2).broadcast_to([P, STMAX, E0]), ALU.is_le))
        ch.done(nc.vector.tensor_tensor(past[:, :, :], past[:, :, :], cnt[:, 5, :].unsqueeze(1).broadcast_to([P, STMAX, E0]), ALU.mult))
        ch.done(nc.vector.reduce_sum(moved[:, :], past[:, :, :], AX.X))
        ch.mark(nc.vector.scalar_tensor_tensor(g["from"][:, :], step[:, :], float(ST // P), moved[:, :], ALU.mult, ALU.add))
        ch.wait()
        dve.sem_inc(s["tables_ready"], 1)
        ch.mark(nc.vector.tensor_copy(rank[:, 0, :, :], g["place"][:, :, :]))
        ch.done(nc.vector.tensor_scalar(rank[:, 1, :, :], g["choice"][:, :, :], float(CAP), -float(E0 * CAP), ALU.mult, ALU.add))
        ch.mark(nc.vector.tensor_tensor(rank[:, 2, :, :], rank[:, 0, :, :], rank[:, 1, :, :], ALU.add))
        for n in range(2):
            ch.done(nc.vector.tensor_tensor(chosen[n][:, :, :], down[:, :].unsqueeze(1).broadcast_to(S3),
                                            g["choice"][:, n, :].unsqueeze(2).broadcast_to(S3), ALU.is_equal))
            ch.done(nc.vector.tensor_tensor(chosen[n][:, :, :], chosen[n][:, :, :],
                                            cnt[:, 4, :].unsqueeze(1).broadcast_to(S3), ALU.mult))
            ch.done(nc.vector.reduce_sum(start[:, n, :], chosen[n][:, :, :], AX.X))
        ch.done(nc.vector.tensor_tensor(g["slot"][:, :, :], start[:, :, :], rank[:, 2, :, :], ALU.add))

    return gpsimd, sync, vector, s["tables_ready"], s["cleared"]


def experts(nc, io, g):
    with ExitStack() as ctx:
        pr = Prog(nc, ctx, "e_")
        NT = ST // P
        w1 = pr.sb("w1", [P, 2, KD, H0], F32)
        w2 = pr.sb("w2", [P, 2, HB, D], F32)
        b1 = pr.sb("b1", [P, 2, HB], F32)
        b2 = pr.sb("b2", [P, 2, D], F32)
        xr = pr.sb("xr", [P, NT, D], F32)
        xt = pr.sb("xt", [P, KD, ST], F32)
        h = pr.sb("h", [P, HB, ST], F32)
        y = pr.sb("y", [P, NT, D], F32)
        px = pr.ps("px", [P, KD, ST])
        ph = [pr.ps(f"ph{n}", [P, ST]) for n in range(HB)]
        py = pr.ps("py", [P, NT, D])
        s = {n: pr.sem(n) for n in ("w_in0", "w_in1", "w_free0", "w_free1", "rows_in", "turned", "xt_ready", "h_mm",
                                    "h_done", "y_mm", "y_done", "y_out")}
        route_gpsimd, route_sync, route_vector, tables_ready, cleared = route(nc, pr, g)
        LOADS = 4 * 16
        block = ctx.enter_context(nc.Block())
        total_on = lambda eng: eng.value_load(g["tiles"][0:1, 2, 0:1], min_val=E0, max_val=STMAX)

        def tiles_on(eng, e):
            return (eng.value_load(g["tiles"][0:1, 0, ds(e, 1)], min_val=1, max_val=STMAX),
                    eng.value_load(g["tiles"][0:1, 1, ds(e, 1)], min_val=0, max_val=STMAX))

        @block.sync
        def _(sp):
            route_sync(sp)
            sp.wait_ge(tables_ready, 1)
            total = total_on(sp)
            tile_of = lambda ap, j: ap.rearrange("(t p) d -> p t d", p=P)[:, ds(j * NT, NT), :]

            def load(j):
                rows = sp.value_load(g["from"][0:1, ds(j, 1)], min_val=0, max_val=E0 * CAP // P - NT)
                sp.wait_ge(s["turned"], j)
                sp.dma_start(xr[:, :, :], g["slots_in"].rearrange("(t p) d -> p t d", p=P)[:, ds(rows, NT), :]
                             ).then_inc(s["rows_in"], 16)

            def store(j, count):
                sp.wait_ge(s["y_done"], count)
                sp.dma_start(tile_of(g["slots_out"], j), y[:, :, :]).then_inc(s["y_out"], 16)

            load(0)
            load(1)
            with sp.Fori(2, total) as j:
                load(j)
                store(sp.snap(j - 2), j)
            store(total - 2, total)
            store(total - 1, total + 1)

        @block.tensor
        def _(pe):
            pe.wait_ge(tables_ready, 1)

            def turn(j):
                pe.wait_ge(s["rows_in"], 16 * (j + 1))
                for k in range(KD):
                    for t in range(NT):
                        ins = nc.tensor.transpose(px[:, k, t * P:(t + 1) * P], xr[:, t, k * P:(k + 1) * P], g["ident"][:, :])
                ins.then_inc(s["turned"], 1)

            def first_product(j, u):
                pe.wait_ge(s["xt_ready"], j + 1)
                for n in range(HB):
                    for k in range(KD):
                        ins = nc.tensor.matmul(ph[n][:, :], w1[:, u, k, n * P:(n + 1) * P], xt[:, k, :],
                                               start=k == 0, stop=k == KD - 1)
                    ins.then_inc(s["h_mm"], 1)

            def second_product(before, u):
                pe.wait_ge(s["h_done"], HB * before)
                pe.wait_ge(s["y_done"], before)
                for t in range(NT):
                    for n in range(HB):
                        ins = nc.tensor.matmul(py[:, t, :], h[:, n, t * P:(t + 1) * P], w2[:, u, n, :],
                                               start=n == 0, stop=n == HB - 1)
                ins.then_inc(s["y_mm"], 1)

            def expert(e, u, uses):
                tiles, at = tiles_on(pe, e)
                if not isinstance(e, int) or e > 0:
                    turn(at)
                    second_product(at, 1 - u)
                else:
                    at = 0
                    turn(at)
                pe.wait_ge(s[f"w_in{u}"], LOADS * (uses + 1))
                first_product(at, u)
                with pe.If(tiles > 1):
                    with pe.Fori(1, tiles) as i:
                        j = pe.snap(at + i)
                        turn(j)
                        second_product(j, u)
                        first_product(j, u)
                with pe.Else():
                    pe.nop()

            expert(0, 0, 0)
            with pe.Fori(0, E0 // 2 - 1) as k:
                expert(k * 2 + 1, 1, k)
                expert(k * 2 + 2, 0, k + 1)
            expert(E0 - 1, 1, E0 // 2 - 1)
            total = total_on(pe)
            second_product(total, 1)

        @block.scalar
        def _(act):
            act.wait_ge(tables_ready, 1)

            def expert(e, u):
                tiles, at = tiles_on(act, e)
                with act.Fori(0, tiles) as i:
                    j = act.snap(at + i)
                    act.wait_ge(s["turned"], j + 1)
                    nc.scalar.activation(xt[:, :, :], px[:, :, :], ACT.Identity).then_inc(s["xt_ready"], 1)
                    for n in range(HB):
                        act.wait_ge(s["h_mm"], HB * j + n + 1)
                        nc.scalar.activation(h[:, n, :], ph[n][:, :], ACT.Gelu, bias=b1[:, u, n:n + 1]
                                             ).then_inc(s["h_done"], 1)

            with act.Fori(0, E0 // 2) as k:
                expert(k * 2, 0)
                expert(k * 2 + 1, 1)

        @block.vector
        def _(dve):
            route_vector(dve)

            def expert(e, u):
                tiles, at = tiles_on(dve, e)
                with dve.Fori(0, tiles) as i:
                    j = dve.snap(at + i)
                    dve.wait_ge(s["y_out"], 16 * j)
                    dve.wait_ge(s["y_mm"], j + 1)
                    nc.vector.tensor_tensor(y[:, :, :], py[:, :, :], b2[:, u, :].unsqueeze(1).broadcast_to([P, NT, D]),
                                            ALU.add).then_inc(s["y_done"], 1)
                dve.wait_ge(s["y_done"], at + tiles + 1)
                dve.sem_inc(s[f"w_free{u}"], 1)

            dve.sem_inc(s["y_done"], 1)
            with dve.Fori(0, E0 // 2) as k:
                expert(k * 2, 0)
                expert(k * 2 + 1, 1)

        @block.gpsimd
        def _(pool):
            route_gpsimd()

            def load(e, u, uses):
                pool.wait_ge(s[f"w_free{u}"], uses)
                for to, fr in ((w1[:, u, :, :], io["L0_ffn_W1"].rearrange("e (k p) h -> p (e k) h", p=P)[:, ds(e * KD, KD), :]),
                               (w2[:, u, :, :], io["L0_ffn_W2"].rearrange("e (k p) d -> p (e k) d", p=P)[:, ds(e * HB, HB), :]),
                               (b1[:, u, :], io["L0_ffn_b1"].rearrange("e (k p) -> p (e k)", p=P)[:, ds(e * HB, HB)]),
                               (b2[:, u, :], io["L0_ffn_b2"][ds(e, 1), :].broadcast_to([P, D]))):
                    pool.dma_start(to, fr, allow_slow_non_contiguous=True).then_inc(s[f"w_in{u}"], 16)

            load(0, 0, 0)
            pool.wait_ge(cleared, 16 * E0)
            load(1, 1, 0)
            with pool.Fori(1, E0 // 2) as k:
                load(k * 2, 0, k)
                load(k * 2 + 1, 1, k)
            pool.wait_ge(tables_ready, 1)
            pool.wait_ge(s["y_out"], 16 * total_on(pool))


def last_experts(nc, io, g, rows_from, out):
    with ExitStack() as ctx:
        pr = Prog(nc, ctx, "m_")
        F = "L1_ffn_"
        sw1 = pr.sb("sw1", [P, KD, SH1], F32)
        sw2 = pr.sb("sw2", [P, SH1 // P, SH2], F32)
        sw3 = pr.sb("sw3", [P, D], F32)
        ew1 = pr.sb("ew1", [P, KD, E1, EH1], F32)
        ew2 = pr.sb("ew2", [P, E1, EH2], F32)
        ew3 = pr.sb("ew3", [EH2 + 1, E1, D], F32)
        sb1 = pr.sb("sb1", [P, SH1 // P], F32)
        sb2 = pr.sb("sb2", [P, 1], F32)
        sb3 = pr.sb("sb3", [P, D], F32)
        eb1 = pr.sb("eb1", [P, E1], F32)
        eb2 = pr.sb("eb2", [EH2, E1], F32)
        xt = pr.sb("xt", [P, KD, ROWS], F32)
        h1 = pr.sb("h1", [P, SH1 // P, CH], F32)
        h2 = pr.sb("h2", [P, CH], F32)
        eh1 = pr.sb("eh1", [P, 2, CH], F32)
        eh2 = pr.sb("eh2", [EH2 + 1, 2, CH], F32)
        acc = pr.sb("acc", [P, TILES, D], F32)
        weight = pr.sb("weight", [P, CT, E1], F32)
        down_i = pr.sb("down_i", [P, E1], I32)
        down = pr.sb("down", [P, E1], F32)
        S3 = [P, TILES, E1]
        f = {n: pr.sb(n, S3, F32) for n in ("sc", "d", "ex", "gate", "eq", "rank", "o1", "o2", "w1", "w2", "wt")}
        f2 = {n: pr.sb(n, [P, TILES], F32) for n in ("mx", "sm", "rs", "m1", "m2", "mv", "dd", "t", "t1", "r2", "v2")}
        bank = [pr.ps(f"bank{i}", [P, 512]) for i in range(7)]
        s = {n: pr.sem(n) for n in ("first_w_in", "w_in", "xt_in", "acc_in", "down_ready", "chain", "exp_in1", "exp_in2",
                                    "exp1", "exp2", "mm", "act_took", "dve_took", "ready", "out_done")}
        block = ctx.enter_context(nc.Block())
        NB = len(bank)
        FIRST, REST = 5, 8
        ORDER = ["S1", "E1.0", "S2", "E2.0", "E1.1", "S3", "E3.0", "E2.1", "E1.2", "E3.1", "E2.2", "E1.3", "E3.2",
                 "E2.3", "E3.3"]
        GROUPS = {"S1": 4, "S2": 2, "S3": BT, "E1": 2, "E2": 2, "E3": BT}
        first, n = {}, 0
        for name in ORDER:
            first[name] = n
            n += GROUPS[name[:2]]
        TOTAL = n
        by_dve = [x[:2] in ("S3", "E3") for x in ORDER for _ in range(GROUPS[x[:2]])]
        taken = [sum(1 for b in by_dve[:i + 1] if b == by_dve[i]) for i in range(TOTAL)]
        ACT_N, DVE_N = by_dve.count(False), by_dve.count(True)

        def group_taken(eng, c, i):
            if by_dve[i]:
                eng.wait_ge(s["dve_took"], (c + 1) * DVE_N + taken[i])
            else:
                eng.wait_ge(s["act_took"], (c + 1) * ACT_N + taken[i])

        @block.sync
        def _(sp):
            first = [(sw1[:, :, :], io[F + "sW1"].rearrange("(k p) n -> p k n", p=P))] + [
                (ew1[:, k, :, :], io[F + "eW1"][:, k * P:(k + 1) * P, :].rearrange("e p n -> p e n")) for k in range(KD)]
            first += [(sb1[:, :], io[F + "sb1"].rearrange("(k p) -> p k", p=P)),
                      (eb1[:, :], io[F + "eb1"].rearrange("e p -> p e"))]
            rest = [
                (sw2[:, :, :], io[F + "sW2"].rearrange("(k p) n -> p k n", p=P)),
                (sb2[:, :], io[F + "sb2"].rearrange("(p a) -> p a", a=1)),
                (ew2[:, :, :], io[F + "eW2"].rearrange("e p n -> p e n")),
                (eb2[:, :], io[F + "eb2"].rearrange("e p -> p e")),
                (sw3[:, :], io[F + "sW3"]),
                (sb3[:, :], io[F + "sb3"].rearrange("(a n) -> a n", a=1).broadcast_to([P, D])),
                (ew3[EH2:EH2 + 1, :, :], io[F + "eb3"].rearrange("(a e) n -> a e n", a=1)),
                (ew3[0:EH2, :, :], io[F + "eW3"].rearrange("e p n -> p e n")),
            ]
            assert (len(first), len(rest)) == (FIRST, REST)
            for to, fr in first:
                sp.dma_start(to, fr, allow_slow_non_contiguous=True).then_inc(s["first_w_in"], 16)
            sp.dma_start(xt[:, :, 0:CH], g["xt"][:, :, 0:CH]).then_inc(s["xt_in"], 16)
            for to, fr in rest:
                sp.dma_start(to, fr, allow_slow_non_contiguous=True).then_inc(s["w_in"], 16)
            for c in range(CHUNKS):
                if c:
                    sp.wait_ge(s["xt_in"], 16 * c)
                    sp.wait_ge(s["acc_in"], 16 * c)
                    sp.dma_start(xt[:, :, c * CH:(c + 1) * CH], g["xt"][:, :, c * CH:(c + 1) * CH]).then_inc(s["xt_in"], 16)
                sp.dma_start(acc[:, c * CT:(c + 1) * CT, :],
                             rows_from.rearrange("(t p) d -> p t d", p=P)[:, c * CT:(c + 1) * CT, :]).then_inc(s["acc_in"], 16)

        @block.gpsimd
        def _(pool):
            nc.gpsimd.iota(down_i[:, :], pattern=[[-1, E1]], base=E1, channel_multiplier=0).then_inc(s["down_ready"], 1)
            with pool.Fori(0, CHUNKS - 1) as c:
                pool.wait_ge(s["dve_took"], DVE_N * (c + 2))
                pool.dma_start(out[ds(c * CH, CH), :].rearrange("(t p) d -> p t d", p=P), acc[:, ds(c * CT, CT), :]).then_inc(s["out_done"], 16)
            pool.wait_ge(s["dve_took"], DVE_N * (CHUNKS + 1))
            at = (CHUNKS - 1) * CH
            full = (NODES - at) // P
            pool.dma_start(out[at:at + full * P, :].rearrange("(t p) d -> p t d", p=P), acc[:, TILES - CT:TILES - CT + full, :]).then_inc(s["out_done"], 16)
            rest = NODES - at - full * P
            pool.dma_start(out[NODES - rest:NODES, :], acc[0:rest, TILES - CT + full, :]).then_inc(s["out_done"], 16)
            pool.wait_ge(s["out_done"], 16 * (CHUNKS + 1))

        @block.tensor
        def _(pe):
            pe.wait_ge(s["first_w_in"], 16 * FIRST)
            pe.wait_ge(s["ready"], 1)
            with pe.Fori(0, CHUNKS) as c:
                pe.wait_ge(s["xt_in"], 16 * (c + 1))
                for name in ORDER:
                    kind, e = name[:2], int(name[3:] or 0)
                    if name == "S2":
                        pe.wait_ge(s["w_in"], 16 * REST)
                    need = {"S2": "S1", "S3": "S2", "E2": f"E1.{e}", "E3": f"E2.{e}"}.get(kind)
                    if need:
                        group_taken(pe, c, first[need] + GROUPS[need[:2]] - 1)
                    for n in range(GROUPS[kind]):
                        i = first[name] + n
                        if i >= NB:
                            group_taken(pe, c, i - NB)
                        else:
                            group_taken(pe, c - 1, max(j for j in range(TOTAL) if j % NB == i))
                        b = bank[i % NB]
                        half = slice((n if kind != "S1" else n // 2) * SUB, ((n if kind != "S1" else n // 2) + 1) * SUB)
                        if kind == "S1":
                            for k in range(KD):
                                ins = nc.tensor.matmul(b[:, 0:SUB], sw1[:, k, n % 2 * P:(n % 2 + 1) * P], xt[:, k, ds(c * CH + half.start, SUB)],
                                                       start=k == 0, stop=k == KD - 1)
                        elif kind == "E1":
                            for k in range(KD):
                                ins = nc.tensor.matmul(b[:, 0:SUB], ew1[:, k, e, :], xt[:, k, ds(c * CH + half.start, SUB)], start=k == 0, stop=k == KD - 1)
                        elif kind == "S2":
                            for k in range(SH1 // P):
                                ins = nc.tensor.matmul(b[:, 0:SUB], sw2[:, k, :], h1[:, k, half], start=k == 0, stop=k == SH1 // P - 1)
                        elif kind == "E2":
                            ins = nc.tensor.matmul(b[0:EH2, 0:SUB], ew2[:, e, :], eh1[:, e % 2, half], start=True, stop=True)
                        else:
                            for t in range(2 * n, min(2 * n + 2, CT)):
                                to = b[:, t % 2 * D:(t % 2 + 1) * D]
                                if kind == "S3":
                                    ins = nc.tensor.matmul(to, h2[:, t * P:(t + 1) * P], sw3[:, :], start=True, stop=True)
                                else:
                                    ins = nc.tensor.matmul(to, eh2[:, e % 2, t * P:(t + 1) * P], ew3[:, e, :], start=True, stop=True)
                        ins.then_inc(s["mm"], 1)

        @block.scalar
        def _(act):
            act.sem_inc(s["act_took"], ACT_N)
            act.wait_ge(s["exp_in1"], 1)
            nc.scalar.activation(f["ex"][:, :, :], f["d"][:, :, :], ACT.Exp).then_inc(s["exp1"], 1)
            act.wait_ge(s["exp_in2"], 1)
            nc.scalar.activation(f2["t"][:, :], f2["dd"][:, :], ACT.Exp).then_inc(s["exp2"], 1)
            act.wait_ge(s["first_w_in"], 16 * FIRST)
            with act.Fori(0, CHUNKS) as c:
                for name in ORDER:
                    kind, e = name[:2], int(name[3:] or 0)
                    if kind in ("S3", "E3"):
                        continue
                    if name == "S2":
                        act.wait_ge(s["w_in"], 16 * REST)
                    for n in range(GROUPS[kind]):
                        i = first[name] + n
                        b = bank[i % NB]
                        half = slice((n if kind != "S1" else n // 2) * SUB, ((n if kind != "S1" else n // 2) + 1) * SUB)
                        act.wait_ge(s["mm"], c * TOTAL + i + 1)
                        if kind == "S1":
                            to, fr, bias = h1[:, n % 2, half], b[:, 0:SUB], sb1[:, n % 2:n % 2 + 1]
                        elif kind == "E1":
                            to, fr, bias = eh1[:, e % 2, half], b[:, 0:SUB], eb1[:, e:e + 1]
                        elif kind == "S2":
                            to, fr, bias = h2[:, half], b[:, 0:SUB], sb2[:, 0:1]
                        else:
                            to, fr, bias = eh2[0:EH2, e % 2, half], b[0:EH2, 0:SUB], eb2[:, e:e + 1]
                        nc.scalar.activation(to, fr, ACT.Relu, bias=bias).then_inc(s["act_took"], 1)

        @block.vector
        def _(dve):
            ch = Chain(dve, s["chain"])
            dve.sem_inc(s["dve_took"], DVE_N)
            dve.wait_ge(s["down_ready"], 1)
            ch.mark(nc.vector.tensor_copy(down[:, :], down_i[:, :]))
            ch.done(nc.vector.memset(eh2[EH2:EH2 + 1, :, :], 1.0))
            nc.vector.memset(f2["sm"][:, :], 1.0).then_inc(s["ready"], 1)
            dve.wait_ge(s["ready"], 1)
            a = {n: v[:, :, :] for n, v in f.items()}
            a2 = {n: v[:, :] for n, v in f2.items()}
            bc = lambda ap: ap.unsqueeze(2).broadcast_to(S3)
            ch.done(nc.vector.tensor_copy(a["sc"], g["scores"][:, :, :]))
            ch.done(nc.vector.reduce_max(a2["mx"], a["sc"], AX.X))
            nc.vector.tensor_tensor(a["d"], a["sc"], bc(a2["mx"]), ALU.subtract).then_inc(s["exp_in1"], 1)
            dve.wait_ge(s["exp1"], 1)
            ch.done(nc.vector.reduce_sum(a2["sm"], a["ex"], AX.X))
            ch.done(nc.vector.reciprocal(a2["rs"], a2["sm"]))
            ch.done(nc.vector.tensor_tensor(a["gate"], a["ex"], bc(a2["rs"]), ALU.mult))
            first_of_largest(nc, ch, a["gate"], a2["m1"], a["eq"], a["rank"], a2["mv"], a["o1"], down[:, :], S3)
            ch.done(nc.vector.scalar_tensor_tensor(a["gate"], a["o1"], -2.0, a["gate"], ALU.mult, ALU.add))
            first_of_largest(nc, ch, a["gate"], a2["m2"], a["eq"], a["rank"], a2["mv"], a["o2"], down[:, :], S3)
            nc.vector.tensor_tensor(a2["dd"], a2["m2"], a2["m1"], ALU.subtract).then_inc(s["exp_in2"], 1)
            dve.wait_ge(s["exp2"], 1)
            ch.done(nc.vector.tensor_scalar(a2["t1"], a2["t"], 1.0, None, ALU.add))
            ch.done(nc.vector.reciprocal(a2["r2"], a2["t1"]))
            ch.mark(nc.vector.tensor_tensor(a2["v2"], a2["t"], a2["r2"], ALU.mult))
            ch.done(nc.vector.tensor_tensor(a["w1"], a["o1"], bc(a2["r2"]), ALU.mult))
            ch.done(nc.vector.tensor_tensor(a["w2"], a["o2"], bc(a2["v2"]), ALU.mult))
            ch.done(nc.vector.tensor_tensor(a["wt"], a["w1"], a["w2"], ALU.add))
            dve.wait_ge(s["w_in"], 16 * REST)
            with ch.loop(0, CHUNKS, 2) as c:
                dve.wait_ge(s["acc_in"], 16 * (c + 1))
                dve.wait_ge(s["dve_took"], DVE_N * (c + 1))
                ch.mark(nc.vector.tensor_copy(weight[:, :, :], f["wt"][:, ds(c * CT, CT), :]))
                rows = acc[:, ds(c * CT, CT), :]
                ch.done(nc.vector.tensor_tensor(rows, rows, sb3[:, :].unsqueeze(1).broadcast_to([P, CT, D]), ALU.add))
                for name in ORDER:
                    kind, e = name[:2], int(name[3:] or 0)
                    if kind not in ("S3", "E3"):
                        continue
                    for n in range(GROUPS[kind]):
                        i = first[name] + n
                        dve.wait_ge(s["mm"], c * TOTAL + i + 1)
                        tiles, b = in_bank([bank[i % NB]] * BT, n)
                        if kind == "S3":
                            rows = acc[:, ds(c * CT + tiles.start, tiles.stop - tiles.start), :]
                            ins = nc.vector.tensor_tensor(rows, b, rows, ALU.add)
                        else:
                            dve.wait_ge(s["dve_took"], (c + 1) * DVE_N + taken[i] - BT)
                            for t in range(tiles.start, tiles.stop):
                                row = acc[:, ds(c * CT + t, 1), :].rearrange("p a d -> p (a d)")
                                ins = nc.vector.scalar_tensor_tensor(row, b[:, t - tiles.start, :], weight[:, t, e:e + 1],
                                                                     row, ALU.mult, ALU.add)
                        ins.then_inc(s["dve_took"], 1)


def program(nc, io, out):
    dram = lambda name, shape, dt: nc.dram_tensor(name, shape, dt).ap()
    g = {
        "parts": dram("parts", (P, TILES * 2 * D), F16),
        "xt": dram("xt", (P, KD, ROWS), F32),
        "ht": dram("ht", (P, KD, ROWS), F32),
        "slots_in": dram("slots_in", (E0 * CAP, D), F32),
        "slots_out": dram("slots_out", (SLOTS, D), F32),
        "x1": dram("x1", (ROWS, D), F32),
        "x2": dram("x2", (ROWS, D), F32),
        "x3": dram("x3", (ROWS, D), F32),
        "upper": dram("upper", (ROWS, ROWS), F16),
        "degree": dram("degree", (1, ROWS), F32),
        "sums": dram("sums", (P, KD, ROWS), F32),
        "inv": dram("inv", (1, ROWS), F32),
        "keys": dram("keys", (2, P, WINS * VIS, 2), F16),
    }
    with ExitStack() as ctx:
        pr = Prog(nc, ctx)
        g["ident"] = pr.sb("ident", [P, P], F32)
        g["flag"] = pr.sb("flag", [1, 1], I32)
        g["scale"] = pr.sb("scale", [P, KD], F32)
        g["unscale"] = pr.sb("unscale", [P, KD], F32)
        first_block(nc, io, g)
        last_scores = pr.sb("last_scores", [P, TILES, E1], F32)
        held = ctx.enter_context(ExitStack())
        adj = held.enter_context(nc.sbuf_tensor("adj", [P, TILES, ROWS], F16))
        build_counts(nc, io, g, adj)
        for name, shape in (("choice", [P, 2, TILES]), ("counts", [P, E0])):
            g[name] = held.enter_context(nc.sbuf_tensor(name, shape, F32))
        g["place"] = held.enter_context(nc.sbuf_tensor("place", [P, 2, TILES], I32))
        summed_conv(nc, io, g, "l0a_", ("L0_gnn_W1l", "L0_gnn_b1", "L0_gnn_W1r"))
        with nc.sbuf_tensor("l0_parts", [P, TILES, 2, D], F16) as parts:
            second_conv(nc, io, g, adj, parts, "l0b_", ("L0_gnn_W2l", "L0_gnn_b2", "L0_gnn_W2r"),
                        ("L0_ffn_Wg", "L0_ffn_bg"), io["x"], g["x1"], routing=True, loading=True)
        for name, shape in (("slot", [P, 2, TILES]), ("tiles", [P, 3, E0]), ("from", [P, STMAX])):
            g[name] = held.enter_context(nc.sbuf_tensor(name, shape, I32))
        experts(nc, io, g)
        normalise_sum(nc, g)
        g["scores"] = last_scores
        with nc.sbuf_tensor("l1_parts", [P, TILES, 2, D], F16) as parts:
            first_conv(nc, io, g, adj, parts, "l1a_", ("L1_gnn_w1_l", "L1_gnn_b1", "L1_gnn_w1_r"))
            second_conv(nc, io, g, adj, parts, "l1b_", ("L1_gnn_w2_l", "L1_gnn_b2", "L1_gnn_w2_r"),
                        ("L1_ffn_gW", "L1_ffn_gb"), g["x2"], g["x3"])
        held.close()
        last_experts(nc, io, g, g["x3"], out)


GNN_WEIGHTS = ("L0_gnn_W1l", "L0_gnn_W1r", "L0_gnn_W2l", "L0_gnn_W2r",
               "L1_gnn_w1_l", "L1_gnn_w1_r", "L1_gnn_w2_l", "L1_gnn_w2_r")


def layout(inputs):
    import numpy as np

    def padded(a, rows, value):
        return np.concatenate([a, np.full((rows - a.shape[0],) + a.shape[1:], value, a.dtype)])

    arrays = {n: np.ascontiguousarray(a) for n, a in inputs.items()}
    arrays["x"] = padded(arrays["x"], ROWS, 0)
    arrays["src"] = padded(arrays["src"], EPAD, 0)
    arrays["dst"] = padded(arrays["dst"], EPAD, FAR)
    for n in GNN_WEIGHTS:
        arrays[n + "_T"] = np.ascontiguousarray(arrays[n].T)
    return arrays


def kernel(**inputs):
    import concourse.bacc as bacc
    from concourse.bass_utils import run_bass_kernel_spmd

    nc = bacc.Bacc("TRN2", target_bir_lowering=False, num_devices=1)
    arrays = layout(inputs)
    io = {n: nc.dram_tensor("in_" + n, a.shape, mybir.dt.from_np(a.dtype), kind="ExternalInput").ap()
          for n, a in arrays.items()}
    out = nc.dram_tensor("out", (NODES, D), F32, kind="ExternalOutput").ap()
    program(nc, io, out)
    r = run_bass_kernel_spmd(nc, [{"in_" + n: a for n, a in arrays.items()}], core_ids=[0])
    return r.results[0]["out"]
```
